# Optimizing a Trainium2 kernel written in Bass

```python
import numpy as np
import jax
import jax.numpy as jnp

def _softmax(x, axis=-1):
    return jax.nn.softmax(x, axis=axis)

def _gelu(x):
    return jax.nn.gelu(x, approximate=True)

def _silu(x):
    return jax.nn.silu(x)

def _sigmoid(x):
    return jax.nn.sigmoid(x)

def _layernorm(x, axis=-1, eps=1e-05):
    m = jnp.mean(x, axis=axis, keepdims=True)
    v = jnp.var(x, axis=axis, keepdims=True)
    return (x - m) / jnp.sqrt(v + eps)

def _scatter_add(tgt, idx, src, axis=0):
    return tgt.at[idx].add(src)

def _segment_sum(src, seg, n):
    return jax.ops.segment_sum(src, seg, n)
kernel_name = 'mk_adaln_ffn_d2_seqx_r8_858c47'

def setup_inputs(seed: int=0):
    np.random.seed(seed)
    _w = jnp.asarray

    def _rec_inputs():
        import jax
        import jax.numpy as jnp
        _rk = jax.random.key(seed)
        x = -0.0003929 + 0.9999 * jax.random.normal(jax.random.fold_in(_rk, 1), (128, 32, 256), jnp.float32)
        _lenS = 32 - jax.random.randint(jax.random.fold_in(_rk, 7), (128,), 0, max(1, 32 // 4) + 1, jnp.int32)
        _lenS2 = 32 - jax.random.randint(jax.random.fold_in(_rk, 8), (128,), 0, max(1, 32 // 4) + 1, jnp.int32)
        itok_B_0_7 = jax.random.randint(jax.random.fold_in(_rk, 11), (128,), 0, 8, jnp.int32)
        itok_B_0_6 = jax.random.randint(jax.random.fold_in(_rk, 12), (128,), 0, 7, jnp.int32)
        return (x, itok_B_0_7, itok_B_0_6)
    x, itok_B_0_7, itok_B_0_6 = _rec_inputs()

    def _L0_cond_setup():
        import jax, jax.numpy as jnp
        import numpy as np

        def _lora_linear(x, W, A, B, adapter_indices):
            base = jnp.einsum('bsd,df->bsf', x, W)
            Ai = A[adapter_indices]
            Bi = B[adapter_indices]
            lora = jnp.einsum('bsr,brf->bsf', jnp.einsum('bsd,bdr->bsr', x, Ai), Bi)
            return base + lora
        key = jax.random.key(seed)
        ks = jax.random.split(key, 10)
        H, I, N, R = (256, 1024, 8, 16)
        B, S = (4, 256)
        std_h = 1.0 / np.sqrt(H)
        std_i = 1.0 / np.sqrt(I)
        x = jax.random.normal(ks[0], (B, S, H), dtype=jnp.float32)
        adapter_indices = jax.random.randint(ks[1], (B,), 0, N, dtype=jnp.int32)
        Wg = jax.random.normal(ks[2], (H, I), dtype=jnp.float32) * std_h
        Wu = jax.random.normal(ks[3], (H, I), dtype=jnp.float32) * std_h
        Wd = jax.random.normal(ks[4], (I, H), dtype=jnp.float32) * std_i
        Ag = jax.random.normal(ks[5], (N, H, R), dtype=jnp.float32) * std_h
        Bg = jnp.zeros((N, R, I), dtype=jnp.float32) + 0.01
        Au = jax.random.normal(ks[6], (N, H, R), dtype=jnp.float32) * std_h
        Bu = jnp.zeros((N, R, I), dtype=jnp.float32) + 0.01
        Ad = jax.random.normal(ks[7], (N, I, R), dtype=jnp.float32) * std_i
        Bd = jnp.zeros((N, R, H), dtype=jnp.float32) + 0.01
        return {'x': x, 'Wg': Wg, 'Wu': Wu, 'Wd': Wd, 'Ag': Ag, 'Bg': Bg, 'Au': Au, 'Bu': Bu, 'Ad': Ad, 'Bd': Bd, 'adapter_indices': adapter_indices}
    _L0_cond_all = _L0_cond_setup()
    _L0_cond_in = {k: v for k, v in _L0_cond_all.items() if k in ('Wg', 'Wu', 'Wd', 'Ag', 'Bg', 'Au', 'Bu', 'Ad', 'Bd')}
    del _L0_cond_all

    def _L0_ffn_setup():
        import jax, jax.numpy as jnp
        import numpy as np
        H = 256
        I = 176
        E = 8
        K = 2
        B, S = (2, 256)
        key = jax.random.key(seed)
        k0, k1, k2, k3, k4 = jax.random.split(key, 5)
        scale = 1.0 / np.sqrt(H)
        x = jax.random.normal(k0, (B, S, H), dtype=jnp.float32)
        Wr = jax.random.normal(k1, (H, E), dtype=jnp.float32) * scale
        Wg = jax.random.normal(k2, (E, H, I), dtype=jnp.float32) * scale
        Wu = jax.random.normal(k3, (E, H, I), dtype=jnp.float32) * scale
        Wd = jax.random.normal(k4, (E, I, H), dtype=jnp.float32) * (1.0 / np.sqrt(I))
        return {'x': x, 'Wr': Wr, 'Wg': Wg, 'Wu': Wu, 'Wd': Wd}
    _L0_ffn_all = _L0_ffn_setup()
    _L0_ffn_in = {k: v for k, v in _L0_ffn_all.items() if k in ('Wr', 'Wg', 'Wu', 'Wd')}
    del _L0_ffn_all

    def _L1_cond_setup():
        import jax, jax.numpy as jnp
        import numpy as np
        B, T, D_IN, D_OUT = (16, 256, 256, 256)
        N_ADAPTERS, RANK = (8, 16)
        key = jax.random.key(seed)
        k_x, k_w, k_a, k_b, k_s, k_idx = jax.random.split(key, 6)
        x = jax.random.normal(k_x, (B, T, D_IN), dtype=jnp.float32)
        W = jax.random.normal(k_w, (D_OUT, D_IN), dtype=jnp.float32) * (1.0 / np.sqrt(D_IN))
        A = jax.random.normal(k_a, (N_ADAPTERS, RANK, D_IN), dtype=jnp.float32) * 0.02
        Bm = jax.random.normal(k_b, (N_ADAPTERS, D_OUT, RANK), dtype=jnp.float32) * 0.02
        scalings = jnp.ones((N_ADAPTERS,), dtype=jnp.float32)
        adapter_idx = jax.random.randint(k_idx, (B,), 0, N_ADAPTERS, dtype=jnp.int32)
        return {'x': x, 'W': W, 'A': A, 'Bm': Bm, 'scalings': scalings, 'adapter_idx': adapter_idx}
    _L1_cond_all = _L1_cond_setup()
    _L1_cond_in = {k: v for k, v in _L1_cond_all.items() if k in ('W', 'A', 'Bm', 'scalings')}
    del _L1_cond_all

    def _L1_ffn_setup():
        import jax, jax.numpy as jnp
        import numpy as np
        NUM_EXPERTS = 8
        TOP_K = 2
        LORA_ALPHA = 2.0
        LORA_RANK = 16
        D_MODEL = 256
        D_HIDDEN = 704
        key = jax.random.key(seed)
        ks = jax.random.split(key, 11)
        B, S, D, H, E, R = (2, 128, D_MODEL, D_HIDDEN, NUM_EXPERTS, LORA_RANK)
        sd = 1.0 / np.sqrt(D)
        sh = 1.0 / np.sqrt(H)
        x = jax.random.normal(ks[0], (B, S, D), jnp.float32)
        gate_w = jax.random.normal(ks[1], (E, D), jnp.float32) * sd
        w_up = jax.random.normal(ks[2], (H, D), jnp.float32) * sd
        w_gate = jax.random.normal(ks[3], (H, D), jnp.float32) * sd
        w_down = jax.random.normal(ks[4], (D, H), jnp.float32) * sh
        up_A = jax.random.normal(ks[5], (E, R, D), jnp.float32) * sd
        up_B = jax.random.normal(ks[6], (E, H, R), jnp.float32) * 0.02
        gate_A = jax.random.normal(ks[7], (E, R, D), jnp.float32) * sd
        gate_B = jax.random.normal(ks[8], (E, H, R), jnp.float32) * 0.02
        down_A = jax.random.normal(ks[9], (E, R, H), jnp.float32) * sh
        down_B = jax.random.normal(ks[10], (E, D, R), jnp.float32) * 0.02
        return {'x': x, 'gate_w': gate_w, 'w_up': w_up, 'w_gate': w_gate, 'w_down': w_down, 'up_A': up_A, 'up_B': up_B, 'gate_A': gate_A, 'gate_B': gate_B, 'down_A': down_A, 'down_B': down_B}
    _L1_ffn_all = _L1_ffn_setup()
    _L1_ffn_in = {k: v for k, v in _L1_ffn_all.items() if k in ('gate_w', 'w_up', 'w_gate', 'w_down', 'up_A', 'up_B', 'gate_A', 'gate_B', 'down_A', 'down_B')}
    del _L1_ffn_all
    return {'x': x, 'itok_B_0_7': itok_B_0_7, 'itok_B_0_6': itok_B_0_6, 'L0_cond_Wg': _L0_cond_in['Wg'], 'L0_cond_Wu': _L0_cond_in['Wu'], 'L0_cond_Wd': _L0_cond_in['Wd'], 'L0_cond_Ag': _L0_cond_in['Ag'], 'L0_cond_Bg': _L0_cond_in['Bg'], 'L0_cond_Au': _L0_cond_in['Au'], 'L0_cond_Bu': _L0_cond_in['Bu'], 'L0_cond_Ad': _L0_cond_in['Ad'], 'L0_cond_Bd': _L0_cond_in['Bd'], 'L0_ffn_Wr': _L0_ffn_in['Wr'], 'L0_ffn_Wg': _L0_ffn_in['Wg'], 'L0_ffn_Wu': _L0_ffn_in['Wu'], 'L0_ffn_Wd': _L0_ffn_in['Wd'], 'L1_cond_W': _L1_cond_in['W'], 'L1_cond_A': _L1_cond_in['A'], 'L1_cond_Bm': _L1_cond_in['Bm'], 'L1_cond_scalings': _L1_cond_in['scalings'], 'L1_ffn_gate_w': _L1_ffn_in['gate_w'], 'L1_ffn_w_up': _L1_ffn_in['w_up'], 'L1_ffn_w_gate': _L1_ffn_in['w_gate'], 'L1_ffn_w_down': _L1_ffn_in['w_down'], 'L1_ffn_up_A': _L1_ffn_in['up_A'], 'L1_ffn_up_B': _L1_ffn_in['up_B'], 'L1_ffn_gate_A': _L1_ffn_in['gate_A'], 'L1_ffn_gate_B': _L1_ffn_in['gate_B'], 'L1_ffn_down_A': _L1_ffn_in['down_A'], 'L1_ffn_down_B': _L1_ffn_in['down_B']}

def reference(x, itok_B_0_7, itok_B_0_6, L0_cond_Wg, L0_cond_Wu, L0_cond_Wd, L0_cond_Ag, L0_cond_Bg, L0_cond_Au, L0_cond_Bu, L0_cond_Ad, L0_cond_Bd, L0_ffn_Wr, L0_ffn_Wg, L0_ffn_Wu, L0_ffn_Wd, L1_cond_W, L1_cond_A, L1_cond_Bm, L1_cond_scalings, L1_ffn_gate_w, L1_ffn_w_up, L1_ffn_w_gate, L1_ffn_w_down, L1_ffn_up_A, L1_ffn_up_B, L1_ffn_gate_A, L1_ffn_gate_B, L1_ffn_down_A, L1_ffn_down_B):
    import jax
    import jax.numpy as jnp

    def _L0_cond_ref(x, Wg, Wu, Wd, Ag, Bg, Au, Bu, Ad, Bd, adapter_indices):
        import jax, jax.numpy as jnp
        import numpy as np

        def _lora_linear(x, W, A, B, adapter_indices):
            base = jnp.einsum('bsd,df->bsf', x, W)
            Ai = A[adapter_indices]
            Bi = B[adapter_indices]
            lora = jnp.einsum('bsr,brf->bsf', jnp.einsum('bsd,bdr->bsr', x, Ai), Bi)
            return base + lora
        gate = _lora_linear(x, Wg, Ag, Bg, adapter_indices)
        up = _lora_linear(x, Wu, Au, Bu, adapter_indices)
        h = jax.nn.silu(gate) * up
        return _lora_linear(h, Wd, Ad, Bd, adapter_indices)

    def _L0_ffn_ref(x, Wr, Wg, Wu, Wd):
        import jax, jax.numpy as jnp
        import numpy as np
        H = 256
        I = 176
        E = 8
        K = 2
        B, S = (2, 256)
        router_logits = jnp.einsum('bsh,he->bse', x, Wr)
        probs = jax.nn.softmax(router_logits.astype(jnp.float32), axis=-1)
        topk_w, topk_idx = jax.lax.top_k(probs, K)
        topk_w = topk_w / jnp.sum(topk_w, axis=-1, keepdims=True)
        onehot = jax.nn.one_hot(topk_idx, E, dtype=topk_w.dtype)
        combine = jnp.einsum('bsk,bske->bse', topk_w, onehot)
        g = jnp.einsum('bsh,ehi->besi', x, Wg)
        u = jnp.einsum('bsh,ehi->besi', x, Wu)
        h = jax.nn.silu(g) * u
        y = jnp.einsum('besi,eih->besh', h, Wd)
        out = jnp.einsum('bse,besh->bsh', combine.astype(x.dtype), y)
        return out

    def _L1_cond_ref(x, W, A, Bm, scalings, adapter_idx):
        import jax, jax.numpy as jnp
        import numpy as np
        B, T, D_IN, D_OUT = (16, 256, 256, 256)
        N_ADAPTERS, RANK = (8, 16)
        H = jnp.einsum('btd,od->bto', x, W)
        A_b = A[adapter_idx]
        B_b = Bm[adapter_idx]
        s_b = scalings[adapter_idx]
        xa = jnp.einsum('btd,brd->btr', x, A_b)
        delta = jnp.einsum('btr,bor->bto', xa, B_b)
        delta = jax.lax.stop_gradient(delta * s_b[:, None, None])
        return H + delta

    def _L1_ffn_ref(x, gate_w, w_up, w_gate, w_down, up_A, up_B, gate_A, gate_B, down_A, down_B):
        import jax, jax.numpy as jnp
        import numpy as np
        NUM_EXPERTS = 8
        TOP_K = 2
        LORA_ALPHA = 2.0
        LORA_RANK = 16
        D_MODEL = 256
        D_HIDDEN = 704
        B, S, D = x.shape
        H = w_up.shape[0]
        gate_logits = jnp.einsum('bsd,ed->bse', x, gate_w)
        topw, sel = jax.lax.top_k(gate_logits, TOP_K)
        topw = jax.nn.softmax(topw.astype(jnp.float32), axis=1).astype(x.dtype)
        xt = x.reshape(-1, D)
        wf = topw.reshape(-1, TOP_K)
        sf = sel.reshape(-1, TOP_K)
        base_up = xt @ w_up.T
        base_gate = xt @ w_gate.T
        mixed_h = jnp.zeros((xt.shape[0], H), x.dtype)
        lora_down = jnp.zeros_like(xt)
        for e in range(NUM_EXPERTS):
            c = jnp.sum(jnp.where(sf == e, wf, 0.0), axis=1)
            lo_up = LORA_ALPHA * (xt @ up_A[e].T @ up_B[e].T)
            lo_gate = LORA_ALPHA * (xt @ gate_A[e].T @ gate_B[e].T)
            h_e = jax.nn.silu(base_up + lo_up) * (base_gate + lo_gate)
            ch = c[:, None] * h_e
            mixed_h = mixed_h + ch
            lora_down = lora_down + LORA_ALPHA * (ch @ down_A[e].T @ down_B[e].T)
        out = mixed_h @ w_down.T + lora_down
        return out.reshape(B, S, D)
    x = x + _L0_ffn_ref(_L0_cond_ref(x, L0_cond_Wg, L0_cond_Wu, L0_cond_Wd, L0_cond_Ag, L0_cond_Bg, L0_cond_Au, L0_cond_Bu, L0_cond_Ad, L0_cond_Bd, itok_B_0_7), L0_ffn_Wr, L0_ffn_Wg, L0_ffn_Wu, L0_ffn_Wd)
    x = x + _L1_ffn_ref(_L1_cond_ref(x, L1_cond_W, L1_cond_A, L1_cond_Bm, L1_cond_scalings, itok_B_0_6), L1_ffn_gate_w, L1_ffn_w_up, L1_ffn_w_gate, L1_ffn_w_down, L1_ffn_up_A, L1_ffn_up_B, L1_ffn_gate_A, L1_ffn_gate_B, L1_ffn_down_A, L1_ffn_down_B)
    return x

_drawn_inputs = setup_inputs


def setup_inputs(seed=0):
    import zlib

    import numpy as np

    out = dict(_drawn_inputs(seed))
    spreads = {'L0_cond_Bg': (0.009999999776482582, 0.6),
     'L0_cond_Bu': (0.009999999776482582, 0.6),
     'L0_cond_Bd': (0.009999999776482582, 0.6),
     'L1_cond_scalings': (1.0, 0.6)}
    factors = {'L0_cond_Ag': 2.689,
     'L0_cond_Ad': 2.839,
     'L1_cond_A': 8.0,
     'L1_cond_Bm': 8.0,
     'L1_ffn_up_A': 8.0,
     'L1_ffn_up_B': 8.0,
     'L1_ffn_gate_A': 8.0,
     'L1_ffn_gate_B': 8.0,
     'L1_ffn_down_A': 8.0,
     'L1_ffn_down_B': 8.0}
    for name, (base, spread) in spreads.items():
        noise = np.random.default_rng([zlib.crc32(name.encode()), seed]).standard_normal(out[name].shape)
        drawn = base * np.exp(spread * noise) if base else spread * noise
        out[name] = jnp.asarray(drawn.astype(out[name].dtype))
    for name, factor in factors.items():
        out[name] = (out[name] * factor).astype(out[name].dtype)
    return out
```

```python
from contextlib import ExitStack

import numpy as np

import concourse.bass as bass
from concourse import mybir

P = 128
B, S, D = 128, 32, 256
T = B * S
G = 512
NG = T // G
GB = G // S
SUB = G // P
KD = D // P
E = 8
R = 16
I0 = 1024
C0 = I0 // P
IM = 176
CM = E * IM // P
H1 = 704
C1 = -(-H1 // P)
ALPHA = 2.0

F32 = mybir.dt.float32
F32R = mybir.dt.float32r
BF16 = mybir.dt.bfloat16
I32 = mybir.dt.int32
U32 = mybir.dt.uint32
ALU = mybir.AluOpType
ACT = mybir.ActivationFunctionType
X = mybir.AxisListType.X

BLK0 = 2 * D + 2 * P + D + P
W0_A = 0
W0_BLK = 2 * D
W0_BD = W0_BLK + C0 * BLK0
W0_WR = W0_BD + D
W0_COLS = W0_WR + KD * E
BLKM = 3 * D
WM_COLS = CM * BLKM
W1_A = 0
W1_W = D
W1_B = W1_W + KD * D
W1_GW = W1_B + D
W1_UA = W1_GW + KD * E
W1_GA = W1_UA + D
W1_BLK = W1_GA + D
BLK1 = 2 * D + 2 * P + P + D
W1_DB = W1_BLK + C1 * BLK1
W1_COLS = W1_DB + D

PIECES = 4
PM = -(-WM_COLS // (PIECES * (NG - 1)))
P1W = -(-W1_COLS // (PIECES * NG))
WM_PAD = PM * PIECES * (NG - 1)
W1_PAD = P1W * PIECES * NG
STAGE = max(PM, P1W)
SPLIT = W0_BLK + -(-(W1_PAD - W0_BLK) // P) * P
RING = 3

N_SEL1 = 5
NC0 = 3 * E
NC1 = 2 * E + 6


def reach(eng, sem, value):
    if isinstance(value, int) and value <= 0:
        return
    eng.wait_ge(sem, value)


def reach_then(eng, sem, value, passed):
    reach(eng, sem, value)
    if not isinstance(value, int):
        eng.sem_inc(passed, 1)


def mm3(pe, out, w, x, start, stop):
    (wh, wl), (xh, xl) = w, x
    pe.matmul(out, wh, xl, start=start, stop=False, skip_group_check=True)
    pe.matmul(out, wl, xh, start=False, stop=False, skip_group_check=True)
    return pe.matmul(out, wh, xh, start=False, stop=stop, skip_group_check=True)


def over_tokens(mask, t):
    return mask[:, bass.ds(t * GB, GB)].unsqueeze(2).broadcast_to([P, GB, S])


def by_batch(ap):
    return ap.rearrange("p (b s) -> p b s", s=S)


class Mem:

    def __init__(self, nc, memory, signals, prefix):
        self.nc, self.memory, self.signals, self.prefix = nc, memory, signals, prefix

    def sb(self, name, shape, dt=F32):
        return self.memory.enter_context(self.nc.sbuf_tensor(f"{self.prefix}_{name}", shape, dt))

    def pb(self, name, shape):
        return self.memory.enter_context(self.nc.psum_tensor(f"{self.prefix}_{name}", shape, F32))

    def sem(self, name):
        return self.signals.enter_context(self.nc.semaphore(f"{self.prefix}_{name}"))


def last_user(c, n, ring):
    return c - ring if c >= ring else max(b for b in range(n) if b % ring == c) - n


def over_groups(eng, body):
    body(0, True, False)
    with eng.Fori(1, NG - 1) as t:
        body(t, False, False)
    body(NG - 1, False, True)


def route0_steps(dve, k, lo, hi):
    base = k.group * ROUTE0
    z, ex, pr, v8, i8, if8, w2, st, o0, o1, c24 = k.t

    def each(a):
        return a.unsqueeze(2).broadcast_to([P, SUB, E])

    steps = [
        lambda: dve.reduce_max(st[:, :, 0], k.logits, X),
        lambda: dve.tensor_tensor(z[:, :, :], k.logits, each(st[:, :, 0]), ALU.subtract),
        lambda: dve.reduce_sum(st[:, :, 1], ex[:, :, :], X),
        lambda: dve.reciprocal(st[:, :, 2], st[:, :, 1]),
        lambda: dve.tensor_tensor(pr[:, :, :], ex[:, :, :], each(st[:, :, 2]), ALU.mult),
    ] + [
        (lambda s=s: dve.max(v8[:, s, :], pr[:, s, :])) for s in range(SUB)
    ] + [
        (lambda s=s: dve.max_index(i8[:, s, :], v8[:, s, :], pr[:, s, :])) for s in range(SUB)
    ] + [
        lambda: dve.tensor_tensor(st[:, :, 3], v8[:, :, 0], v8[:, :, 1], ALU.add),
        lambda: dve.reciprocal(st[:, :, 0], st[:, :, 3]),
        lambda: dve.tensor_tensor(w2[:, :, :], v8[:, :, 0:2], st[:, :, 0].unsqueeze(2).broadcast_to([P, SUB, 2]), ALU.mult),
        lambda: dve.tensor_copy(if8[:, :, :], i8[:, :, 0:2]),
        lambda: dve.tensor_tensor(o0[:, :, :], k.iota, each(if8[:, :, 0]), ALU.is_equal),
        lambda: dve.tensor_tensor(o1[:, :, :], k.iota, each(if8[:, :, 1]), ALU.is_equal),
        lambda: dve.tensor_tensor(o0[:, :, :], o0[:, :, :], each(w2[:, :, 0]), ALU.mult),
        lambda: dve.tensor_tensor(o1[:, :, :], o1[:, :, :], each(w2[:, :, 1]), ALU.mult),
        lambda: dve.tensor_tensor(o0[:, :, :], o0[:, :, :], o1[:, :, :], ALU.add),
        lambda: dve.tensor_copy(c24[:, :, 0:E], o0[:, :, :]),
        lambda: dve.tensor_tensor(o0[:, :, :], o0[:, :, :], c24[:, :, 0:E], ALU.subtract),
        lambda: dve.tensor_copy(c24[:, :, E:2 * E], o0[:, :, :]),
        lambda: dve.tensor_tensor(c24[:, :, 2 * E:3 * E], o0[:, :, :], c24[:, :, E:2 * E], ALU.subtract),
    ]
    assert len(steps) == ROUTE0
    for n in range(lo, hi):
        steps[n]().then_inc(k.route, 1)
        reach_then(dve, k.route, base + n + 1, k.passed)


def route1_steps(dve, k, lo, hi):
    base = k.group * ROUTE1
    vt, vr, er, wt, v8, i8, if8, st, c22, rest = k.t

    def each(a, n):
        return a.unsqueeze(2).broadcast_to([P, SUB, n])

    steps = [
        (lambda s=s: dve.max(v8[:, s, :], k.logits[:, s, :])) for s in range(SUB)
    ] + [
        (lambda s=s: dve.max_index(i8[:, s, :], v8[:, s, :], k.logits[:, s, :])) for s in range(SUB)
    ] + [
        lambda: dve.tensor_copy(vt[:, :, 0:2], v8[:, :, 0:2]),
        lambda: dve.transpose(vr[:, :], vt[:, :, :].rearrange("p s f -> p (s f)")),
        lambda: dve.reduce_max(st[:, :, 0], by_sub(vr), X),
        lambda: dve.tensor_tensor(by_sub(vr), by_sub(vr), each(st[:, :, 0], S), ALU.subtract),
        lambda: dve.reduce_sum(st[:, :, 1], by_sub(er), X),
        lambda: dve.reciprocal(st[:, :, 2], st[:, :, 1]),
        lambda: dve.tensor_tensor(by_sub(er), by_sub(er), each(st[:, :, 2], S), ALU.mult),
        lambda: dve.transpose(wt[:, :, :].rearrange("p s f -> p (s f)"), er[:, :]),
        lambda: dve.tensor_copy(if8[:, :, :], i8[:, :, 0:2]),
        lambda: dve.tensor_tensor(c22[:, :, 0:E], k.iota, each(if8[:, :, 0], E), ALU.is_equal),
        lambda: dve.tensor_tensor(c22[:, :, E:2 * E], k.iota, each(if8[:, :, 1], E), ALU.is_equal),
        lambda: dve.tensor_copy(c22[:, :, 2 * E:2 * E + 2], wt[:, :, 0:2]),
        lambda: dve.tensor_tensor(rest[:, :, :], wt[:, :, 0:2], c22[:, :, 2 * E:2 * E + 2], ALU.subtract),
        lambda: dve.tensor_copy(c22[:, :, 2 * E + 2:2 * E + 4], rest[:, :, :]),
        lambda: dve.tensor_tensor(c22[:, :, 2 * E + 4:2 * E + 6], rest[:, :, :], c22[:, :, 2 * E + 2:2 * E + 4], ALU.subtract),
    ]
    assert len(steps) == ROUTE1
    for n in range(lo, hi):
        steps[n]().then_inc(k.route, 1)
        reach_then(dve, k.route, base + n + 1, k.passed)


def by_sub(rows):
    return rows[:, :].rearrange("p (s t) -> p s t", t=S)


ROUTE0 = 26
EXP0 = 2
ROUTE1 = 23
EXP1 = 12


class Route:

    def __init__(self, group, passed, route, logits, iota, t):
        self.passed, self.group, self.route, self.logits, self.iota, self.t = passed, group, route, logits, iota, t


def phase_1(nc, A, big, signals):
    wh, wl, mh, ml, raw, cf, ident = (big[n] for n in ("wh", "wl", "mh", "ml", "raw", "cf", "ident"))
    iota = cf[:, 2:2 + SUB * E].rearrange("p (s e) -> p s e", e=E)

    def parts(a, b):
        if a >= SPLIT:
            return big["xwh"][:, a - SPLIT:b - SPLIT], big["xwl"][:, a - SPLIT:b - SPLIT]
        assert b <= SPLIT
        return wh[:, a:b], wl[:, a:b]

    with ExitStack() as memory:
        m = Mem(nc, memory, signals, "p1")
        sp_passed, dve_passed, pool_passed = m.sem("sp_passed"), m.sem("dve_passed"), m.sem("pool_passed")
        xraw = m.sb("xraw", [P, KD, G])
        xh, xl = m.sb("xh", [P, KD, G], F32R), m.sb("xl", [P, KD, G], F32R)
        xam = m.sb("xam", [P, 2, G])
        xah, xal = m.sb("xah", [P, 2, G], F32R), m.sb("xal", [P, 2, G], F32R)
        s = m.sb("s", [P, 2, G])
        hh, hl = m.sb("hh", [P, RING, G], F32R), m.sb("hl", [P, RING, G], F32R)
        dm = xam[:, 0, :]
        dh, dl = m.sb("dh", [P, G], F32R), m.sb("dl", [P, G], F32R)
        of = m.sb("of", [P, KD, G])
        oh, ol = m.sb("oh", [P, KD, G], F32R), m.sb("ol", [P, KD, G], F32R)
        stage = m.sb("stage", [P, 2, PM])
        mask = m.sb("mask", [P, B])
        idx = of[:, 0, 0:B].bitcast(I32)
        tiles = [m.sb(n, [P, SUB, w], dt) for n, w, dt in (
            ("z", E, F32), ("ex", E, F32), ("pr", E, F32), ("v8", 8, F32), ("i8", 8, U32), ("if8", 2, F32),
            ("w2", 2, F32), ("st", 4, F32), ("o0", E, F32), ("o1", E, F32), ("c24", NC0, BF16))]
        z, ex, c24 = tiles[0], tiles[1], tiles[-1]
        cT = m.sb("cT", [NC0, G], BF16)

        pair = [[m.pb(f"pair{i}{j}", [P, G]) for j in range(2)] for i in range(2)]
        po = m.pb("po", [P, KD, G])
        pd = m.pb("pd", [P, G])
        pm = m.pb("pm", [P, G])
        logits = pm[:, 0:SUB * E].rearrange("p (s e) -> p s e", e=E)
        turned = pm[:, :].bitcast(BF16)[0:NC0, 0:G]

        raw_in = [m.sem(f"raw_in{n}") for n in range(C0 + 3)]
        (w_hi, w_lo, x_in, x_hi, x_lo, idx_in, mask_made, xa_done, xa_masked, xa_hi, xa_lo, gu_done, s_done,
         h_done, h_hi, h_lo, down_done, d_masked, d_hi, d_lo, out_done, out_hi, out_f, out_lo, stored,
         logits_done, route, e_done, turned_done, cT_done, cT_stored, piece_hi, piece_lo) = (
            m.sem(n) for n in (
                "w_hi w_lo x_in x_hi x_lo idx_in mask_made xa_done xa_masked xa_hi xa_lo gu_done s_done "
                "h_done h_hi h_lo down_done d_masked d_hi d_lo out_done out_hi out_f out_lo stored "
                "logits_done route e_done turned_done cT_done cT_stored piece_hi piece_lo").split())
        piece_in = [m.sem(f"piece_in{n}") for n in range(2)]

        x_v = A["xT"].rearrange("(k p) t -> p k t", p=P)
        h_v = A["h"].rearrange("(k p) t -> p k t", p=P)
        ends = [0, W0_BLK] + [W0_BLK + (c + 1) * BLK0 for c in range(C0)] + [W0_COLS]
        cuts = list(zip(sorted({*ends[:-1], SPLIT}), sorted({*ends[1:], SPLIT})))
        split_for = [sum(b <= ends[c + 2] for _, b in cuts) for c in range(C0)]

        def w(o, n=P):
            return parts(o, o + n)

        def x(k):
            return xh[:, k, :], xl[:, k, :]

        def free_slot(c):
            return last_user(c, C0, RING)

        with nc.Block() as block:
            @block.sync
            def _(sp):
                sp.dma_start(xraw[:, :, :], x_v[:, :, 0:G]).then_inc(x_in, 16)
                sp.dma_start(raw[:, cuts[0][0]:cuts[0][1]], A["w0"][:, cuts[0][0]:cuts[0][1]]).then_inc(raw_in[0], 16)
                sp.dma_start(idx, A["idx0"].partition_broadcast(P)).then_inc(idx_in, 16)
                for n, (a, b) in enumerate(cuts[1:]):
                    sp.dma_start(raw[:, a:b], A["w0"][:, a:b]).then_inc(raw_in[n + 1], 16)

                def store(t):
                    reach_then(sp, out_f, t + 1, sp_passed)
                    sp.dma_start(h_v[:, :, bass.ds(t * G, G)], of[:, :, :]).then_inc(stored, 16)

                def store_routing(t):
                    reach_then(sp, cT_done, t + 1, sp_passed)
                    sp.dma_start(A["comb"][:, bass.ds(t * G, G)], cT[:, :]).then_inc(cT_stored, 16)

                def body(t, first, last):
                    if not last:
                        reach_then(sp, x_lo, t + 1, sp_passed)
                        sp.dma_start(xraw[:, :, :], x_v[:, :, bass.ds((t + 1) * G, G)]).then_inc(x_in, 16)
                    if first:
                        return
                    for j in range(PIECES):
                        n = (t - 1) * PIECES + j
                        reach_then(sp, piece_lo, n + 1, sp_passed)
                        sp.dma_start(stage[:, j % 2, :], A["wm"][:, bass.ds(n * PM, PM)]).then_inc(piece_in[j % 2], 16)
                        if j == 1:
                            store(t - 1)
                    store_routing(t - 1)

                over_groups(sp, body)
                store(NG - 1)
                store_routing(NG - 1)
                sp.wait_ge(stored, 16 * NG)
                sp.wait_ge(cT_stored, 16 * NG)

            @block.tensor
            def _(pe):
                def adapters(t):
                    pe.wait_ge(x_lo, t + 1)
                    reach(pe, cT_done, t - 1)
                    for j in range(2):
                        if j == 1:
                            reach(pe, h_done, t * C0)
                        out = (pm, pair[1][0])[j]
                        for k in range(KD):
                            last = mm3(pe, out[:, :], w(W0_A + (j * KD + k) * P), x(k), k == 0, k == KD - 1)
                        last.then_inc(xa_done, 1)

                def gate_up(t, c, first):
                    if first:
                        pe.wait_ge(w_lo, split_for[c])
                    reach(pe, h_done, t * C0 + c - 1)
                    o = W0_BLK + c * BLK0
                    for j in range(2):
                        for k in range(KD):
                            mm3(pe, pair[c % 2][j][:, :], w(o + (j * KD + k) * P), x(k), k == 0, False)
                    for j in range(2):
                        if c == 0:
                            pe.wait_ge(xa_lo, 2 * t + j + 1)
                        last = mm3(pe, pair[c % 2][j][:, :], w(o + 2 * D + j * P), (xah[:, j, :], xal[:, j, :]), False, True)
                    last.then_inc(gu_done, 1)

                def down(t, c):
                    pe.wait_ge(h_lo, t * C0 + c + 1)
                    if c == 0:
                        reach(pe, d_masked, t)
                        reach(pe, out_hi, t)
                        reach(pe, out_f, t)
                        reach(pe, out_lo, t)
                    o = W0_BLK + c * BLK0 + 2 * D + 2 * P
                    h = hh[:, c % RING, :], hl[:, c % RING, :]
                    mm3(pe, pd[:, :], w(o + D), h, c == 0, c == C0 - 1)
                    for k in range(KD):
                        last = mm3(pe, po[:, k, :], w(o + k * P), h, c == 0, False)
                    last.then_inc(down_done, 1)

                def adapted(t):
                    pe.wait_ge(d_lo, t + 1)
                    for k in range(KD):
                        last = mm3(pe, po[:, k, :], w(W0_BD + k * P), (dh[:, :], dl[:, :]), False, True)
                    last.then_inc(out_done, 1)

                def route_logits(t):
                    pe.wait_ge(out_lo, t + 1)
                    for b in range(SUB):
                        tok = slice(b * P, (b + 1) * P)
                        for k in range(KD):
                            last = mm3(pe, logits[:, b, :], (oh[:, k, tok], ol[:, k, tok]), w(W0_WR + k * E, E),
                                       k == 0, k == KD - 1)
                    last.then_inc(logits_done, 1)

                def route_turn(t):
                    pe.wait_ge(route, (t + 1) * ROUTE0)
                    for b in range(SUB):
                        last = pe.transpose(turned[:, b * P:(b + 1) * P], c24[:, b, :], ident[:, :])
                    last.then_inc(turned_done, 1)

                def body(t, first, last):
                    for c in range(C0):
                        gate_up(t, c, first)
                        if c == 0 and not first:
                            adapted(t - 1)
                        if c >= 2:
                            down(t, c - 2)
                        if c == 2 and not first:
                            route_logits(t - 1)
                    if not first:
                        route_turn(t - 1)
                    down(t, C0 - 2)
                    if not last:
                        adapters(t + 1)
                    down(t, C0 - 1)

                pe.wait_ge(w_lo, 1)
                adapters(0)
                over_groups(pe, body)
                adapted(NG - 1)
                route_logits(NG - 1)
                route_turn(NG - 1)

            @block.scalar
            def _(act):
                def split_weights(n):
                    a, b = cuts[n]
                    act.wait_ge(raw_in[n], 16)
                    nc.scalar.copy(parts(a, b)[0], raw[:, a:b]).then_inc(w_hi, 1)

                def split_x(t):
                    act.wait_ge(x_in, 16 * (t + 1))
                    reach(act, gu_done, t * C0)
                    nc.scalar.copy(xh[:, :, :], xraw[:, :, :]).then_inc(x_hi, 1)

                def split_adapters(t):
                    for j in range(2):
                        act.wait_ge(xa_masked, 2 * t + j + 1)
                        nc.scalar.copy(xah[:, j, :], xam[:, j, :]).then_inc(xa_hi, 1)

                def silu(t, c):
                    act.wait_ge(gu_done, t * C0 + c + 1)
                    reach(act, h_lo, t * C0 + c - 1)
                    nc.scalar.activation(s[:, c % 2, :], pair[c % 2][0][:, :], ACT.Silu).then_inc(s_done, 1)

                def split_hidden(t, c):
                    act.wait_ge(h_done, t * C0 + c + 1)
                    reach(act, down_done, t * C0 + free_slot(c) + 1)
                    nc.scalar.copy(hh[:, c % RING, :], s[:, c % 2, :]).then_inc(h_hi, 1)

                def split_down(t):
                    act.wait_ge(d_masked, t + 1)
                    reach(act, out_done, t)
                    nc.scalar.copy(dh[:, :], dm).then_inc(d_hi, 1)

                def take_output(t):
                    act.wait_ge(out_done, t + 1)
                    reach(act, logits_done, t)
                    nc.scalar.copy(oh[:, :, :], po[:, :, :]).then_inc(out_hi, 1)
                    reach(act, stored, 16 * t)
                    nc.scalar.copy(of[:, :, :], po[:, :, :]).then_inc(out_f, 1)

                def route_exp(t):
                    act.wait_ge(route, t * ROUTE0 + EXP0)
                    nc.scalar.activation(ex[:, :, :], z[:, :, :], ACT.Exp).then_inc(e_done, 1)

                def take_routing(t):
                    act.wait_ge(turned_done, t + 1)
                    reach(act, cT_stored, 16 * t)
                    nc.scalar.copy(cT[:, :], turned).then_inc(cT_done, 1)

                def body(t, first, last):
                    if not first:
                        split_down(t - 1)
                    for c in range(C0):
                        if first:
                            for n in range(split_for[c], split_for[c + 1] if c + 1 < C0 else len(cuts)):
                                split_weights(n)
                        silu(t, c)
                        if c == 0 and not first:
                            take_output(t - 1)
                        if c >= 1:
                            split_hidden(t, c - 1)
                        if c == 3 and not first:
                            route_exp(t - 1)
                    if not first:
                        take_routing(t - 1)
                    if not last:
                        split_x(t + 1)
                    split_hidden(t, C0 - 1)
                    if not last:
                        split_adapters(t + 1)

                split_weights(0)
                split_x(0)
                split_weights(1)
                split_adapters(0)
                over_groups(act, body)
                split_down(NG - 1)
                take_output(NG - 1)
                route_exp(NG - 1)
                take_routing(NG - 1)

            @block.vector
            def _(dve):
                def split_weights(n):
                    a, b = cuts[n]
                    dve.wait_ge(w_hi, n + 1)
                    nc.vector.tensor_tensor(parts(a, b)[1], raw[:, a:b], parts(a, b)[0], ALU.subtract).then_inc(w_lo, 1)

                def split_x(t):
                    dve.wait_ge(x_hi, t + 1)
                    nc.vector.tensor_tensor(xl[:, :, :], xraw[:, :, :], xh[:, :, :], ALU.subtract).then_inc(x_lo, 1)

                def mask_adapters(t):
                    for j in range(2):
                        dve.wait_ge(xa_done, 2 * t + j + 1)
                        if j == 0:
                            reach(dve, d_lo, t - 1)
                        else:
                            reach(dve, xa_lo, 2 * t)
                        nc.vector.tensor_tensor(by_batch(xam[:, j, :]), by_batch((pm, pair[1][0])[j][:, :]),
                                                over_tokens(mask, t), ALU.mult).then_inc(xa_masked, 1)
                    for j in range(2):
                        dve.wait_ge(xa_hi, 2 * t + j + 1)
                        nc.vector.tensor_tensor(xal[:, j, :], xam[:, j, :], xah[:, j, :], ALU.subtract).then_inc(xa_lo, 1)

                def hidden(t, c):
                    dve.wait_ge(s_done, t * C0 + c + 1)
                    nc.vector.tensor_tensor(s[:, c % 2, :], s[:, c % 2, :], pair[c % 2][1][:, :], ALU.mult).then_inc(h_done, 1)

                def mask_down(t):
                    dve.wait_ge(down_done, (t + 1) * C0)
                    dve.wait_ge(xa_lo, 2 * NG if isinstance(t, int) and t == NG - 1 else 2 * (t + 2))
                    nc.vector.tensor_tensor(by_batch(dm), by_batch(pd[:, :]), over_tokens(mask, t),
                                            ALU.mult).then_inc(d_masked, 1)
                    dve.wait_ge(d_hi, t + 1)
                    nc.vector.tensor_tensor(dl[:, :], dm, dh[:, :], ALU.subtract).then_inc(d_lo, 1)

                def split_output(t):
                    dve.wait_ge(out_f, t + 1)
                    nc.vector.tensor_tensor(ol[:, :, :], po[:, :, :], oh[:, :, :], ALU.subtract).then_inc(out_lo, 1)

                def route_part(t, part):
                    r = Route(t, dve_passed, route, logits, iota, tiles)
                    if part == 0:
                        dve.wait_ge(logits_done, t + 1)
                        route0_steps(nc.vector, r, 0, EXP0)
                    elif part == 1:
                        dve.wait_ge(e_done, t + 1)
                        route0_steps(nc.vector, r, EXP0, 13)
                    elif part == 2:
                        route0_steps(nc.vector, r, 13, 22)
                    else:
                        reach(dve, turned_done, t)
                        route0_steps(nc.vector, r, 22, ROUTE0)

                def body(t, first, last):
                    if not first:
                        mask_down(t - 1)
                    for c in range(C0):
                        if first:
                            for n in range(split_for[c], split_for[c + 1] if c + 1 < C0 else len(cuts)):
                                split_weights(n)
                        hidden(t, c)
                        if first:
                            continue
                        if c == 0:
                            split_output(t - 1)
                        if c >= 3 and c < 7:
                            route_part(t - 1, c - 3)
                    if not last:
                        split_x(t + 1)
                        mask_adapters(t + 1)

                dve.wait_ge(idx_in, 16)
                dve.wait_ge(big["cst_in"], 32)
                nc.vector.tensor_scalar(mask[:, :], idx, cf[:, 0:1], None, ALU.is_equal).then_inc(mask_made, 1)
                split_weights(0)
                split_x(0)
                split_weights(1)
                dve.wait_ge(mask_made, 1)
                mask_adapters(0)
                over_groups(dve, body)
                mask_down(NG - 1)
                split_output(NG - 1)
                for part in range(4):
                    route_part(NG - 1, part)

            @block.gpsimd
            def _(pool):
                def body(t, first, last):
                    for c in range(C0):
                        pool.wait_ge(h_hi, t * C0 + c + 1)
                        nc.gpsimd.tensor_tensor(hl[:, c % RING, :], s[:, c % 2, :], hh[:, c % RING, :],
                                                ALU.subtract).then_inc(h_lo, 1)
                        if not first and c % 2 == 1:
                            split_piece(t, c // 2)

                def split_piece(t, j):
                    n = (t - 1) * PIECES + j
                    pool.wait_ge(piece_in[j % 2], 16 * ((t - 1) * (PIECES // 2) + j // 2 + 1))
                    pool.wait_ge(w_lo, len(cuts))
                    nc.gpsimd.tensor_copy(mh[:, bass.ds(n * PM, PM)], stage[:, j % 2, :]).then_inc(piece_hi, 1)
                    pool.wait_ge(piece_hi, n + 1)
                    nc.gpsimd.tensor_tensor(ml[:, bass.ds(n * PM, PM)], stage[:, j % 2, :], mh[:, bass.ds(n * PM, PM)],
                                            ALU.subtract).then_inc(piece_lo, 1)

                pool.sem_inc(piece_lo, 2)
                over_groups(pool, body)


def phase_2(nc, A, big, signals):
    wh, wl, mh, ml = (big[n] for n in ("wh", "wl", "mh", "ml"))
    with ExitStack() as memory:
        m = Mem(nc, memory, signals, "p2")
        sp_passed, dve_passed, pool_passed = m.sem("sp_passed"), m.sem("dve_passed"), m.sem("pool_passed")
        xraw = m.sb("xraw", [P, KD, G])
        xh, xl = m.sb("xh", [P, KD, G], F32R), m.sb("xl", [P, KD, G], F32R)
        s = m.sb("s", [P, 2, G])
        hh, hl = m.sb("hh", [P, RING, G], F32R), m.sb("hl", [P, RING, G], F32R)
        of = m.sb("of", [P, KD, G])
        stage = m.sb("stage", [P, 2, P1W])
        sel = m.sb("sel", [NC0, CM * P], BF16)
        cin = m.sb("cin", [NC0, G], BF16)
        cT = m.sb("cT", [NC0, G], BF16)

        pair = [[m.pb(f"pair{i}{j}", [P, G]) for j in range(2)] for i in range(2)]
        po = m.pb("po", [P, KD, G])
        pc = [m.pb(f"pc{i}", [P, G]) for i in range(2)]

        (x_in, x_hi, x_lo, c_in, c_copied, gu_done, cb_done, s_done, hu_done, h_done, h_hi, h_lo, down_done,
         out_done, res_in, added, stored, piece_hi, piece_lo, sel_in) = (m.sem(n) for n in (
             "x_in x_hi x_lo c_in c_copied gu_done cb_done s_done hu_done h_done h_hi h_lo down_done "
             "out_done res_in added stored piece_hi piece_lo sel_in").split())
        piece_in = [m.sem(f"piece_in{n}") for n in range(2)]

        x_v = A["xT"].rearrange("(k p) t -> p k t", p=P)
        h_v = A["h"].rearrange("(k p) t -> p k t", p=P)
        x1_v = A["x1"].rearrange("(k p) t -> p k t", p=P)

        def w(o, n=P):
            return mh[:, o:o + n], ml[:, o:o + n]

        def x(k):
            return xh[:, k, :], xl[:, k, :]

        def pair_free(t, c):
            return t * CM + last_user(c, CM, 2) + 1

        with nc.Block() as block:
            @block.sync
            def _(sp):
                def load(t):
                    if not (isinstance(t, int) and t == 0):
                        reach_then(sp, x_lo, t, sp_passed)
                    sp.dma_start(xraw[:, :, :], h_v[:, :, bass.ds(t * G, G)]).then_inc(x_in, 16)
                    if not (isinstance(t, int) and t == 0):
                        reach_then(sp, c_copied, t, sp_passed)
                    sp.dma_start(cin[:, :], A["comb"][:, bass.ds(t * G, G)]).then_inc(c_in, 16)

                def body(t, first, last):
                    if not first:
                        store(t - 1)
                    if not (isinstance(t, int) and t == 0):
                        reach_then(sp, stored, 16 * t, sp_passed)
                    sp.dma_start(of[:, :, :], x_v[:, :, bass.ds(t * G, G)]).then_inc(res_in, 16)
                    if not last:
                        load(t + 1)
                    for j in range(PIECES):
                        n = t * PIECES + j
                        reach_then(sp, piece_lo, n + 1, sp_passed)
                        sp.dma_start(stage[:, j % 2, :], A["w1"][:, bass.ds(n * P1W, P1W)]).then_inc(piece_in[j % 2], 16)

                def store(t):
                    reach_then(sp, added, t + 1, sp_passed)
                    sp.dma_start(x1_v[:, :, bass.ds(t * G, G)], of[:, :, :]).then_inc(stored, 16)

                sp.dma_start(sel[:, :], A["sel_m"]).then_inc(sel_in, 16)
                load(0)
                over_groups(sp, body)
                store(NG - 1)
                sp.wait_ge(stored, 16 * NG)

            @block.tensor
            def _(pe):
                def gate_up(t, c):
                    if c == 0:
                        pe.wait_ge(x_lo, t + 1)
                    reach(pe, hu_done, pair_free(t, c))
                    for j in range(2):
                        for k in range(KD):
                            last = mm3(pe, pair[c % 2][j][:, :], w(c * BLKM + (j * KD + k) * P), x(k), k == 0, k == KD - 1)
                    last.then_inc(gu_done, 1)
                    if c == 0:
                        pe.wait_ge(c_copied, t + 1)
                    reach(pe, h_done, pair_free(t, c))
                    pe.matmul(pc[c % 2][:, :], sel[:, c * P:(c + 1) * P], cT[:, :],
                              start=True, stop=True).then_inc(cb_done, 1)

                def down(t, c):
                    pe.wait_ge(h_lo, t * CM + c + 1)
                    if c == 0:
                        reach(pe, added, t)
                    for k in range(KD):
                        last = mm3(pe, po[:, k, :], w(c * BLKM + 2 * D + k * P), (hh[:, c % RING, :], hl[:, c % RING, :]),
                                   c == 0, c == CM - 1)
                    last.then_inc(down_done, 1)

                def body(t, first, last):
                    for c in range(CM):
                        gate_up(t, c)
                        if c >= 2:
                            down(t, c - 2)
                    down(t, CM - 2)
                    down(t, CM - 1)

                pe.wait_ge(sel_in, 16)
                over_groups(pe, body)

            @block.scalar
            def _(act):
                def split_x(t):
                    act.wait_ge(x_in, 16 * (t + 1))
                    reach(act, gu_done, t * CM)
                    nc.scalar.copy(xh[:, :, :], xraw[:, :, :]).then_inc(x_hi, 1)

                def silu(t, c):
                    act.wait_ge(gu_done, t * CM + c + 1)
                    reach(act, h_lo, pair_free(t, c))
                    nc.scalar.activation(s[:, c % 2, :], pair[c % 2][0][:, :], ACT.Silu).then_inc(s_done, 1)

                def split_hidden(t, c):
                    act.wait_ge(h_done, t * CM + c + 1)
                    reach(act, down_done, t * CM + last_user(c, CM, RING) + 1)
                    nc.scalar.copy(hh[:, c % RING, :], s[:, c % 2, :]).then_inc(h_hi, 1)

                def body(t, first, last):
                    for c in range(CM):
                        if c == 0 and not first:
                            split_hidden(t - 1, CM - 1)
                        silu(t, c)
                        if c >= 1:
                            split_hidden(t, c - 1)
                    if not last:
                        split_x(t + 1)

                split_x(0)
                over_groups(act, body)
                split_hidden(NG - 1, CM - 1)

            @block.vector
            def _(dve):
                def split_x(t):
                    dve.wait_ge(x_hi, t + 1)
                    nc.vector.tensor_tensor(xl[:, :, :], xraw[:, :, :], xh[:, :, :], ALU.subtract).then_inc(x_lo, 1)

                def hidden(t, c):
                    dve.wait_ge(s_done, t * CM + c + 1)
                    nc.vector.tensor_tensor(s[:, c % 2, :], s[:, c % 2, :], pair[c % 2][1][:, :], ALU.mult).then_inc(hu_done, 1)
                    dve.wait_ge(hu_done, t * CM + c + 1)
                    dve.wait_ge(cb_done, t * CM + c + 1)
                    nc.vector.tensor_tensor(s[:, c % 2, :], s[:, c % 2, :], pc[c % 2][:, :], ALU.mult).then_inc(h_done, 1)

                def add(t):
                    dve.wait_ge(down_done, (t + 1) * CM)
                    dve.wait_ge(res_in, 16 * (t + 1))
                    nc.vector.tensor_tensor(of[:, :, :], of[:, :, :], po[:, :, :], ALU.add).then_inc(added, 1)

                def body(t, first, last):
                    for c in range(CM):
                        hidden(t, c)
                        if c == 0 and not first:
                            add(t - 1)
                    if not last:
                        split_x(t + 1)

                split_x(0)
                over_groups(dve, body)
                add(NG - 1)

            @block.gpsimd
            def _(pool):
                def copy_c(t):
                    reach(pool, cb_done, t * CM)
                    reach_then(pool, c_in, 16 * (t + 1), pool_passed)
                    nc.gpsimd.tensor_copy(cT[:, :], cin[:, :]).then_inc(c_copied, 1)

                def split_piece(t, j):
                    n = t * PIECES + j
                    reach_then(pool, piece_in[j % 2], 16 * (t * (PIECES // 2) + j // 2 + 1), pool_passed)
                    nc.gpsimd.tensor_copy(wh[:, bass.ds(n * P1W, P1W)], stage[:, j % 2, :]).then_inc(piece_hi, 1)
                    pool.wait_ge(piece_hi, n + 1)
                    nc.gpsimd.tensor_tensor(wl[:, bass.ds(n * P1W, P1W)], stage[:, j % 2, :], wh[:, bass.ds(n * P1W, P1W)],
                                            ALU.subtract).then_inc(piece_lo, 1)

                def body(t, first, last):
                    for c in range(CM):
                        pool.wait_ge(h_hi, t * CM + c + 1)
                        nc.gpsimd.tensor_tensor(hl[:, c % RING, :], s[:, c % 2, :], hh[:, c % RING, :],
                                                ALU.subtract).then_inc(h_lo, 1)
                        if c % 2 == 1 and c < 2 * PIECES:
                            split_piece(t, c // 2)
                    if not last:
                        copy_c(t + 1)

                pool.sem_inc(piece_lo, 2)
                copy_c(0)
                over_groups(pool, body)


EVENTS = [(0, 0)] + [e for c in range(1, C1) for e in ((c, 0), (c - 1, 1))] + [(C1 - 1, 1)]
NE = len(EVENTS)
AT = {e: n for n, e in enumerate(EVENTS)}


def phase_3(nc, A, big, signals):
    wh, wl, cf, ident = (big[n] for n in ("wh", "wl", "cf", "ident"))
    iota = cf[:, 2:2 + SUB * E].rearrange("p (s e) -> p s e", e=E)
    with ExitStack() as memory:
        m = Mem(nc, memory, signals, "p3")
        sp_passed, dve_passed, pool_passed = m.sem("sp_passed"), m.sem("dve_passed"), m.sem("pool_passed")
        xraw = m.sb("xraw", [P, KD, G])
        xh, xl = m.sb("xh", [P, KD, G], F32R), m.sb("xl", [P, KD, G], F32R)
        xam = m.sb("xam", [P, G])
        xah, xal = m.sb("xah", [P, G], F32R), m.sb("xal", [P, G], F32R)
        yh, yl = m.sb("yh", [P, 2, KD, G], F32R), m.sb("yl", [P, 2, KD, G], F32R)
        ua = m.sb("ua", [P, 2, G])
        um = m.sb("um", [P, 2, G])
        uh, ul = m.sb("uh", [P, 4, G], F32R), m.sb("ul", [P, 4, G], F32R)
        mk = m.sb("mk", [P, 2, 3, G], BF16)
        wv = m.sb("wv", [P, 2, 2, G])
        s = m.sb("s", [P, 2, 2, G])
        ch, cl = m.sb("ch", [P, 2, 2, G], F32R), m.sb("cl", [P, 2, 2, G], F32R)
        mx = m.sb("mx", [P, 2, G])
        mh, ml = m.sb("mh", [P, C1, G], F32R), m.sb("ml", [P, C1, G], F32R)
        ta = um
        th, tl = m.sb("th", [P, G], F32R), m.sb("tl", [P, G], F32R)
        yo = m.sb("yo", [P, KD, G])
        mask = m.sb("mask", [P, B])
        idx = yo[:, 0, 0:B].bitcast(I32)
        vt = m.sb("vt", [P, SUB, S])
        vr = m.sb("vr", [P, SUB * S])
        v8 = m.sb("v8", [P, SUB, 8])
        i8 = m.sb("i8", [P, SUB, 8], U32)
        if8 = m.sb("if8", [P, SUB, 2])
        st = m.sb("st", [P, SUB, 3])
        c22 = m.sb("c22", [P, SUB, NC1], BF16)
        rest = m.sb("rest", [P, SUB, 2])
        cT = m.sb("cT", [NC1, G], BF16)
        sel = m.sb("sel", [NC1, N_SEL1 * P], BF16)
        tiles = (vt, vr, vr, vt, v8, i8, if8, st, c22, rest)

        pair = [[m.pb(f"pair{i}{j}", [P, G]) for j in range(2)] for i in range(2)]
        pa = m.pb("pa", [P, 2, G])
        pf = m.pb("pf", [P, 2, G])
        logits = pf[:, 1, 0:SUB * E].rearrange("p (s e) -> p s e", e=E)
        turned = pf[:, 0, :].bitcast(BF16)[0:NC1, 0:G]

        (x_in, x_hi, x_lo, idx_in, mask_made, vt_zero, xa_done, xa_masked, xa_hi, xa_lo, y_done, y_hi, y_lo,
         logits_done, route, e_done, ua_done, ua_copied, turned_done, turned_copied, bc_done, bc_copied, um_done,
         u_hi, u_lo, p_done, s_done, m_done, c_done, c_hi, c_lo, acc_done, mix_done, mix_hi, mix_lo, down_done,
         t_masked, t_done, t_hi, t_lo, out_done, res_in, added, stored, sel_in) = (m.sem(n) for n in (
             "x_in x_hi x_lo idx_in mask_made vt_zero xa_done xa_masked xa_hi xa_lo y_done y_hi y_lo "
             "logits_done route e_done ua_done ua_copied turned_done turned_copied bc_done bc_copied um_done "
             "u_hi u_lo p_done s_done m_done c_done c_hi c_lo acc_done mix_done mix_hi mix_lo down_done "
             "t_masked t_done t_hi t_lo out_done res_in added stored sel_in").split())

        x1_v = A["x1"].rearrange("(k p) t -> p k t", p=P)
        out_v = A["out"].rearrange("(k p) t -> p k t", p=P)

        def w(o, n=P):
            return wh[:, o:o + n], wl[:, o:o + n]

        def x(k):
            return xh[:, k, :], xl[:, k, :]

        def event(t, c, slot):
            if c < 0:
                return (t - 1) * NE + AT[(c + C1, slot)] + 1
            return t * NE + AT[(c, slot)] + 1

        def over_pairs(eng, body):
            body(0, 0, True, False)
            with eng.Fori(0, NG // 2 - 1) as i:
                body(i * 2 + 1, 1, False, False)
                body(i * 2 + 2, 0, False, False)
            body(NG - 1, 1, False, True)

        BC = [(0, 1), (1, 0), (2, 1), (3, 0), (4, 1)]

        with nc.Block() as block:
            @block.sync
            def _(sp):
                def load(t):
                    if not (isinstance(t, int) and t == 0):
                        reach_then(sp, x_lo, t, sp_passed)
                    sp.dma_start(xraw[:, :, :], x1_v[:, :, bass.ds(t * G, G)]).then_inc(x_in, 16)

                def store(t):
                    reach_then(sp, added, t + 1, sp_passed)
                    sp.dma_start(out_v[:, :, bass.ds(t * G, G)], yo[:, :, :]).then_inc(stored, 16)

                def body(t, q, first, last):
                    if not last:
                        load(t + 1)
                    if not first:
                        store(t - 1)
                    if first:
                        sp.wait_ge(mask_made, 1)
                    if not (isinstance(t, int) and t == 0):
                        reach_then(sp, stored, 16 * t, sp_passed)
                    sp.dma_start(yo[:, :, :], x1_v[:, :, bass.ds(t * G, G)]).then_inc(res_in, 16)

                sp.dma_start(idx, A["idx1"].partition_broadcast(P)).then_inc(idx_in, 16)
                sp.dma_start(sel[:, :], A["sel_1"]).then_inc(sel_in, 16)
                load(0)
                over_pairs(sp, body)
                store(NG - 1)
                sp.wait_ge(stored, 16 * NG)

            @block.tensor
            def _(pe):
                def adapters(g):
                    pe.wait_ge(x_lo, g + 1)
                    reach(pe, added, g - 1)
                    for k in range(KD):
                        last = mm3(pe, pf[:, 0, :], w(W1_A + k * P), x(k), k == 0, k == KD - 1)
                    last.then_inc(xa_done, 1)

                def project(g):
                    pe.wait_ge(xa_lo, g + 1)
                    for o in range(KD):
                        for k in range(KD):
                            mm3(pe, pf[:, o, :], w(W1_W + k * D + o * P), x(k), k == 0, False)
                        last = mm3(pe, pf[:, o, :], w(W1_B + o * P), (xah[:, :], xal[:, :]), False, True)
                    last.then_inc(y_done, 1)

                def prepare_c(g, q):
                    pe.wait_ge(y_lo, g + 1)
                    for b in range(SUB):
                        tok = slice(b * P, (b + 1) * P)
                        for k in range(KD):
                            last = mm3(pe, logits[:, b, :], (yh[:, q, k, tok], yl[:, q, k, tok]), w(W1_GW + k * E, E),
                                       k == 0, k == KD - 1)
                    last.then_inc(logits_done, 1)
                    for k in range(KD):
                        last = mm3(pe, pf[:, 0, :], w(W1_UA + k * P), (yh[:, q, k, :], yl[:, q, k, :]), k == 0, k == KD - 1)
                    last.then_inc(ua_done, 1)

                def prepare_ag(g, q):
                    pe.wait_ge(route, g * ROUTE1 + 8)
                    for k in range(KD):
                        last = mm3(pe, pf[:, 1, :], w(W1_GA + k * P), (yh[:, q, k, :], yl[:, q, k, :]), k == 0, k == KD - 1)
                    last.then_inc(ua_done, 1)

                def turn(g):
                    pe.wait_ge(route, (g + 1) * ROUTE1)
                    pe.wait_ge(ua_copied, 2 * g + 1)
                    for b in range(SUB):
                        last = pe.transpose(turned[:, b * P:(b + 1) * P], c22[:, b, :], ident[:, :])
                    last.then_inc(turned_done, 1)

                def spread(g, n):
                    pe.wait_ge(turned_copied, g + 1)
                    if n == 0:
                        pe.wait_ge(ua_copied, 2 * g + 2)
                    else:
                        reach(pe, bc_copied, g * N_SEL1 + n - 1)
                    i, bank = BC[n]
                    pe.matmul(pf[:, bank, :], sel[:, i * P:(i + 1) * P], cT[:, :],
                              start=True, stop=True).then_inc(bc_done, 1)

                def main(t, c, q):
                    if c < 2:
                        reach(pe, m_done, event(t, c - 2, 1) if not (isinstance(t, int) and t == 0) else 0)
                    else:
                        pe.wait_ge(m_done, event(t, c - 2, 1))
                    o = W1_BLK + c * BLK1
                    for j in range(2):
                        for k in range(KD):
                            mm3(pe, pair[c % 2][j][:, :], w(o + (j * KD + k) * P), (yh[:, q, k, :], yl[:, q, k, :]), k == 0, False)
                    if c == 0:
                        pe.wait_ge(u_lo, 4 * (t + 1))
                    for j in range(2):
                        last = mm3(pe, pair[c % 2][j][:, :], w(o + 2 * D + j * P), (uh[:, 2 * j, :], ul[:, 2 * j, :]), False, True)
                    last.then_inc(p_done, 1)

                def delta(t, c):
                    pe.wait_ge(m_done, event(t, c, 0))
                    o = W1_BLK + c * BLK1 + 2 * D
                    for j in range(2):
                        last = mm3(pe, pair[c % 2][j][:, :], w(o + j * P), (uh[:, 2 * j + 1, :], ul[:, 2 * j + 1, :]), False, True)
                    last.then_inc(p_done, 1)

                def accumulate(t, c):
                    pe.wait_ge(c_lo, event(t, c, 1))
                    if c == 0:
                        reach(pe, t_masked, 2 * t)
                    for i in range(2):
                        last = mm3(pe, pa[:, i, :], w(W1_BLK + c * BLK1 + 2 * D + 2 * P), (ch[:, c % 2, i, :], cl[:, c % 2, i, :]),
                                   c == 0, c == C1 - 1)
                    last.then_inc(acc_done, 1)

                def down(t, last_group):
                    if not last_group:
                        pe.wait_ge(bc_copied, N_SEL1 * (t + 2))
                    for o in range(KD):
                        for c in range(C1):
                            pe.wait_ge(mix_lo, t * C1 + c + 1)
                            last = mm3(pe, pf[:, o, :], w(W1_BLK + c * BLK1 + 2 * D + 3 * P + o * P), (mh[:, c, :], ml[:, c, :]),
                                       c == 0, False)
                    last.then_inc(down_done, 1)
                    pe.wait_ge(t_lo, t + 1)
                    for o in range(KD):
                        last = mm3(pe, pf[:, o, :], w(W1_DB + o * P), (th[:, :], tl[:, :]), False, True)
                    last.then_inc(out_done, 1)

                def body(t, q, first, last):
                    more = not last
                    g, r = t + 1, 1 - q
                    main(t, 0, q)
                    main(t, 1, q)
                    delta(t, 0)
                    if more:
                        adapters(g)
                    main(t, 2, q)
                    delta(t, 1)
                    accumulate(t, 0)
                    if more:
                        project(g)
                    main(t, 3, q)
                    delta(t, 2)
                    accumulate(t, 1)
                    if more:
                        prepare_c(g, r)
                    main(t, 4, q)
                    delta(t, 3)
                    accumulate(t, 2)
                    if more:
                        prepare_ag(g, r)
                    main(t, 5, q)
                    if more:
                        turn(g)
                    delta(t, 4)
                    if more:
                        spread(g, 0)
                    accumulate(t, 3)
                    if more:
                        spread(g, 1)
                    delta(t, 5)
                    if more:
                        spread(g, 2)
                    accumulate(t, 4)
                    if more:
                        spread(g, 3)
                    accumulate(t, 5)
                    if more:
                        spread(g, 4)
                    down(t, last)

                adapters(0)
                project(0)
                prepare_c(0, 0)
                prepare_ag(0, 0)
                turn(0)
                pe.wait_ge(sel_in, 16)
                for n in range(N_SEL1):
                    spread(0, n)
                over_pairs(pe, body)

            @block.scalar
            def _(act):
                def split_x(g):
                    act.wait_ge(x_in, 16 * (g + 1))
                    reach(act, y_done, g)
                    nc.scalar.copy(xh[:, :, :], xraw[:, :, :]).then_inc(x_hi, 1)

                def split_adapters(g):
                    act.wait_ge(xa_masked, g + 1)
                    nc.scalar.copy(xah[:, :], xam[:, :]).then_inc(xa_hi, 1)

                def split_y(g, q):
                    act.wait_ge(y_done, g + 1)
                    nc.scalar.copy(yh[:, q, :, :], pf[:, :, :]).then_inc(y_hi, 1)

                def take_ua(g, j):
                    act.wait_ge(ua_done, 2 * g + j + 1)
                    reach(act, um_done, 4 * g)
                    nc.scalar.copy(ua[:, j, :], pf[:, j, :]).then_inc(ua_copied, 1)

                def route_exp(g):
                    act.wait_ge(route, g * ROUTE1 + EXP1)
                    nc.scalar.activation(vr[:, :], vr[:, :], ACT.Exp).then_inc(e_done, 1)

                def take_turned(g):
                    act.wait_ge(turned_done, g + 1)
                    nc.scalar.copy(cT[:, :], turned).then_inc(turned_copied, 1)

                def take_spread(g, n, q):
                    i, bank = BC[n]
                    act.wait_ge(bc_done, g * N_SEL1 + n + 1)
                    to = mk[:, q, i, :] if i < 3 else wv[:, q, i - 3, :]
                    nc.scalar.copy(to, pf[:, bank, :]).then_inc(bc_copied, 1)

                def split_u(g):
                    for n in range(4):
                        act.wait_ge(um_done, 4 * g + n + 1)
                        nc.scalar.copy(uh[:, n, :], um[:, n % 2, :]).then_inc(u_hi, 1)

                def silu(t, c, i):
                    act.wait_ge(p_done, event(t, c, i))
                    if not (isinstance(t, int) and t == 0 and c < 2):
                        act.wait_ge(mix_done, t * C1 + c - 1)
                        act.wait_ge(c_lo, event(t, c - 2, i))
                    nc.scalar.activation(s[:, c % 2, i, :], pair[c % 2][0][:, :], ACT.Silu).then_inc(s_done, 1)

                def split_c(t, c, i):
                    act.wait_ge(c_done, event(t, c, i))
                    reach(act, acc_done, t * C1 + c - 1)
                    nc.scalar.copy(ch[:, c % 2, i, :], s[:, c % 2, i, :]).then_inc(c_hi, 1)

                def split_mix(t, c):
                    act.wait_ge(mix_done, t * C1 + c + 1)
                    reach(act, down_done, t)
                    nc.scalar.copy(mh[:, c, :], mx[:, c % 2, :]).then_inc(mix_hi, 1)

                def split_t(t):
                    act.wait_ge(t_done, t + 1)
                    nc.scalar.copy(th[:, :], ta[:, 0, :]).then_inc(t_hi, 1)

                def body(t, q, first, last):
                    more = not last
                    g, r = t + 1, 1 - q
                    for n, (c, i) in enumerate(EVENTS):
                        silu(t, c, i)
                        if more and n == 11:
                            take_spread(g, 2, r)
                        if n >= 1 and EVENTS[n - 1][1] == 0:
                            split_c(t, *EVENTS[n - 1])
                        if i == 1:
                            split_c(t, c, i)
                            if c < C1 - 1:
                                split_mix(t, c)
                        if not more:
                            continue
                        if n == 0:
                            split_x(g)
                        if n == 2:
                            split_adapters(g)
                        if n == 4:
                            split_y(g, r)
                        if n == 6:
                            take_ua(g, 0)
                            route_exp(g)
                        if n == 8:
                            take_ua(g, 1)
                        if n == 9:
                            take_turned(g)
                        if n == 10:
                            take_spread(g, 0, r)
                            take_spread(g, 1, r)
                    if more:
                        take_spread(g, 3, r)
                        take_spread(g, 4, r)
                    split_mix(t, C1 - 1)
                    split_t(t)
                    if more:
                        split_u(g)

                split_x(0)
                split_adapters(0)
                split_y(0, 0)
                take_ua(0, 0)
                route_exp(0)
                take_ua(0, 1)
                take_turned(0)
                for n in range(N_SEL1):
                    take_spread(0, n, 0)
                split_u(0)
                over_pairs(act, body)

            @block.vector
            def _(dve):
                V = nc.vector

                def split_x(g):
                    dve.wait_ge(x_hi, g + 1)
                    V.tensor_tensor(xl[:, :, :], xraw[:, :, :], xh[:, :, :], ALU.subtract).then_inc(x_lo, 1)

                def mask_adapters(g):
                    dve.wait_ge(xa_done, g + 1)
                    reach(dve, xa_lo, g)
                    V.tensor_tensor(by_batch(xam[:, :]), by_batch(pf[:, 0, :]), over_tokens(mask, g),
                                    ALU.mult).then_inc(xa_masked, 1)
                    dve.wait_ge(xa_hi, g + 1)
                    V.tensor_tensor(xal[:, :], xam[:, :], xah[:, :], ALU.subtract).then_inc(xa_lo, 1)

                def split_y(g, q):
                    dve.wait_ge(y_hi, g + 1)
                    V.tensor_tensor(yl[:, q, :, :], pf[:, :, :], yh[:, q, :, :], ALU.subtract).then_inc(y_lo, 1)

                def route_part(g, part):
                    r = Route(g, dve_passed, route, logits, iota, tiles)
                    if part == 0:
                        reach_then(dve, logits_done, g + 1, dve_passed)
                        route1_steps(V, r, 0, EXP1)
                    else:
                        dve.wait_ge(e_done, g + 1)
                        reach(dve, turned_done, g)
                        route1_steps(V, r, EXP1, ROUTE1)

                def mask_u(g, q):
                    dve.wait_ge(bc_copied, g * N_SEL1 + 2)
                    dve.wait_ge(ua_copied, 2 * (g + 1))
                    reach(dve, t_lo, g)
                    for n in range(4):
                        reach(dve, u_lo, 4 * g + n - 1)
                        V.tensor_tensor(um[:, n % 2, :], ua[:, n // 2, :], mk[:, q, n % 2, :], ALU.mult).then_inc(um_done, 1)

                def hidden(t, c, i, q):
                    dve.wait_ge(s_done, event(t, c, i))
                    sv = s[:, c % 2, i, :]
                    V.tensor_tensor(sv, sv, pair[c % 2][1][:, :], ALU.mult).then_inc(m_done, 1)
                    dve.wait_ge(m_done, event(t, c, i))
                    V.tensor_tensor(sv, sv, wv[:, q, i, :], ALU.mult).then_inc(c_done, 1)
                    if i == 1:
                        dve.wait_ge(c_done, event(t, c, i))
                        reach(dve, mix_lo, t * C1 + c - 1)
                        V.tensor_tensor(mx[:, c % 2, :], s[:, c % 2, 0, :], s[:, c % 2, 1, :], ALU.add).then_inc(mix_done, 1)

                def tail(t, q):
                    dve.wait_ge(acc_done, (t + 1) * C1)
                    reach(dve, t_lo, t)
                    V.tensor_tensor(ta[:, 0, :], pa[:, 0, :], mk[:, q, 0, :], ALU.mult).then_inc(t_masked, 1)
                    V.tensor_tensor(ta[:, 1, :], pa[:, 1, :], mk[:, q, 2, :], ALU.mult).then_inc(t_masked, 1)
                    dve.wait_ge(t_masked, 2 * (t + 1))
                    V.tensor_tensor(ta[:, 0, :], ta[:, 0, :], ta[:, 1, :], ALU.add).then_inc(t_done, 1)

                def add(t):
                    dve.wait_ge(out_done, t + 1)
                    dve.wait_ge(res_in, 16 * (t + 1))
                    V.tensor_tensor(yo[:, :, :], yo[:, :, :], pf[:, :, :], ALU.add).then_inc(added, 1)

                def body(t, q, first, last):
                    more = not last
                    g, r = t + 1, 1 - q
                    for n, (c, i) in enumerate(EVENTS):
                        hidden(t, c, i, q)
                        if n == 0 and not first:
                            add(t - 1)
                        if not more:
                            continue
                        if n == 0:
                            split_x(g)
                        if n == 2:
                            mask_adapters(g)
                        if n == 4:
                            split_y(g, r)
                        if n == 6:
                            route_part(g, 0)
                        if n == 8:
                            route_part(g, 1)
                    tail(t, q)
                    if more:
                        mask_u(g, r)

                dve.wait_ge(idx_in, 16)
                V.tensor_scalar(mask[:, :], idx, cf[:, 0:1], cf[:, 1:2], ALU.is_equal, ALU.mult).then_inc(mask_made, 1)
                V.memset(vt[:, :, :], 0.0).then_inc(vt_zero, 1)
                split_x(0)
                dve.wait_ge(mask_made, 1)
                mask_adapters(0)
                split_y(0, 0)
                dve.wait_ge(vt_zero, 1)
                route_part(0, 0)
                route_part(0, 1)
                mask_u(0, 0)
                over_pairs(dve, body)
                add(NG - 1)

            @block.gpsimd
            def _(pool):
                def sub(out, a, b, sem):
                    nc.gpsimd.tensor_tensor(out, a, b, ALU.subtract).then_inc(sem, 1)

                def split_u(g):
                    for n in range(4):
                        pool.wait_ge(u_hi, 4 * g + n + 1)
                        sub(ul[:, n, :], um[:, n % 2, :], uh[:, n, :], u_lo)

                def split_mix(t, c):
                    pool.wait_ge(mix_hi, t * C1 + c + 1)
                    sub(ml[:, c, :], mx[:, c % 2, :], mh[:, c, :], mix_lo)

                def body(t, q, first, last):
                    for n, (c, i) in enumerate(EVENTS):
                        pool.wait_ge(c_hi, event(t, c, i))
                        sub(cl[:, c % 2, i, :], s[:, c % 2, i, :], ch[:, c % 2, i, :], c_lo)
                        if i == 1:
                            split_mix(t, c)
                    pool.wait_ge(t_hi, t + 1)
                    sub(tl[:, :], ta[:, 0, :], th[:, :], t_lo)
                    if not last:
                        split_u(t + 1)

                split_u(0)
                over_pairs(pool, body)


def program(nc, A):
    with ExitStack() as ctx:
        signals = ctx.enter_context(ExitStack())
        m = Mem(nc, ctx, signals, "w")
        big = {"wh": m.sb("wh", [P, SPLIT], F32R), "wl": m.sb("wl", [P, SPLIT], F32R),
               "cf": m.sb("cf", [P, 2 + SUB * E]), "ident": m.sb("ident", [P, P], BF16),
               "cst_in": m.sem("cst_in")}
        with nc.Block() as block:
            @block.sync
            def _(sp):
                sp.dma_start(big["cf"][:, :], A["cf"]).then_inc(big["cst_in"], 16)
                sp.dma_start(big["ident"][:, :], A["ident"]).then_inc(big["cst_in"], 16)
                sp.wait_ge(big["cst_in"], 32)
        with ExitStack() as experts:
            e = Mem(nc, experts, signals, "m")
            big["xwh"] = e.sb("xwh", [P, W0_COLS - SPLIT], F32R)
            big["xwl"] = e.sb("xwl", [P, W0_COLS - SPLIT], F32R)
            with nc.sbuf_tensor("w_raw", [P, W0_COLS], F32) as raw:
                big["raw"] = raw
            big["mh"] = e.sb("mh", [P, WM_PAD], F32R)
            big["ml"] = e.sb("ml", [P, WM_PAD], F32R)
            phase_1(nc, A, big, signals)
            phase_2(nc, A, big, signals)
        phase_3(nc, A, big, signals)


def _rows(a):
    k = a.shape[0] // P
    return np.ascontiguousarray(a.reshape(k, P, a.shape[1]).transpose(1, 0, 2)).reshape(P, -1)


def _cols(parts, width):
    out = np.concatenate(parts, axis=1)
    return np.ascontiguousarray(np.concatenate([out, np.zeros((P, width - out.shape[1]), np.float32)], axis=1))


def _a_cols(a):
    return a.transpose(1, 0, 2).reshape(a.shape[1], E * R)


def _b_rows(a):
    return a.reshape(E * R, a.shape[2])


def _pack_0(v):
    parts = [_rows(_a_cols(v["L0_cond_Ag"])), _rows(_a_cols(v["L0_cond_Au"]))]
    ad = _a_cols(v["L0_cond_Ad"])
    for c in range(C0):
        b = slice(c * P, (c + 1) * P)
        parts += [_rows(v["L0_cond_Wg"][:, b]), _rows(v["L0_cond_Wu"][:, b]), _b_rows(v["L0_cond_Bg"])[:, b],
                  _b_rows(v["L0_cond_Bu"])[:, b], v["L0_cond_Wd"][b], ad[b]]
    parts += [_b_rows(v["L0_cond_Bd"]), _rows(v["L0_ffn_Wr"])]
    return _cols(parts, W0_COLS)


def _pack_m(v):
    g, u = (v[n].transpose(1, 0, 2).reshape(D, E * IM) for n in ("L0_ffn_Wg", "L0_ffn_Wu"))
    d = v["L0_ffn_Wd"].reshape(E * IM, D)
    parts = []
    for c in range(CM):
        b = slice(c * P, (c + 1) * P)
        parts += [_rows(g[:, b]), _rows(u[:, b]), d[b]]
    return _cols(parts, WM_PAD)


def _pack_1(v):
    def wide(a):
        return np.concatenate([a, np.zeros((a.shape[0], C1 * P - H1), np.float32)], axis=1)

    up, gate = wide(v["L1_ffn_w_up"].T), wide(v["L1_ffn_w_gate"].T)
    ub, gb = (wide(_b_rows(v[n].transpose(0, 2, 1))) for n in ("L1_ffn_up_B", "L1_ffn_gate_B"))
    da = wide(v["L1_ffn_down_A"].reshape(E * R, H1)).T
    wd = wide(v["L1_ffn_w_down"]).T
    parts = [_rows(v["L1_cond_A"].reshape(E * R, D).T), _rows(v["L1_cond_W"].T),
             _b_rows(v["L1_cond_Bm"].transpose(0, 2, 1)), _rows(v["L1_ffn_gate_w"].T),
             _rows(v["L1_ffn_up_A"].reshape(E * R, D).T), _rows(v["L1_ffn_gate_A"].reshape(E * R, D).T)]
    for c in range(C1):
        b = slice(c * P, (c + 1) * P)
        parts += [_rows(up[:, b]), _rows(gate[:, b]), ub[:, b], gb[:, b], da[b], wd[b]]
    parts += [_b_rows(v["L1_ffn_down_B"].transpose(0, 2, 1))]
    return _cols(parts, W1_PAD)


def _constants(scalings):
    row = np.arange(P)
    cf = np.concatenate([(row // R).astype(np.float32)[:, None], np.repeat(scalings, R)[:, None],
                         np.tile(np.arange(E, dtype=np.float32), (P, SUB))], axis=1).astype(np.float32)
    hidden = np.arange(CM * P)
    sel_m = np.zeros((NC0, CM * P), np.float32)
    for part in range(3):
        sel_m[part * E + hidden // IM, hidden] = 1.0
    sel_1 = np.zeros((NC1, N_SEL1, P), np.float32)
    for e in range(E):
        rows = row[row // R == e]
        sel_1[e, 0, rows] = ALPHA
        sel_1[E + e, 1, rows] = ALPHA
        sel_1[e, 1, rows] = -ALPHA
        sel_1[E + e, 2, rows] = ALPHA
    for part in range(3):
        for slot in range(2):
            sel_1[2 * E + 2 * part + slot, 3 + slot] = 1.0
    bf16 = mybir.dt.np(BF16)
    return {"cf": cf, "ident": np.eye(P).astype(bf16), "sel_m": sel_m.astype(bf16),
            "sel_1": sel_1.reshape(NC1, -1).astype(bf16)}


def kernel(**inputs):
    import concourse.bacc as bacc
    from concourse.bass_utils import run_bass_kernel_spmd

    v = {n: np.asarray(a) for n, a in inputs.items()}
    arrays = {
        "xT": np.ascontiguousarray(v["x"].reshape(T, D).T),
        "idx0": np.ascontiguousarray(v["itok_B_0_7"]),
        "idx1": np.ascontiguousarray(v["itok_B_0_6"]),
        "w0": _pack_0(v), "wm": _pack_m(v), "w1": _pack_1(v),
        **_constants(v["L1_cond_scalings"]),
    }
    nc = bacc.Bacc("TRN2", target_bir_lowering=False, num_devices=1)
    A = {n: nc.dram_tensor(n, a.shape, mybir.dt.from_np(a.dtype), kind="ExternalInput").ap() for n, a in arrays.items()}
    A["out"] = nc.dram_tensor("out", (D, T), F32, kind="ExternalOutput").ap()
    A["h"] = nc.dram_tensor("h", (D, T), F32).ap()
    A["comb"] = nc.dram_tensor("comb", (NC0, T), BF16).ap()
    A["x1"] = nc.dram_tensor("x1", (D, T), F32).ap()
    program(nc, A)
    r = run_bass_kernel_spmd(nc, [arrays], core_ids=[0])
    return np.ascontiguousarray(r.results[0]["out"].T).reshape(B, S, D)
```

```python
from contextlib import ExitStack

import numpy as np

import concourse.bass as bass
from concourse import mybir

P = 128
B, S, D = 128, 32, 256
T = B * S
G = 512
NG = T // G
GB = G // S
SUB = G // P
KD = D // P
E = 8
R = 16
I0 = 1024
C0 = I0 // P
IM = 176
CM = E * IM // P
H1 = 704
C1 = -(-H1 // P)
HALF = P // 2
assert H1 == (C1 - 1) * P + HALF
ALPHA = 2.0

F32 = mybir.dt.float32
F32R = mybir.dt.float32r
BF16 = mybir.dt.bfloat16
I32 = mybir.dt.int32
U32 = mybir.dt.uint32
ALU = mybir.AluOpType
ACT = mybir.ActivationFunctionType
X = mybir.AxisListType.X

BLK0 = 2 * D + 2 * P + D + P
W0_A = 0
W0_BLK = 2 * D
W0_BD = W0_BLK + C0 * BLK0
W0_WR = W0_BD + D
W0_COLS = W0_WR + KD * E
BLKM = 3 * D
WM_COLS = CM * BLKM
W1_A = 0
W1_W = D
W1_B = W1_W + KD * D
W1_GW = W1_B + D
W1_UA = W1_GW + KD * E
W1_GA = W1_UA + D
W1_BLK = W1_GA + D
BLK1 = 2 * D + 2 * P + P + D
W1_DB = W1_BLK + C1 * BLK1
W1_COLS = W1_DB + D

PIECES = 4
PM = -(-WM_COLS // (PIECES * (NG - 1)))
P1W = -(-W1_COLS // (PIECES * NG))
WM_PAD = PM * PIECES * (NG - 1)
W1_PAD = P1W * PIECES * NG
STAGE = max(PM, P1W)
SPLIT = W0_BLK + -(-(W1_PAD - W0_BLK) // P) * P
RING = 3

N_SEL1 = 5
NC0 = 3 * E
NC1 = 2 * E + 6


def reach(eng, sem, value):
    if isinstance(value, int) and value <= 0:
        return
    eng.wait_ge(sem, value)


def reach_then(eng, sem, value, passed):
    reach(eng, sem, value)
    if not isinstance(value, int):
        eng.sem_inc(passed, 1)


def mm3(pe, out, w, x, start, stop):
    (wh, wl), (xh, xl) = w, x
    pe.matmul(out, wh, xl, start=start, stop=False, skip_group_check=True)
    pe.matmul(out, wl, xh, start=False, stop=False, skip_group_check=True)
    return pe.matmul(out, wh, xh, start=False, stop=stop, skip_group_check=True)


def over_tokens(mask, t):
    return mask[:, bass.ds(t * GB, GB)].unsqueeze(2).broadcast_to([P, GB, S])


def by_batch(ap):
    return ap.rearrange("p (b s) -> p b s", s=S)


class Mem:

    def __init__(self, nc, memory, signals, prefix):
        self.nc, self.memory, self.signals, self.prefix = nc, memory, signals, prefix

    def sb(self, name, shape, dt=F32):
        return self.memory.enter_context(self.nc.sbuf_tensor(f"{self.prefix}_{name}", shape, dt))

    def pb(self, name, shape):
        return self.memory.enter_context(self.nc.psum_tensor(f"{self.prefix}_{name}", shape, F32))

    def sem(self, name):
        return self.signals.enter_context(self.nc.semaphore(f"{self.prefix}_{name}"))


def last_user(c, n, ring):
    return c - ring if c >= ring else max(b for b in range(n) if b % ring == c) - n


def over_groups(eng, body):
    body(0, True, False)
    with eng.Fori(1, NG - 1) as t:
        body(t, False, False)
    body(NG - 1, False, True)


def over_pairs(eng, body):
    body(0, 0, True, False)
    with eng.Fori(0, NG // 2 - 1) as i:
        body(i * 2 + 1, 1, False, False)
        body(i * 2 + 2, 0, False, False)
    body(NG - 1, 1, False, True)


def route0_steps(dve, k, lo, hi):
    base = k.group * ROUTE0
    z, ex, pr, v8, i8, if8, w2, st, o0, o1, c24 = k.t

    def each(a):
        return a.unsqueeze(2).broadcast_to([P, SUB, E])

    steps = [
        lambda: dve.reduce_max(st[:, :, 0], k.logits, X),
        lambda: dve.tensor_tensor(z[:, :, :], k.logits, each(st[:, :, 0]), ALU.subtract),
        lambda: dve.reduce_sum(st[:, :, 1], ex[:, :, :], X),
        lambda: dve.reciprocal(st[:, :, 2], st[:, :, 1]),
        lambda: dve.tensor_tensor(pr[:, :, :], ex[:, :, :], each(st[:, :, 2]), ALU.mult),
    ] + [
        (lambda s=s: dve.max(v8[:, s, :], pr[:, s, :])) for s in range(SUB)
    ] + [
        (lambda s=s: dve.max_index(i8[:, s, :], v8[:, s, :], pr[:, s, :])) for s in range(SUB)
    ] + [
        lambda: dve.tensor_tensor(st[:, :, 3], v8[:, :, 0], v8[:, :, 1], ALU.add),
        lambda: dve.reciprocal(st[:, :, 0], st[:, :, 3]),
        lambda: dve.tensor_tensor(w2[:, :, :], v8[:, :, 0:2], st[:, :, 0].unsqueeze(2).broadcast_to([P, SUB, 2]), ALU.mult),
        lambda: dve.tensor_copy(if8[:, :, :], i8[:, :, 0:2]),
        lambda: dve.tensor_tensor(o0[:, :, :], k.iota, each(if8[:, :, 0]), ALU.is_equal),
        lambda: dve.tensor_tensor(o1[:, :, :], k.iota, each(if8[:, :, 1]), ALU.is_equal),
        lambda: dve.tensor_tensor(o0[:, :, :], o0[:, :, :], each(w2[:, :, 0]), ALU.mult),
        lambda: dve.tensor_tensor(o1[:, :, :], o1[:, :, :], each(w2[:, :, 1]), ALU.mult),
        lambda: dve.tensor_tensor(o0[:, :, :], o0[:, :, :], o1[:, :, :], ALU.add),
        lambda: dve.tensor_copy(c24[:, :, 0:E], o0[:, :, :]),
        lambda: dve.tensor_tensor(o0[:, :, :], o0[:, :, :], c24[:, :, 0:E], ALU.subtract),
        lambda: dve.tensor_copy(c24[:, :, E:2 * E], o0[:, :, :]),
        lambda: dve.tensor_tensor(c24[:, :, 2 * E:3 * E], o0[:, :, :], c24[:, :, E:2 * E], ALU.subtract),
    ]
    assert len(steps) == ROUTE0
    for n in range(lo, hi):
        steps[n]().then_inc(k.route, 1)
        reach_then(dve, k.route, base + n + 1, k.passed)


def route1_steps(dve, k, lo, hi):
    base = k.group * ROUTE1
    vt, vr, er, wt, v8, i8, if8, st, c22, rest, lg = k.t

    def each(a, n):
        return a.unsqueeze(2).broadcast_to([P, SUB, n])

    steps = [
        lambda: dve.tensor_copy(lg[:, :, :], k.logits[:, :, 0:E]),
        lambda: dve.tensor_tensor(lg[:, :, :], lg[:, :, :], k.logits[:, :, E:2 * E], ALU.add),
    ] + [
        (lambda s=s: dve.max(v8[:, s, :], lg[:, s, :])) for s in range(SUB)
    ] + [
        (lambda s=s: dve.max_index(i8[:, s, :], v8[:, s, :], lg[:, s, :])) for s in range(SUB)
    ] + [
        lambda: dve.tensor_copy(vt[:, :, 0:2], v8[:, :, 0:2]),
        lambda: dve.transpose(vr[:, :], vt[:, :, :].rearrange("p s f -> p (s f)")),
        lambda: dve.reduce_max(st[:, :, 0], by_sub(vr), X),
        lambda: dve.tensor_tensor(by_sub(vr), by_sub(vr), each(st[:, :, 0], S), ALU.subtract),
        lambda: dve.tensor_copy(if8[:, :, :], i8[:, :, 0:2]),
        lambda: dve.tensor_tensor(c22[:, :, 0:E], k.iota, each(if8[:, :, 0], E), ALU.is_equal),
        lambda: dve.tensor_tensor(c22[:, :, E:2 * E], k.iota, each(if8[:, :, 1], E), ALU.is_equal),
        lambda: dve.reduce_sum(st[:, :, 1], by_sub(er), X),
        lambda: dve.reciprocal(st[:, :, 2], st[:, :, 1]),
        lambda: dve.tensor_tensor(by_sub(er), by_sub(er), each(st[:, :, 2], S), ALU.mult),
        lambda: dve.transpose(wt[:, :, :].rearrange("p s f -> p (s f)"), er[:, :]),
        lambda: dve.tensor_copy(c22[:, :, 2 * E:2 * E + 2], wt[:, :, 0:2]),
        lambda: dve.tensor_tensor(rest[:, :, :], wt[:, :, 0:2], c22[:, :, 2 * E:2 * E + 2], ALU.subtract),
        lambda: dve.tensor_copy(c22[:, :, 2 * E + 2:2 * E + 4], rest[:, :, :]),
        lambda: dve.tensor_tensor(c22[:, :, 2 * E + 4:2 * E + 6], rest[:, :, :], c22[:, :, 2 * E + 2:2 * E + 4], ALU.subtract),
    ]
    assert len(steps) == ROUTE1
    for n in range(lo, hi):
        steps[n]().then_inc(k.route, 1)
        reach_then(dve, k.route, base + n + 1, k.passed)


def by_sub(rows):
    return rows[:, :].rearrange("p (s t) -> p s t", t=S)


ROUTE0 = 26
EXP0 = 2
ROUTE1 = 25
EXP1 = 14
MASKS1 = 17
CUT1 = 21


class Route:

    def __init__(self, group, passed, route, logits, iota, t):
        self.passed, self.group, self.route, self.logits, self.iota, self.t = passed, group, route, logits, iota, t


def phase_1(nc, A, big, signals):
    wh, wl, mh, ml, raw, cf, ident = (big[n] for n in ("wh", "wl", "mh", "ml", "raw", "cf", "ident"))
    iota = cf[:, 2:2 + SUB * E].rearrange("p (s e) -> p s e", e=E)

    def parts(a, b):
        if a >= SPLIT:
            return big["xwh"][:, a - SPLIT:b - SPLIT], big["xwl"][:, a - SPLIT:b - SPLIT]
        assert b <= SPLIT
        return wh[:, a:b], wl[:, a:b]

    with ExitStack() as memory:
        m = Mem(nc, memory, signals, "p1")
        sp_passed, dve_passed, pool_passed = m.sem("sp_passed"), m.sem("dve_passed"), m.sem("pool_passed")
        xraw, xh, xl = big["xraw"], big["xh"], big["xl"]
        xam = m.sb("xam", [P, 2, G])
        xah, xal = m.sb("xah", [P, 2, G], F32R), m.sb("xal", [P, 2, G], F32R)
        s = m.sb("s", [P, 2, G])
        hh, hl = m.sb("hh", [P, RING, G], F32R), m.sb("hl", [P, RING, G], F32R)
        dm = xam[:, 0, :]
        dh, dl = m.sb("dh", [P, G], F32R), m.sb("dl", [P, G], F32R)
        of = m.sb("of", [P, KD, G])
        oh, ol = m.sb("oh", [P, KD, G], F32R), m.sb("ol", [P, KD, G], F32R)
        stage = m.sb("stage", [P, 2, PM])
        mask = m.sb("mask", [P, B])
        idx = of[:, 0, 0:B].bitcast(I32)
        tiles = [m.sb(n, [P, SUB, w], dt) for n, w, dt in (
            ("z", E, F32), ("ex", E, F32), ("pr", E, F32), ("v8", 8, F32), ("i8", 8, U32), ("if8", 2, F32),
            ("w2", 2, F32), ("st", 4, F32), ("o0", E, F32), ("o1", E, F32), ("c24", NC0, BF16))]
        z, ex, c24 = tiles[0], tiles[1], tiles[-1]
        cT = m.sb("cT", [NC0, G], BF16)

        pair = [[m.pb(f"pair{i}{j}", [P, G]) for j in range(2)] for i in range(2)]
        po = m.pb("po", [P, KD, G])
        pd = m.pb("pd", [P, G])
        pm = m.pb("pm", [P, G])
        logits = pm[:, 0:SUB * E].rearrange("p (s e) -> p s e", e=E)
        turned = pm[:, :].bitcast(BF16)[0:NC0, 0:G]

        raw_in = [m.sem(f"raw_in{n}") for n in range(C0 + 3)]
        (w_hi, w_lo, x_in, x_hi, x_lo, idx_in, mask_made, xa_done, xa_masked, xa_hi, xa_lo, gu_done, s_done,
         h_done, h_hi, h_lo, down_done, d_masked, d_hi, d_lo, out_done, out_hi, out_f, out_lo, stored,
         logits_done, route, e_done, turned_done, cT_done, cT_stored, piece_hi, piece_lo, next_in, next_hi,
         next_lo) = (
            m.sem(n) for n in (
                "w_hi w_lo x_in x_hi x_lo idx_in mask_made xa_done xa_masked xa_hi xa_lo gu_done s_done "
                "h_done h_hi h_lo down_done d_masked d_hi d_lo out_done out_hi out_f out_lo stored "
                "logits_done route e_done turned_done cT_done cT_stored piece_hi piece_lo next_in next_hi "
                "next_lo").split())
        piece_in = [m.sem(f"piece_in{n}") for n in range(2)]

        x_v = A["xT"].rearrange("(k p) t -> p k t", p=P)
        h_v = A["h"].rearrange("(k p) t -> p k t", p=P)
        ends = [0, W0_BLK] + [W0_BLK + (c + 1) * BLK0 for c in range(C0)] + [W0_COLS]
        cuts = list(zip(sorted({*ends[:-1], SPLIT}), sorted({*ends[1:], SPLIT})))
        split_for = [sum(b <= ends[c + 2] for _, b in cuts) for c in range(C0)]

        def w(o, n=P):
            return parts(o, o + n)

        def x(k):
            return xh[:, k, :], xl[:, k, :]

        def free_slot(c):
            return last_user(c, C0, RING)

        with nc.Block() as block:
            @block.sync
            def _(sp):
                sp.dma_start(xraw[:, :, :], x_v[:, :, 0:G]).then_inc(x_in, 16)
                sp.dma_start(raw[:, cuts[0][0]:cuts[0][1]], A["w0"][:, cuts[0][0]:cuts[0][1]]).then_inc(raw_in[0], 16)
                sp.dma_start(idx, A["idx0"].partition_broadcast(P)).then_inc(idx_in, 16)
                for n, (a, b) in enumerate(cuts[1:]):
                    sp.dma_start(raw[:, a:b], A["w0"][:, a:b]).then_inc(raw_in[n + 1], 16)

                def store(t):
                    reach_then(sp, out_f, t + 1, sp_passed)
                    sp.dma_start(h_v[:, :, bass.ds(t * G, G)], of[:, :, :]).then_inc(stored, 16)

                def store_routing(t):
                    reach_then(sp, cT_done, t + 1, sp_passed)
                    sp.dma_start(A["comb"][:, bass.ds(t * G, G)], cT[:, :]).then_inc(cT_stored, 16)

                def body(t, first, last):
                    if not last:
                        reach_then(sp, x_lo, t + 1, sp_passed)
                        sp.dma_start(xraw[:, :, :], x_v[:, :, bass.ds((t + 1) * G, G)]).then_inc(x_in, 16)
                    if first:
                        return
                    for j in range(PIECES):
                        n = (t - 1) * PIECES + j
                        reach_then(sp, piece_lo, n + 1, sp_passed)
                        sp.dma_start(stage[:, j % 2, :], A["wm"][:, bass.ds(n * PM, PM)]).then_inc(piece_in[j % 2], 16)
                        if j == 1:
                            store(t - 1)
                    store_routing(t - 1)

                over_groups(sp, body)
                sp.wait_ge(x_lo, NG)
                sp.wait_ge(stored, 16 * (NG - 1))
                sp.dma_start(xraw[:, :, :], h_v[:, :, 0:G]).then_inc(next_in, 16)
                store(NG - 1)
                store_routing(NG - 1)
                sp.wait_ge(stored, 16 * NG)
                sp.wait_ge(cT_stored, 16 * NG)

            @block.tensor
            def _(pe):
                def adapters(t):
                    pe.wait_ge(x_lo, t + 1)
                    reach(pe, cT_done, t - 1)
                    for j in range(2):
                        if j == 1:
                            reach(pe, h_done, t * C0)
                        out = (pm, pair[1][0])[j]
                        for k in range(KD):
                            last = mm3(pe, out[:, :], w(W0_A + (j * KD + k) * P), x(k), k == 0, k == KD - 1)
                        last.then_inc(xa_done, 1)

                def gate_up(t, c, first):
                    if first:
                        pe.wait_ge(w_lo, split_for[c])
                    reach(pe, h_done, t * C0 + c - 1)
                    o = W0_BLK + c * BLK0
                    for j in range(2):
                        for k in range(KD):
                            mm3(pe, pair[c % 2][j][:, :], w(o + (j * KD + k) * P), x(k), k == 0, False)
                    for j in range(2):
                        if c == 0:
                            pe.wait_ge(xa_lo, 2 * t + j + 1)
                        last = mm3(pe, pair[c % 2][j][:, :], w(o + 2 * D + j * P), (xah[:, j, :], xal[:, j, :]), False, True)
                    last.then_inc(gu_done, 1)

                def down(t, c):
                    pe.wait_ge(h_lo, t * C0 + c + 1)
                    if c == 0:
                        reach(pe, d_masked, t)
                        reach(pe, out_hi, t)
                        reach(pe, out_f, t)
                        reach(pe, out_lo, t)
                    o = W0_BLK + c * BLK0 + 2 * D + 2 * P
                    h = hh[:, c % RING, :], hl[:, c % RING, :]
                    mm3(pe, pd[:, :], w(o + D), h, c == 0, c == C0 - 1)
                    for k in range(KD):
                        last = mm3(pe, po[:, k, :], w(o + k * P), h, c == 0, False)
                    last.then_inc(down_done, 1)

                def adapted(t):
                    pe.wait_ge(d_lo, t + 1)
                    for k in range(KD):
                        last = mm3(pe, po[:, k, :], w(W0_BD + k * P), (dh[:, :], dl[:, :]), False, True)
                    last.then_inc(out_done, 1)

                def route_logits(t):
                    pe.wait_ge(out_lo, t + 1)
                    for b in range(SUB):
                        tok = slice(b * P, (b + 1) * P)
                        for k in range(KD):
                            last = mm3(pe, logits[:, b, :], (oh[:, k, tok], ol[:, k, tok]), w(W0_WR + k * E, E),
                                       k == 0, k == KD - 1)
                    last.then_inc(logits_done, 1)

                def route_turn(t):
                    pe.wait_ge(route, (t + 1) * ROUTE0)
                    for b in range(SUB):
                        last = pe.transpose(turned[:, b * P:(b + 1) * P], c24[:, b, :], ident[:, :])
                    last.then_inc(turned_done, 1)

                def body(t, first, last):
                    for c in range(C0):
                        gate_up(t, c, first)
                        if c == 0 and not first:
                            adapted(t - 1)
                        if c >= 2:
                            down(t, c - 2)
                        if c == 2 and not first:
                            route_logits(t - 1)
                    if not first:
                        route_turn(t - 1)
                    down(t, C0 - 2)
                    if not last:
                        adapters(t + 1)
                    down(t, C0 - 1)

                pe.wait_ge(w_lo, 1)
                adapters(0)
                over_groups(pe, body)
                adapted(NG - 1)
                route_logits(NG - 1)
                route_turn(NG - 1)

            @block.scalar
            def _(act):
                def split_weights(n):
                    a, b = cuts[n]
                    act.wait_ge(raw_in[n], 16)
                    nc.scalar.copy(parts(a, b)[0], raw[:, a:b]).then_inc(w_hi, 1)

                def split_x(t):
                    act.wait_ge(x_in, 16 * (t + 1))
                    reach(act, gu_done, t * C0)
                    nc.scalar.copy(xh[:, :, :], xraw[:, :, :]).then_inc(x_hi, 1)

                def split_adapters(t):
                    for j in range(2):
                        act.wait_ge(xa_masked, 2 * t + j + 1)
                        nc.scalar.copy(xah[:, j, :], xam[:, j, :]).then_inc(xa_hi, 1)

                def silu(t, c):
                    act.wait_ge(gu_done, t * C0 + c + 1)
                    reach(act, h_lo, t * C0 + c - 1)
                    nc.scalar.activation(s[:, c % 2, :], pair[c % 2][0][:, :], ACT.Silu).then_inc(s_done, 1)

                def split_hidden(t, c):
                    act.wait_ge(h_done, t * C0 + c + 1)
                    reach(act, down_done, t * C0 + free_slot(c) + 1)
                    nc.scalar.copy(hh[:, c % RING, :], s[:, c % 2, :]).then_inc(h_hi, 1)

                def split_down(t):
                    act.wait_ge(d_masked, t + 1)
                    reach(act, out_done, t)
                    nc.scalar.copy(dh[:, :], dm).then_inc(d_hi, 1)

                def take_output(t):
                    act.wait_ge(out_done, t + 1)
                    reach(act, logits_done, t)
                    nc.scalar.copy(oh[:, :, :], po[:, :, :]).then_inc(out_hi, 1)
                    reach(act, stored, 16 * t)
                    nc.scalar.copy(of[:, :, :], po[:, :, :]).then_inc(out_f, 1)

                def route_exp(t):
                    act.wait_ge(route, t * ROUTE0 + EXP0)
                    nc.scalar.activation(ex[:, :, :], z[:, :, :], ACT.Exp).then_inc(e_done, 1)

                def take_routing(t):
                    act.wait_ge(turned_done, t + 1)
                    reach(act, cT_stored, 16 * t)
                    nc.scalar.copy(cT[:, :], turned).then_inc(cT_done, 1)

                def body(t, first, last):
                    if not first:
                        split_down(t - 1)
                    for c in range(C0):
                        if first:
                            for n in range(split_for[c], split_for[c + 1] if c + 1 < C0 else len(cuts)):
                                split_weights(n)
                        silu(t, c)
                        if c == 0 and not first:
                            take_output(t - 1)
                        if c >= 1:
                            split_hidden(t, c - 1)
                        if c == 3 and not first:
                            route_exp(t - 1)
                    if not first:
                        take_routing(t - 1)
                    if not last:
                        split_x(t + 1)
                    split_hidden(t, C0 - 1)
                    if not last:
                        split_adapters(t + 1)

                split_weights(0)
                split_x(0)
                split_weights(1)
                split_adapters(0)
                over_groups(act, body)
                split_down(NG - 1)
                take_output(NG - 1)
                act.wait_ge(next_in, 16)
                act.wait_ge(gu_done, NG * C0)
                nc.scalar.copy(xh[:, :, :], xraw[:, :, :]).then_inc(next_hi, 1)
                route_exp(NG - 1)
                take_routing(NG - 1)

            @block.vector
            def _(dve):
                def split_weights(n):
                    a, b = cuts[n]
                    dve.wait_ge(w_hi, n + 1)
                    nc.vector.tensor_tensor(parts(a, b)[1], raw[:, a:b], parts(a, b)[0], ALU.subtract).then_inc(w_lo, 1)

                def split_x(t):
                    dve.wait_ge(x_hi, t + 1)
                    nc.vector.tensor_tensor(xl[:, :, :], xraw[:, :, :], xh[:, :, :], ALU.subtract).then_inc(x_lo, 1)

                def mask_adapters(t):
                    for j in range(2):
                        dve.wait_ge(xa_done, 2 * t + j + 1)
                        if j == 0:
                            reach(dve, d_lo, t - 1)
                        else:
                            reach(dve, xa_lo, 2 * t)
                        nc.vector.tensor_tensor(by_batch(xam[:, j, :]), by_batch((pm, pair[1][0])[j][:, :]),
                                                over_tokens(mask, t), ALU.mult).then_inc(xa_masked, 1)
                    for j in range(2):
                        dve.wait_ge(xa_hi, 2 * t + j + 1)
                        nc.vector.tensor_tensor(xal[:, j, :], xam[:, j, :], xah[:, j, :], ALU.subtract).then_inc(xa_lo, 1)

                def hidden(t, c):
                    dve.wait_ge(s_done, t * C0 + c + 1)
                    nc.vector.tensor_tensor(s[:, c % 2, :], s[:, c % 2, :], pair[c % 2][1][:, :], ALU.mult).then_inc(h_done, 1)

                def mask_down(t):
                    dve.wait_ge(down_done, (t + 1) * C0)
                    dve.wait_ge(xa_lo, 2 * NG if isinstance(t, int) and t == NG - 1 else 2 * (t + 2))
                    nc.vector.tensor_tensor(by_batch(dm), by_batch(pd[:, :]), over_tokens(mask, t),
                                            ALU.mult).then_inc(d_masked, 1)
                    dve.wait_ge(d_hi, t + 1)
                    nc.vector.tensor_tensor(dl[:, :], dm, dh[:, :], ALU.subtract).then_inc(d_lo, 1)

                def split_output(t):
                    dve.wait_ge(out_f, t + 1)
                    nc.vector.tensor_tensor(ol[:, :, :], po[:, :, :], oh[:, :, :], ALU.subtract).then_inc(out_lo, 1)

                def route_part(t, part):
                    r = Route(t, dve_passed, route, logits, iota, tiles)
                    if part == 0:
                        dve.wait_ge(logits_done, t + 1)
                        route0_steps(nc.vector, r, 0, EXP0)
                    elif part == 1:
                        dve.wait_ge(e_done, t + 1)
                        route0_steps(nc.vector, r, EXP0, 13)
                    elif part == 2:
                        route0_steps(nc.vector, r, 13, 22)
                    else:
                        reach(dve, turned_done, t)
                        route0_steps(nc.vector, r, 22, ROUTE0)

                def body(t, first, last):
                    if not first:
                        mask_down(t - 1)
                    for c in range(C0):
                        if first:
                            for n in range(split_for[c], split_for[c + 1] if c + 1 < C0 else len(cuts)):
                                split_weights(n)
                        hidden(t, c)
                        if first:
                            continue
                        if c == 0:
                            split_output(t - 1)
                        if c >= 3 and c < 7:
                            route_part(t - 1, c - 3)
                    if not last:
                        split_x(t + 1)
                        mask_adapters(t + 1)

                dve.wait_ge(idx_in, 16)
                dve.wait_ge(big["cst_in"], 32)
                nc.vector.tensor_scalar(mask[:, :], idx, cf[:, 0:1], None, ALU.is_equal).then_inc(mask_made, 1)
                split_weights(0)
                split_x(0)
                split_weights(1)
                dve.wait_ge(mask_made, 1)
                mask_adapters(0)
                over_groups(dve, body)
                mask_down(NG - 1)
                split_output(NG - 1)
                for part in range(4):
                    route_part(NG - 1, part)
                dve.wait_ge(next_hi, 1)
                nc.vector.tensor_tensor(xl[:, :, :], xraw[:, :, :], xh[:, :, :], ALU.subtract).then_inc(next_lo, 1)

            @block.gpsimd
            def _(pool):
                def body(t, first, last):
                    for c in range(C0):
                        pool.wait_ge(h_hi, t * C0 + c + 1)
                        nc.gpsimd.tensor_tensor(hl[:, c % RING, :], s[:, c % 2, :], hh[:, c % RING, :],
                                                ALU.subtract).then_inc(h_lo, 1)
                        if not first and c % 2 == 1:
                            split_piece(t, c // 2)

                def split_piece(t, j):
                    n = (t - 1) * PIECES + j
                    pool.wait_ge(piece_in[j % 2], 16 * ((t - 1) * (PIECES // 2) + j // 2 + 1))
                    pool.wait_ge(w_lo, len(cuts))
                    nc.gpsimd.tensor_copy(mh[:, bass.ds(n * PM, PM)], stage[:, j % 2, :]).then_inc(piece_hi, 1)
                    pool.wait_ge(piece_hi, n + 1)
                    nc.gpsimd.tensor_tensor(ml[:, bass.ds(n * PM, PM)], stage[:, j % 2, :], mh[:, bass.ds(n * PM, PM)],
                                            ALU.subtract).then_inc(piece_lo, 1)

                pool.sem_inc(piece_lo, 2)
                over_groups(pool, body)


AHEAD = 6
AHEAD_LAST = 9


def phase_2(nc, A, big, signals):
    wh, wl, mh, ml = (big[n] for n in ("wh", "wl", "mh", "ml"))
    with ExitStack() as memory:
        m = Mem(nc, memory, signals, "p2")
        sp_passed, dve_passed, pool_passed = m.sem("sp_passed"), m.sem("dve_passed"), m.sem("pool_passed")
        xraw = big["xraw"]
        xh = big["xh"], m.sb("xh", [P, KD, G], F32R)
        xl = big["xl"], m.sb("xl", [P, KD, G], F32R)
        s = m.sb("s", [P, 2, G])
        hh, hl = m.sb("hh", [P, RING, G], F32R), m.sb("hl", [P, RING, G], F32R)
        of = m.sb("of", [P, KD, G])
        stage = m.sb("stage", [P, 2, P1W])
        sel = m.sb("sel", [NC0, CM * P], BF16)
        cin = m.sb("cin", [NC0, G], BF16)
        cT = m.sb("cT", [NC0, 2, G], BF16)

        pair = [[m.pb(f"pair{i}{j}", [P, G]) for j in range(2)] for i in range(2)]
        po = m.pb("po", [P, KD, G])
        pc = [m.pb(f"pc{i}", [P, G]) for i in range(2)]

        (x_in, x_hi, x_lo, c_in, c_copied, gu_done, cb_done, s_done, hu_done, h_done, h_hi, h_lo, down_done,
         out_done, res_in, added, stored, piece_hi, piece_lo, sel_in, next_in, next_hi, next_lo) = (m.sem(n) for n in (
             "x_in x_hi x_lo c_in c_copied gu_done cb_done s_done hu_done h_done h_hi h_lo down_done "
             "out_done res_in added stored piece_hi piece_lo sel_in next_in next_hi next_lo").split())
        piece_in = [m.sem(f"piece_in{n}") for n in range(2)]

        x_v = A["xT"].rearrange("(k p) t -> p k t", p=P)
        h_v = A["h"].rearrange("(k p) t -> p k t", p=P)
        x1_v = A["x1"].rearrange("(k p) t -> p k t", p=P)

        def w(o, n=P):
            return mh[:, o:o + n], ml[:, o:o + n]

        def x(k, q):
            return xh[q][:, k, :], xl[q][:, k, :]

        def pair_free(t, c):
            return t * CM + last_user(c, CM, 2) + 1

        with nc.Block() as block:
            @block.sync
            def _(sp):
                def load(t):
                    reach_then(sp, x_lo, t - 1, sp_passed)
                    sp.dma_start(xraw[:, :, :], h_v[:, :, bass.ds(t * G, G)]).then_inc(x_in, 16)
                    load_c(t)

                def load_c(t):
                    reach_then(sp, c_copied, t, sp_passed)
                    sp.dma_start(cin[:, :], A["comb"][:, bass.ds(t * G, G)]).then_inc(c_in, 16)

                def body(t, first, last):
                    if not last:
                        load(t + 1)
                    if not first:
                        store(t - 1)
                    if not (isinstance(t, int) and t == 0):
                        reach_then(sp, stored, 16 * t, sp_passed)
                    sp.dma_start(of[:, :, :], x_v[:, :, bass.ds(t * G, G)]).then_inc(res_in, 16)
                    for j in range(PIECES):
                        n = t * PIECES + j
                        reach_then(sp, piece_lo, n + 1, sp_passed)
                        sp.dma_start(stage[:, j % 2, :], A["w1"][:, bass.ds(n * P1W, P1W)]).then_inc(piece_in[j % 2], 16)

                def store(t):
                    reach_then(sp, added, t + 1, sp_passed)
                    sp.dma_start(x1_v[:, :, bass.ds(t * G, G)], of[:, :, :]).then_inc(stored, 16)

                load_c(0)
                sp.dma_start(sel[:, :], A["sel_m"]).then_inc(sel_in, 16)
                over_groups(sp, body)
                sp.wait_ge(x_lo, NG - 1)
                sp.wait_ge(stored, 16 * (NG - 1))
                sp.dma_start(xraw[:, :, :], x1_v[:, :, 0:G]).then_inc(next_in, 16)
                store(NG - 1)
                sp.wait_ge(stored, 16 * NG)

            @block.tensor
            def _(pe):
                def gate_up(t, c, q):
                    if c == 0:
                        reach(pe, x_lo, t)
                    reach(pe, hu_done, pair_free(t, c))
                    for j in range(2):
                        for k in range(KD):
                            last = mm3(pe, pair[c % 2][j][:, :], w(c * BLKM + (j * KD + k) * P), x(k, q), k == 0, k == KD - 1)
                    last.then_inc(gu_done, 1)
                    if c == 0:
                        if isinstance(t, int) and t == 0:
                            pe.wait_ge(sel_in, 16)
                        pe.wait_ge(c_copied, t + 1)
                    reach(pe, h_done, pair_free(t, c))
                    pe.matmul(pc[c % 2][:, :], sel[:, c * P:(c + 1) * P], cT[:, q, :],
                              start=True, stop=True).then_inc(cb_done, 1)

                def down(t, c):
                    pe.wait_ge(h_lo, t * CM + c + 1)
                    if c == 0:
                        reach(pe, added, t)
                    for k in range(KD):
                        last = mm3(pe, po[:, k, :], w(c * BLKM + 2 * D + k * P), (hh[:, c % RING, :], hl[:, c % RING, :]),
                                   c == 0, c == CM - 1)
                    last.then_inc(down_done, 1)

                def body(t, q, first, last):
                    for c in range(CM):
                        gate_up(t, c, q)
                        if c >= 2:
                            down(t, c - 2)
                        elif not first:
                            down(t - 1, c + CM - 2)
                    if last:
                        down(t, CM - 2)
                        down(t, CM - 1)

                over_pairs(pe, body)

            @block.scalar
            def _(act):
                def split_x(t, q):
                    act.wait_ge(x_in, 16 * t)
                    reach(act, gu_done, (t - 1) * CM)
                    nc.scalar.copy(xh[q][:, :, :], xraw[:, :, :]).then_inc(x_hi, 1)

                def silu(t, c):
                    act.wait_ge(gu_done, t * CM + c + 1)
                    reach(act, h_lo, pair_free(t, c))
                    nc.scalar.activation(s[:, c % 2, :], pair[c % 2][0][:, :], ACT.Silu).then_inc(s_done, 1)

                def split_hidden(t, c):
                    act.wait_ge(h_done, t * CM + c + 1)
                    reach(act, down_done, t * CM + last_user(c, CM, RING) + 1)
                    nc.scalar.copy(hh[:, c % RING, :], s[:, c % 2, :]).then_inc(h_hi, 1)

                def body(t, q, first, last):
                    for c in range(CM):
                        if c == 0 and not first:
                            split_hidden(t - 1, CM - 1)
                        silu(t, c)
                        if c >= 1:
                            split_hidden(t, c - 1)
                        if c == AHEAD and not last:
                            split_x(t + 1, 1 - q)
                        if c == AHEAD_LAST and last:
                            act.wait_ge(next_in, 16)
                            act.wait_ge(gu_done, (NG - 1) * CM)
                            nc.scalar.copy(xh[0][:, :, :], xraw[:, :, :]).then_inc(next_hi, 1)

                over_pairs(act, body)
                split_hidden(NG - 1, CM - 1)

            @block.vector
            def _(dve):
                def split_x(t, q):
                    dve.wait_ge(x_hi, t)
                    nc.vector.tensor_tensor(xl[q][:, :, :], xraw[:, :, :], xh[q][:, :, :], ALU.subtract).then_inc(x_lo, 1)

                def hidden(t, c):
                    dve.wait_ge(s_done, t * CM + c + 1)
                    nc.vector.tensor_tensor(s[:, c % 2, :], s[:, c % 2, :], pair[c % 2][1][:, :], ALU.mult).then_inc(hu_done, 1)
                    dve.wait_ge(hu_done, t * CM + c + 1)
                    dve.wait_ge(cb_done, t * CM + c + 1)
                    nc.vector.tensor_tensor(s[:, c % 2, :], s[:, c % 2, :], pc[c % 2][:, :], ALU.mult).then_inc(h_done, 1)

                def add(t):
                    dve.wait_ge(down_done, (t + 1) * CM)
                    dve.wait_ge(res_in, 16 * (t + 1))
                    nc.vector.tensor_tensor(of[:, :, :], of[:, :, :], po[:, :, :], ALU.add).then_inc(added, 1)

                def body(t, q, first, last):
                    for c in range(CM):
                        hidden(t, c)
                        if c == 1 and not first:
                            add(t - 1)
                        if c == AHEAD and not last:
                            split_x(t + 1, 1 - q)
                        if c == AHEAD_LAST and last:
                            dve.wait_ge(next_hi, 1)
                            nc.vector.tensor_tensor(xl[0][:, :, :], xraw[:, :, :], xh[0][:, :, :],
                                                    ALU.subtract).then_inc(next_lo, 1)

                over_pairs(dve, body)
                add(NG - 1)

            @block.gpsimd
            def _(pool):
                def copy_c(t, q):
                    reach(pool, cb_done, (t - 1) * CM)
                    reach_then(pool, c_in, 16 * (t + 1), pool_passed)
                    nc.gpsimd.tensor_copy(cT[:, q, :], cin[:, :]).then_inc(c_copied, 1)

                def split_piece(t, j):
                    n = t * PIECES + j
                    reach_then(pool, piece_in[j % 2], 16 * (t * (PIECES // 2) + j // 2 + 1), pool_passed)
                    nc.gpsimd.tensor_copy(wh[:, bass.ds(n * P1W, P1W)], stage[:, j % 2, :]).then_inc(piece_hi, 1)
                    pool.wait_ge(piece_hi, n + 1)
                    nc.gpsimd.tensor_tensor(wl[:, bass.ds(n * P1W, P1W)], stage[:, j % 2, :], wh[:, bass.ds(n * P1W, P1W)],
                                            ALU.subtract).then_inc(piece_lo, 1)

                def body(t, q, first, last):
                    for c in range(CM):
                        pool.wait_ge(h_hi, t * CM + c + 1)
                        nc.gpsimd.tensor_tensor(hl[:, c % RING, :], s[:, c % 2, :], hh[:, c % RING, :],
                                                ALU.subtract).then_inc(h_lo, 1)
                        if c % 2 == 1 and c > 1:
                            split_piece(t, c // 2 - 1)
                        if c == AHEAD and not last:
                            copy_c(t + 1, 1 - q)

                pool.sem_inc(piece_lo, 2)
                copy_c(0, 0)
                over_pairs(pool, body)


EVENTS = [(0, 0)] + [e for c in range(1, C1) for e in ((c, 0), (c - 1, 1))] + [(C1 - 1, 1)]
NE = len(EVENTS)
AT = {e: n for n, e in enumerate(EVENTS)}


def phase_3(nc, A, big, signals):
    wh, wl, cf, ident = (big[n] for n in ("wh", "wl", "cf", "ident"))
    iota = cf[:, 2:2 + SUB * E].rearrange("p (s e) -> p s e", e=E)
    ident_f = cf[0:2 * E, 2 + SUB * E:2 + SUB * E + 2 * E]
    with ExitStack() as memory:
        m = Mem(nc, memory, signals, "p3")
        sp_passed, dve_passed, pe_passed = m.sem("sp_passed"), m.sem("dve_passed"), m.sem("pe_passed")
        xraw, xh, xl = big["xraw"], big["xh"], big["xl"]
        xam = m.sb("xam", [P, G])
        xah, xal = m.sb("xah", [P, G], F32R), m.sb("xal", [P, G], F32R)
        yh, yl = m.sb("yh", [P, 2, KD, G], F32R), m.sb("yl", [P, 2, KD, G], F32R)
        ua = m.sb("ua", [P, 2, G])
        um = m.sb("um", [P, 2, G])
        uh, ul = m.sb("uh", [P, 4, G], F32R), m.sb("ul", [P, 4, G], F32R)
        mk = m.sb("mk", [P, 2, 3, G], BF16)
        wv = m.sb("wv", [P, 2, 2, G])
        s = m.sb("s", [P, 2, 2, G])
        ch, cl = m.sb("ch", [P, 2, 2, G], F32R), m.sb("cl", [P, 2, 2, G], F32R)
        mx = m.sb("mx", [P, 2, G])
        mh, ml = m.sb("mh", [P, C1, G], F32R), m.sb("ml", [P, C1, G], F32R)
        ta = um
        th, tl = m.sb("th", [P, G], F32R), m.sb("tl", [P, G], F32R)
        yo = m.sb("yo", [P, KD, G])
        mask = m.sb("mask", [P, B])
        idx = yo[:, 0, 0:B].bitcast(I32)
        vt = m.sb("vt", [P, SUB, S])
        vr = m.sb("vr", [P, SUB * S])
        v8 = m.sb("v8", [P, SUB, 8])
        i8 = m.sb("i8", [P, SUB, 8], U32)
        if8 = m.sb("if8", [P, SUB, 2])
        st = m.sb("st", [P, SUB, 3])
        c22 = m.sb("c22", [P, SUB, NC1], BF16)
        rest = m.sb("rest", [P, SUB, 2])
        lg = m.sb("lg", [P, SUB, E])
        gw = m.sb("gw", [P, KD, 2 * E], F32R)
        lT = xam[0:2 * E, :]
        cT = m.sb("cT", [NC1, G], BF16)
        sel = m.sb("sel", [NC1, N_SEL1 * P], BF16)
        tiles = (vt, vr, vr, vt, v8, i8, if8, st, c22, rest, lg)

        pair = [[m.pb(f"pair{i}{j}", [P, G]) for j in range(2)] for i in range(2)]
        pa = m.pb("pa", [P, 2, G])
        pf = m.pb("pf", [P, 2, G])
        logits = pf[:, 1, 0:SUB * 2 * E].rearrange("p (s e) -> p s e", e=2 * E)
        turned = pf[:, 0, :].bitcast(BF16)[0:NC1, 0:G]

        (x_in, x_hi, x_lo, idx_in, mask_made, vt_zero, xa_done, xa_masked, xa_hi, xa_lo, y_done, y_hi, y_lo,
         logits_done, route, e_done, ua_done, ua_copied, turned_done, turned_copied, bc_done, bc_copied, um_done,
         u_hi, u_lo, p_done, s_done, m_done, c_done, c_hi, c_lo, acc_done, mix_done, mix_hi, mix_lo, down_done,
         t_masked, t_done, t_hi, t_lo, out_done, res_in, added, stored, sel_in, gw_made, lt_done, lt_copied) = (m.sem(n) for n in (
             "x_in x_hi x_lo idx_in mask_made vt_zero xa_done xa_masked xa_hi xa_lo y_done y_hi y_lo "
             "logits_done route e_done ua_done ua_copied turned_done turned_copied bc_done bc_copied um_done "
             "u_hi u_lo p_done s_done m_done c_done c_hi c_lo acc_done mix_done mix_hi mix_lo down_done "
             "t_masked t_done t_hi t_lo out_done res_in added stored sel_in "
             "gw_made lt_done lt_copied").split())

        x1_v = A["x1"].rearrange("(k p) t -> p k t", p=P)
        out_v = A["out"].rearrange("(k p) t -> p k t", p=P)

        def w(o, n=P, c=0):
            return wh[r(c), o:o + n], wl[r(c), o:o + n]

        def r(c):
            return slice(0, min(P, H1 - c * P))

        def up_gate(c):
            if c == C1 - 1:
                return pair[c % 2][0][0:HALF, :], pair[c % 2][0][HALF:P, :]
            return pair[c % 2][0][:, :], pair[c % 2][1][:, :]

        def x(k):
            return xh[:, k, :], xl[:, k, :]

        def event(t, c, slot):
            if c < 0:
                return (t - 1) * NE + AT[(c + C1, slot)] + 1
            return t * NE + AT[(c, slot)] + 1

        BC = [(0, 1), (1, 0), (2, 1), (3, 0), (4, 1)]

        with nc.Block() as block:
            @block.sync
            def _(sp):
                def load(t):
                    reach_then(sp, x_lo, t - 1, sp_passed)
                    sp.dma_start(xraw[:, :, :], x1_v[:, :, bass.ds(t * G, G)]).then_inc(x_in, 16)

                def store(t):
                    reach_then(sp, added, t + 1, sp_passed)
                    sp.dma_start(out_v[:, :, bass.ds(t * G, G)], yo[:, :, :]).then_inc(stored, 16)

                def body(t):
                    if isinstance(t, int) and t == 0:
                        sp.wait_ge(mask_made, 1)
                    else:
                        store(t - 1)
                        reach_then(sp, stored, 16 * t, sp_passed)
                    sp.dma_start(yo[:, :, :], x1_v[:, :, bass.ds(t * G, G)]).then_inc(res_in, 16)

                sp.dma_start(idx, A["idx1"].partition_broadcast(P)).then_inc(idx_in, 16)
                sp.dma_start(sel[:, :], A["sel_1"]).then_inc(sel_in, 16)
                load(1)
                body(0)
                load(2)
                with sp.Fori(1, NG - 2) as t:
                    body(t)
                    load(t + 2)
                body(NG - 2)
                body(NG - 1)
                store(NG - 1)
                sp.wait_ge(stored, 16 * NG)

            @block.tensor
            def _(pe):
                def adapters(g):
                    reach(pe, x_lo, g)
                    reach(pe, added, g - 1)
                    for k in range(KD):
                        last = mm3(pe, pf[:, 0, :], w(W1_A + k * P), x(k), k == 0, k == KD - 1)
                    last.then_inc(xa_done, 1)

                def project(g):
                    pe.wait_ge(xa_lo, g + 1)
                    for o in range(KD):
                        for k in range(KD):
                            mm3(pe, pf[:, o, :], w(W1_W + k * D + o * P), x(k), k == 0, False)
                        last = mm3(pe, pf[:, o, :], w(W1_B + o * P), (xah[:, :], xal[:, :]), False, True)
                    last.then_inc(y_done, 1)

                def prepare_c(g, q):
                    pe.wait_ge(y_lo, g + 1)
                    if isinstance(g, int) and g == 0:
                        pe.wait_ge(gw_made, 2)
                    for k in range(KD):
                        pe.matmul(pf[0:2 * E, 1, :], gw[:, k, :], yh[:, q, k, :], start=k == 0, stop=False,
                                  skip_group_check=True)
                        last = pe.matmul(pf[0:E, 1, :], gw[:, k, 0:E], yl[:, q, k, :], start=False, stop=k == KD - 1,
                                         skip_group_check=True)
                    last.then_inc(lt_done, 1)
                    for k in range(KD):
                        last = mm3(pe, pf[:, 0, :], w(W1_UA + k * P), (yh[:, q, k, :], yl[:, q, k, :]), k == 0, k == KD - 1)
                    last.then_inc(ua_done, 1)
                    reach_then(pe, lt_copied, g + 1, pe_passed)
                    for b in range(SUB):
                        last = pe.transpose(logits[:, b, :], lT[:, b * P:(b + 1) * P], ident_f)
                    last.then_inc(logits_done, 1)

                def prepare_ag(g, q):
                    pe.wait_ge(route, g * ROUTE1 + 2)
                    for k in range(KD):
                        last = mm3(pe, pf[:, 1, :], w(W1_GA + k * P), (yh[:, q, k, :], yl[:, q, k, :]), k == 0, k == KD - 1)
                    last.then_inc(ua_done, 1)

                def turn(g):
                    pe.wait_ge(route, (g + 1) * ROUTE1)
                    pe.wait_ge(ua_copied, 2 * g + 1)
                    for b in range(SUB):
                        last = pe.transpose(turned[:, b * P:(b + 1) * P], c22[:, b, :], ident[:, :])
                    last.then_inc(turned_done, 1)

                def spread(g, n):
                    pe.wait_ge(turned_copied, g + 1)
                    if n == 0:
                        pe.wait_ge(ua_copied, 2 * g + 2)
                    else:
                        reach(pe, bc_copied, g * N_SEL1 + n - 1)
                    i, bank = BC[n]
                    pe.matmul(pf[:, bank, :], sel[:, i * P:(i + 1) * P], cT[:, :],
                              start=True, stop=True).then_inc(bc_done, 1)

                def main(t, c, q):
                    if c < 2:
                        reach(pe, m_done, event(t, c - 2, 1) if not (isinstance(t, int) and t == 0) else 0)
                    else:
                        pe.wait_ge(m_done, event(t, c - 2, 1))
                    o = W1_BLK + c * BLK1
                    for j in range(1 if c == C1 - 1 else 2):
                        for k in range(KD):
                            mm3(pe, pair[c % 2][j][:, :], w(o + (j * KD + k) * P), (yh[:, q, k, :], yl[:, q, k, :]), k == 0, False)
                    if c == 0:
                        pe.wait_ge(u_lo, 4 * (t + 1))
                    for j in range(2):
                        last = mm3(pe, pair[c % 2][0 if c == C1 - 1 else j][:, :], w(o + 2 * D + j * P), (uh[:, 2 * j, :], ul[:, 2 * j, :]), False, True)
                    last.then_inc(p_done, 1)

                def delta(t, c):
                    pe.wait_ge(m_done, event(t, c, 0))
                    o = W1_BLK + c * BLK1 + 2 * D
                    for j in range(2):
                        last = mm3(pe, pair[c % 2][0 if c == C1 - 1 else j][:, :], w(o + j * P), (uh[:, 2 * j + 1, :], ul[:, 2 * j + 1, :]), False, True)
                    last.then_inc(p_done, 1)

                def accumulate(t, c):
                    pe.wait_ge(c_lo, event(t, c, 1))
                    if c == 0:
                        reach(pe, t_masked, 2 * t)
                    for i in range(2):
                        last = mm3(pe, pa[:, i, :], w(W1_BLK + c * BLK1 + 2 * D + 2 * P, P, c), (ch[r(c), c % 2, i, :], cl[r(c), c % 2, i, :]),
                                   c == 0, c == C1 - 1)
                    last.then_inc(acc_done, 1)

                def down(t, last_group):
                    def block(o, c):
                        pe.wait_ge(mix_lo, t * C1 + c + 1)
                        return mm3(pe, pf[:, o, :], w(W1_BLK + c * BLK1 + 2 * D + 3 * P + o * P, P, c), (mh[r(c), c, :], ml[r(c), c, :]),
                                   c == 0, False)

                    for o in range(KD):
                        if not last_group:
                            pe.wait_ge(bc_copied, N_SEL1 * (t + 1) + N_SEL1 - 1 + o)
                        for c in range(C1 - 1):
                            block(o, c)
                        if o == 0:
                            accumulate(t, C1 - 1)
                    for o in range(KD):
                        last = block(o, C1 - 1)
                    last.then_inc(down_done, 1)
                    pe.wait_ge(t_lo, t + 1)
                    for o in range(KD):
                        last = mm3(pe, pf[:, o, :], w(W1_DB + o * P), (th[:, :], tl[:, :]), False, True)
                    last.then_inc(out_done, 1)

                def body(t, q, first, last):
                    more = not last
                    g, other = t + 1, 1 - q
                    main(t, 0, q)
                    main(t, 1, q)
                    delta(t, 0)
                    if more:
                        adapters(g)
                    main(t, 2, q)
                    delta(t, 1)
                    accumulate(t, 0)
                    if more:
                        project(g)
                    main(t, 3, q)
                    if more:
                        prepare_c(g, other)
                    delta(t, 2)
                    accumulate(t, 1)
                    if more:
                        prepare_ag(g, other)
                    main(t, 4, q)
                    delta(t, 3)
                    accumulate(t, 2)
                    main(t, 5, q)
                    if more:
                        turn(g)
                    delta(t, 4)
                    if more:
                        spread(g, 0)
                    accumulate(t, 3)
                    if more:
                        spread(g, 1)
                    delta(t, 5)
                    if more:
                        spread(g, 2)
                        spread(g, 3)
                    accumulate(t, 4)
                    if more:
                        spread(g, 4)
                    down(t, last)

                adapters(0)
                project(0)
                prepare_c(0, 0)
                prepare_ag(0, 0)
                turn(0)
                pe.wait_ge(sel_in, 16)
                for n in range(N_SEL1):
                    spread(0, n)
                over_pairs(pe, body)

            @block.scalar
            def _(act):
                def split_x(g):
                    act.wait_ge(x_in, 16 * g)
                    reach(act, y_done, g)
                    nc.scalar.copy(xh[:, :, :], xraw[:, :, :]).then_inc(x_hi, 1)

                def split_adapters(g):
                    act.wait_ge(xa_masked, g + 1)
                    nc.scalar.copy(xah[:, :], xam[:, :]).then_inc(xa_hi, 1)

                def split_y(g, q):
                    act.wait_ge(y_done, g + 1)
                    nc.scalar.copy(yh[:, q, :, :], pf[:, :, :]).then_inc(y_hi, 1)

                def take_logits(g):
                    act.wait_ge(lt_done, g + 1)
                    act.wait_ge(xa_lo, g + 1)
                    nc.scalar.copy(lT, pf[0:2 * E, 1, :]).then_inc(lt_copied, 1)

                def take_ua(g, j):
                    act.wait_ge(ua_done, 2 * g + j + 1)
                    reach(act, um_done, 4 * g)
                    nc.scalar.copy(ua[:, j, :], pf[:, j, :]).then_inc(ua_copied, 1)

                def route_exp(g):
                    act.wait_ge(route, g * ROUTE1 + EXP1)
                    nc.scalar.activation(vr[:, :], vr[:, :], ACT.Exp).then_inc(e_done, 1)

                def take_turned(g):
                    act.wait_ge(turned_done, g + 1)
                    nc.scalar.copy(cT[:, :], turned).then_inc(turned_copied, 1)

                def take_spread(g, n, q):
                    i, bank = BC[n]
                    act.wait_ge(bc_done, g * N_SEL1 + n + 1)
                    to = mk[:, q, i, :] if i < 3 else wv[:, q, i - 3, :]
                    nc.scalar.copy(to, pf[:, bank, :]).then_inc(bc_copied, 1)

                def split_u(g, a, b):
                    for n in range(a, b):
                        act.wait_ge(um_done, 4 * g + n + 1)
                        nc.scalar.copy(uh[:, n, :], um[:, n % 2, :]).then_inc(u_hi, 1)

                def silu(t, c, i):
                    act.wait_ge(p_done, event(t, c, i))
                    if not (isinstance(t, int) and t == 0 and c < 2):
                        act.wait_ge(mix_done, t * C1 + c - 1)
                        act.wait_ge(c_lo, event(t, c - 2, i))
                    nc.scalar.activation(s[r(c), c % 2, i, :], up_gate(c)[0], ACT.Silu).then_inc(s_done, 1)

                def split_c(t, c, i):
                    act.wait_ge(c_done, event(t, c, i))
                    reach(act, acc_done, t * C1 + c - 1)
                    nc.scalar.copy(ch[r(c), c % 2, i, :], s[r(c), c % 2, i, :]).then_inc(c_hi, 1)

                def split_mix(t, c):
                    act.wait_ge(mix_done, t * C1 + c + 1)
                    reach(act, down_done, t)
                    nc.scalar.copy(mh[r(c), c, :], mx[r(c), c % 2, :]).then_inc(mix_hi, 1)

                def split_t(t):
                    act.wait_ge(t_done, t + 1)
                    nc.scalar.copy(th[:, :], ta[:, 0, :]).then_inc(t_hi, 1)

                def body(t, q, first, last):
                    more = not last
                    g, other = t + 1, 1 - q
                    if more:
                        split_x(g)
                    for n, (c, i) in enumerate(EVENTS):
                        if more and n == NE - 1:
                            split_u(g, 0, 1)
                        silu(t, c, i)
                        if more and n == 10:
                            take_spread(g, 0, other)
                        if more and n == NE - 1:
                            take_spread(g, 2, other)
                            split_u(g, 1, 2)
                            take_spread(g, 3, other)
                        if n >= 1 and EVENTS[n - 1][1] == 0:
                            split_c(t, *EVENTS[n - 1])
                        if i == 1:
                            split_c(t, c, i)
                            if c < C1 - 1:
                                split_mix(t, c)
                        if not more:
                            continue
                        if n == 2:
                            split_adapters(g)
                        if n == 4:
                            split_y(g, other)
                        if n == 5:
                            take_logits(g)
                        if n == 6:
                            take_ua(g, 0)
                            route_exp(g)
                        if n == 7:
                            take_ua(g, 1)
                        if n == 9:
                            take_turned(g)
                        if n == 10:
                            take_spread(g, 1, other)
                    if more:
                        take_spread(g, 4, other)
                        split_u(g, 2, 4)
                    split_mix(t, C1 - 1)
                    split_t(t)

                split_adapters(0)
                split_y(0, 0)
                take_logits(0)
                take_ua(0, 0)
                route_exp(0)
                take_ua(0, 1)
                take_turned(0)
                for n in range(N_SEL1):
                    take_spread(0, n, 0)
                split_u(0, 0, 4)
                over_pairs(act, body)

            @block.vector
            def _(dve):
                V = nc.vector

                def split_x(g):
                    dve.wait_ge(x_hi, g)
                    V.tensor_tensor(xl[:, :, :], xraw[:, :, :], xh[:, :, :], ALU.subtract).then_inc(x_lo, 1)

                def mask_adapters(g):
                    dve.wait_ge(xa_done, g + 1)
                    reach(dve, xa_lo, g)
                    reach(dve, logits_done, g)
                    V.tensor_tensor(by_batch(xam[:, :]), by_batch(pf[:, 0, :]), over_tokens(mask, g),
                                    ALU.mult).then_inc(xa_masked, 1)
                    dve.wait_ge(xa_hi, g + 1)
                    V.tensor_tensor(xal[:, :], xam[:, :], xah[:, :], ALU.subtract).then_inc(xa_lo, 1)

                def split_y(g, q):
                    dve.wait_ge(y_hi, g + 1)
                    V.tensor_tensor(yl[:, q, :, :], pf[:, :, :], yh[:, q, :, :], ALU.subtract).then_inc(y_lo, 1)

                def route_part(g, part):
                    steps = Route(g, dve_passed, route, logits, iota, tiles)
                    if part == 0:
                        reach_then(dve, logits_done, g + 1, dve_passed)
                        route1_steps(V, steps, 0, 2 + 2 * SUB)
                    elif part == 1:
                        route1_steps(V, steps, 2 + 2 * SUB, EXP1)
                        reach(dve, turned_done, g)
                        route1_steps(V, steps, EXP1, MASKS1)
                        dve.wait_ge(e_done, g + 1)
                        route1_steps(V, steps, MASKS1, CUT1)
                    else:
                        route1_steps(V, steps, CUT1, ROUTE1)

                def mask_u(g, q, a, b):
                    dve.wait_ge(ua_copied, 2 * (g + 1))
                    reach(dve, t_lo, g - 1 if a == 0 else 0)
                    for n in range(a, b):
                        if n < 2:
                            dve.wait_ge(bc_copied, g * N_SEL1 + n + 1)
                        reach(dve, u_lo, 4 * g + n - 1)
                        V.tensor_tensor(um[:, n % 2, :], ua[:, n // 2, :], mk[:, q, n % 2, :], ALU.mult).then_inc(um_done, 1)

                def hidden(t, c, i, q):
                    dve.wait_ge(s_done, event(t, c, i))
                    sv = s[r(c), c % 2, i, :]
                    V.tensor_tensor(sv, sv, up_gate(c)[1], ALU.mult).then_inc(m_done, 1)
                    dve.wait_ge(m_done, event(t, c, i))
                    V.tensor_tensor(sv, sv, wv[r(c), q, i, :], ALU.mult).then_inc(c_done, 1)
                    if i == 1:
                        dve.wait_ge(c_done, event(t, c, i))
                        reach(dve, mix_lo, t * C1 + c - 1)
                        V.tensor_tensor(mx[r(c), c % 2, :], s[r(c), c % 2, 0, :], s[r(c), c % 2, 1, :], ALU.add).then_inc(mix_done, 1)

                def tail(t, q, more):
                    dve.wait_ge(acc_done, (t + 1) * C1)
                    reach(dve, t_lo, t)
                    dve.wait_ge(u_lo, 4 * (t + 2) if more else 4 * NG)
                    V.tensor_tensor(ta[:, 0, :], pa[:, 0, :], mk[:, q, 0, :], ALU.mult).then_inc(t_masked, 1)
                    V.tensor_tensor(ta[:, 1, :], pa[:, 1, :], mk[:, q, 2, :], ALU.mult).then_inc(t_masked, 1)
                    dve.wait_ge(t_masked, 2 * (t + 1))
                    V.tensor_tensor(ta[:, 0, :], ta[:, 0, :], ta[:, 1, :], ALU.add).then_inc(t_done, 1)

                def add(t):
                    dve.wait_ge(out_done, t + 1)
                    dve.wait_ge(res_in, 16 * (t + 1))
                    V.tensor_tensor(yo[:, :, :], yo[:, :, :], pf[:, :, :], ALU.add).then_inc(added, 1)

                def body(t, q, first, last):
                    more = not last
                    g, other = t + 1, 1 - q
                    if more:
                        split_x(g)
                    if not first:
                        add(t - 1)
                    for n, (c, i) in enumerate(EVENTS):
                        if more and n == NE - 1:
                            mask_u(g, other, 0, 2)
                        hidden(t, c, i, q)
                        if not more:
                            continue
                        if n == 2:
                            mask_adapters(g)
                        if n == 4:
                            split_y(g, other)
                        if n == 5 or n == 6:
                            route_part(g, n - 5)
                        if n == 8:
                            route_part(g, 2)
                    if more:
                        mask_u(g, other, 2, 4)
                    tail(t, q, more)

                dve.wait_ge(idx_in, 16)
                V.tensor_scalar(mask[:, :], idx, cf[:, 0:1], cf[:, 1:2], ALU.is_equal, ALU.mult).then_inc(mask_made, 1)
                V.memset(vt[:, :, :], 0.0).then_inc(vt_zero, 1)
                for n, part in enumerate((wh, wl)):
                    V.tensor_copy(gw[:, :, n * E:(n + 1) * E],
                                  part[:, W1_GW:W1_GW + KD * E].rearrange("p (k e) -> p k e", e=E)).then_inc(gw_made, 1)
                dve.wait_ge(mask_made, 1)
                mask_adapters(0)
                split_y(0, 0)
                dve.wait_ge(vt_zero, 1)
                for part in range(3):
                    route_part(0, part)
                mask_u(0, 0, 0, 4)
                over_pairs(dve, body)
                add(NG - 1)

            @block.gpsimd
            def _(pool):
                def sub(out, a, b, sem):
                    nc.gpsimd.tensor_tensor(out, a, b, ALU.subtract).then_inc(sem, 1)

                def split_u(g, a, b):
                    for n in range(a, b):
                        pool.wait_ge(u_hi, 4 * g + n + 1)
                        sub(ul[:, n, :], um[:, n % 2, :], uh[:, n, :], u_lo)

                def split_mix(t, c):
                    pool.wait_ge(mix_hi, t * C1 + c + 1)
                    sub(ml[r(c), c, :], mx[r(c), c % 2, :], mh[r(c), c, :], mix_lo)

                def body(t, q, first, last):
                    for n, (c, i) in enumerate(EVENTS):
                        if not last and n == NE - 1:
                            split_u(t + 1, 0, 2)
                        pool.wait_ge(c_hi, event(t, c, i))
                        sub(cl[r(c), c % 2, i, :], s[r(c), c % 2, i, :], ch[r(c), c % 2, i, :], c_lo)
                        if not last and n == NE - 1:
                            split_u(t + 1, 2, 4)
                        if i == 1:
                            split_mix(t, c)
                    pool.wait_ge(t_hi, t + 1)
                    sub(tl[:, :], ta[:, 0, :], th[:, :], t_lo)

                split_u(0, 0, 4)
                over_pairs(pool, body)


def program(nc, A):
    with ExitStack() as ctx:
        signals = ctx.enter_context(ExitStack())
        m = Mem(nc, ctx, signals, "w")
        big = {"wh": m.sb("wh", [P, SPLIT], F32R), "wl": m.sb("wl", [P, SPLIT], F32R),
               "cf": m.sb("cf", [P, 2 + SUB * E + 2 * E]), "ident": m.sb("ident", [P, P], BF16),
               "xraw": m.sb("xraw", [P, KD, G]),
               "xh": m.sb("xh", [P, KD, G], F32R), "xl": m.sb("xl", [P, KD, G], F32R),
               "cst_in": m.sem("cst_in")}
        with nc.Block() as block:
            @block.sync
            def _(sp):
                sp.dma_start(big["cf"][:, :], A["cf"]).then_inc(big["cst_in"], 16)
                sp.dma_start(big["ident"][:, :], A["ident"]).then_inc(big["cst_in"], 16)
                sp.wait_ge(big["cst_in"], 32)
        with ExitStack() as experts:
            e = Mem(nc, experts, signals, "m")
            big["xwh"] = e.sb("xwh", [P, W0_COLS - SPLIT], F32R)
            big["xwl"] = e.sb("xwl", [P, W0_COLS - SPLIT], F32R)
            with nc.sbuf_tensor("w_raw", [P, W0_COLS], F32) as raw:
                big["raw"] = raw
            big["mh"] = e.sb("mh", [P, WM_PAD], F32R)
            big["ml"] = e.sb("ml", [P, WM_PAD], F32R)
            phase_1(nc, A, big, signals)
            phase_2(nc, A, big, signals)
        phase_3(nc, A, big, signals)


def _rows(a):
    k = a.shape[0] // P
    return np.ascontiguousarray(a.reshape(k, P, a.shape[1]).transpose(1, 0, 2)).reshape(P, -1)


def _cols(parts, width):
    out = np.concatenate(parts, axis=1)
    return np.ascontiguousarray(np.concatenate([out, np.zeros((P, width - out.shape[1]), np.float32)], axis=1))


def _a_cols(a):
    return a.transpose(1, 0, 2).reshape(a.shape[1], E * R)


def _b_rows(a):
    return a.reshape(E * R, a.shape[2])


def _pack_0(v):
    parts = [_rows(_a_cols(v["L0_cond_Ag"])), _rows(_a_cols(v["L0_cond_Au"]))]
    ad = _a_cols(v["L0_cond_Ad"])
    for c in range(C0):
        b = slice(c * P, (c + 1) * P)
        parts += [_rows(v["L0_cond_Wg"][:, b]), _rows(v["L0_cond_Wu"][:, b]), _b_rows(v["L0_cond_Bg"])[:, b],
                  _b_rows(v["L0_cond_Bu"])[:, b], v["L0_cond_Wd"][b], ad[b]]
    parts += [_b_rows(v["L0_cond_Bd"]), _rows(v["L0_ffn_Wr"])]
    return _cols(parts, W0_COLS)


def _pack_m(v):
    g, u = (v[n].transpose(1, 0, 2).reshape(D, E * IM) for n in ("L0_ffn_Wg", "L0_ffn_Wu"))
    d = v["L0_ffn_Wd"].reshape(E * IM, D)
    parts = []
    for c in range(CM):
        b = slice(c * P, (c + 1) * P)
        parts += [_rows(g[:, b]), _rows(u[:, b]), d[b]]
    return _cols(parts, WM_PAD)


def _pack_1(v):
    def wide(a):
        return np.concatenate([a, np.zeros((a.shape[0], C1 * P - H1), np.float32)], axis=1)

    up, gate = wide(v["L1_ffn_w_up"].T), wide(v["L1_ffn_w_gate"].T)
    ub, gb = (wide(_b_rows(v[n].transpose(0, 2, 1))) for n in ("L1_ffn_up_B", "L1_ffn_gate_B"))
    da = wide(v["L1_ffn_down_A"].reshape(E * R, H1)).T
    wd = wide(v["L1_ffn_w_down"]).T
    parts = [_rows(v["L1_cond_A"].reshape(E * R, D).T), _rows(v["L1_cond_W"].T),
             _b_rows(v["L1_cond_Bm"].transpose(0, 2, 1)), _rows(v["L1_ffn_gate_w"].T),
             _rows(v["L1_ffn_up_A"].reshape(E * R, D).T), _rows(v["L1_ffn_gate_A"].reshape(E * R, D).T)]
    for c in range(C1):
        b = slice(c * P, (c + 1) * P)
        if c < C1 - 1:
            parts += [_rows(up[:, b]), _rows(gate[:, b]), ub[:, b], gb[:, b], da[b], wd[b]]
        else:
            a, n = slice(c * P, H1), np.zeros((P, HALF), np.float32)
            parts += [_rows(np.concatenate([up[:, a], gate[:, a]], axis=1)), np.zeros((P, D), np.float32),
                      ub[:, a], n, n, gb[:, a], da[b], wd[b]]
    parts += [_b_rows(v["L1_ffn_down_B"].transpose(0, 2, 1))]
    return _cols(parts, W1_PAD)


def _constants(scalings):
    row = np.arange(P)
    cf = np.concatenate([(row // R).astype(np.float32)[:, None], np.repeat(scalings, R)[:, None],
                         np.tile(np.arange(E, dtype=np.float32), (P, SUB)), np.eye(P, 2 * E)], axis=1).astype(np.float32)
    hidden = np.arange(CM * P)
    sel_m = np.zeros((NC0, CM * P), np.float32)
    for part in range(3):
        sel_m[part * E + hidden // IM, hidden] = 1.0
    sel_1 = np.zeros((NC1, N_SEL1, P), np.float32)
    for e in range(E):
        rows = row[row // R == e]
        sel_1[e, 0, rows] = ALPHA
        sel_1[E + e, 1, rows] = ALPHA
        sel_1[e, 1, rows] = -ALPHA
        sel_1[E + e, 2, rows] = ALPHA
    for part in range(3):
        for slot in range(2):
            sel_1[2 * E + 2 * part + slot, 3 + slot] = 1.0
    bf16 = mybir.dt.np(BF16)
    return {"cf": cf, "ident": np.eye(P).astype(bf16), "sel_m": sel_m.astype(bf16),
            "sel_1": sel_1.reshape(NC1, -1).astype(bf16)}


def kernel(**inputs):
    import concourse.bacc as bacc
    from concourse.bass_utils import run_bass_kernel_spmd

    v = {n: np.asarray(a) for n, a in inputs.items()}
    arrays = {
        "xT": np.ascontiguousarray(v["x"].reshape(T, D).T),
        "idx0": np.ascontiguousarray(v["itok_B_0_7"]),
        "idx1": np.ascontiguousarray(v["itok_B_0_6"]),
        "w0": _pack_0(v), "wm": _pack_m(v), "w1": _pack_1(v),
        **_constants(v["L1_cond_scalings"]),
    }
    nc = bacc.Bacc("TRN2", target_bir_lowering=False, num_devices=1)
    A = {n: nc.dram_tensor(n, a.shape, mybir.dt.from_np(a.dtype), kind="ExternalInput").ap() for n, a in arrays.items()}
    A["out"] = nc.dram_tensor("out", (D, T), F32, kind="ExternalOutput").ap()
    A["h"] = nc.dram_tensor("h", (D, T), F32).ap()
    A["comb"] = nc.dram_tensor("comb", (NC0, T), BF16).ap()
    A["x1"] = nc.dram_tensor("x1", (D, T), F32).ap()
    program(nc, A)
    r = run_bass_kernel_spmd(nc, [arrays], core_ids=[0])
    return np.ascontiguousarray(r.results[0]["out"].T).reshape(B, S, D)
```

```python
from contextlib import ExitStack

import numpy as np

import concourse.bass as bass
from concourse import mybir

P = 128
B, S, D = 128, 32, 256
T = B * S
G = 512
NG = T // G
GB = G // S
SUB = G // P
KD = D // P
E = 8
R = 16
I0 = 1024
C0 = I0 // P
IM = 176
IMR = IM - P
H1 = 704
C1 = -(-H1 // P)
HALF = P // 2
assert H1 == (C1 - 1) * P + HALF
ALPHA = 2.0

F32 = mybir.dt.float32
F32R = mybir.dt.float32r
BF16 = mybir.dt.bfloat16
I32 = mybir.dt.int32
U32 = mybir.dt.uint32
ALU = mybir.AluOpType
ACT = mybir.ActivationFunctionType
X = mybir.AxisListType.X

BLK0 = 2 * D + 2 * P + D + P
W0_A = 0
W0_BLK = 2 * D
W0_BD = W0_BLK + C0 * BLK0
W0_WR = W0_BD + D
W0_COLS = W0_WR + KD * E
BLKM = KD * 2 * IM + D
WM_COLS = E * BLKM
W1_A = 0
W1_W = D
W1_B = W1_W + KD * D
W1_GW = W1_B + D
W1_UA = W1_GW + KD * E
W1_GA = W1_UA + D
W1_BLK = W1_GA + D
BLK1 = 2 * D + 2 * P + P + D
W1_DB = W1_BLK + C1 * BLK1
W1_COLS = W1_DB + D

PIECES = 4
PM = -(-WM_COLS // (PIECES * (NG - 1)))
UNROLL = 8
NT = -(-(2 * T // P + E - 1) // UNROLL) * UNROLL
TURNS = NT // UNROLL
NK = T // P
P1W = -(-W1_COLS // (PIECES * TURNS))
WM_PAD = PM * PIECES * (NG - 1)
W1_PAD = P1W * PIECES * TURNS
STAGE = max(PM, P1W)
NROW = P + 2 * E
CK_STEP = 0
CK_TOKEN = CK_STEP + NK
CK_OWNER = CK_TOKEN + SUB
CK_FROM = CK_OWNER + 2 * E
CK_BEFORE = CK_FROM + 1
CK_EXPERT = CK_BEFORE + 2 * E
CK_POWER = CK_EXPERT + 2
CK_COLS = CK_POWER + UNROLL
assert E * NK == 2 * P
SPLIT = W0_BLK + -(-(W1_PAD - W0_BLK) // P) * P
RING = 3

N_SEL1 = 5
NC1 = 2 * E + 6


def reach(eng, sem, value):
    if isinstance(value, int) and value <= 0:
        return
    eng.wait_ge(sem, value)


def reach_then(eng, sem, value, passed):
    reach(eng, sem, value)
    if not isinstance(value, int):
        eng.sem_inc(passed, 1)


def mm3(pe, out, w, x, start, stop):
    (wh, wl), (xh, xl) = w, x
    pe.matmul(out, wh, xl, start=start, stop=False, skip_group_check=True)
    pe.matmul(out, wl, xh, start=False, stop=False, skip_group_check=True)
    return pe.matmul(out, wh, xh, start=False, stop=stop, skip_group_check=True)


def over_tokens(mask, t):
    return mask[:, bass.ds(t * GB, GB)].unsqueeze(2).broadcast_to([P, GB, S])


def by_batch(ap):
    return ap.rearrange("p (b s) -> p b s", s=S)


class Mem:

    def __init__(self, nc, memory, signals, prefix):
        self.nc, self.memory, self.signals, self.prefix = nc, memory, signals, prefix

    def sb(self, name, shape, dt=F32):
        return self.memory.enter_context(self.nc.sbuf_tensor(f"{self.prefix}_{name}", shape, dt))

    def pb(self, name, shape):
        return self.memory.enter_context(self.nc.psum_tensor(f"{self.prefix}_{name}", shape, F32))

    def sem(self, name):
        return self.signals.enter_context(self.nc.semaphore(f"{self.prefix}_{name}"))


def last_user(c, n, ring):
    return c - ring if c >= ring else max(b for b in range(n) if b % ring == c) - n


def over_groups(eng, body):
    body(0, True, False)
    body(1, False, False)
    with eng.Fori(2, NG - 1) as t:
        body(t, False, False)
    body(NG - 1, False, True)


def over_pairs(eng, body):
    body(0, 0, True, False)
    with eng.Fori(0, NG // 2 - 1) as i:
        body(i * 2 + 1, 1, False, False)
        body(i * 2 + 2, 0, False, False)
    body(NG - 1, 1, False, True)


def route0_steps(dve, k, lo, hi):
    base = k.group * ROUTE0
    z, ex, pr, v8, i8, if8, st, o0, o1, taken, lg, ranks, upto, r2, over, tk, lane, col = k.t
    kept = bass.ds(k.group * SUB, SUB)

    def each(a):
        return a.unsqueeze(2).broadcast_to([P, SUB, E])

    def pairs(a):
        return a[:, :, :].rearrange("p s k -> p (s k)")

    steps = [
        lambda: dve.tensor_tensor(z[:, :, :], lg[:, :, 0, 0:E], lg[:, :, 0, E:2 * E], ALU.add),
        lambda: dve.tensor_tensor(ex[:, :, :], lg[:, :, 1, 0:E], lg[:, :, 1, E:2 * E], ALU.add),
        lambda: dve.tensor_tensor(z[:, :, :], z[:, :, :], ex[:, :, :], ALU.add),
        lambda: dve.reduce_max(st[:, :, 0], z[:, :, :], X),
        lambda: dve.tensor_tensor(z[:, :, :], z[:, :, :], each(st[:, :, 0]), ALU.subtract),
        lambda: dve.reduce_sum(st[:, :, 1], ex[:, :, :], X),
        lambda: dve.reciprocal(st[:, :, 2], st[:, :, 1]),
        lambda: dve.tensor_tensor(pr[:, :, :], ex[:, :, :], each(st[:, :, 2]), ALU.mult),
    ] + [
        (lambda s=s: dve.max(v8[:, s, :], pr[:, s, :])) for s in range(SUB)
    ] + [
        (lambda s=s: dve.max_index(i8[:, s, :], v8[:, s, :], pr[:, s, :])) for s in range(SUB)
    ] + [
        lambda: dve.tensor_tensor(st[:, :, 3], v8[:, :, 0], v8[:, :, 1], ALU.add),
        lambda: dve.reciprocal(st[:, :, 0], st[:, :, 3]),
        lambda: dve.tensor_tensor(k.share[:, kept, :], v8[:, :, 0:2], st[:, :, 0].unsqueeze(2).broadcast_to([P, SUB, 2]), ALU.mult),
        lambda: dve.tensor_copy(if8[:, :, :], i8[:, :, 0:2]),
        lambda: dve.tensor_tensor(o0[:, :, :], k.iota, each(if8[:, :, 0]), ALU.is_equal),
        lambda: dve.tensor_tensor(o1[:, :, :], k.iota, each(if8[:, :, 1]), ALU.is_equal),
        lambda: dve.tensor_tensor(taken[:, :, :], o0[:, :, :], o1[:, :, :], ALU.add),
        lambda: dve.tensor_tensor(ranks[:, :, :], k.before, upto[:, :].unsqueeze(1).broadcast_to([P, SUB, E]), ALU.add),
        lambda: dve.tensor_tensor(upto[:, :], upto[:, :], k.total, ALU.add),
        lambda: dve.tensor_tensor(o0[:, :, :], o0[:, :, :], ranks[:, :, :], ALU.mult),
        lambda: dve.tensor_tensor(o1[:, :, :], o1[:, :, :], ranks[:, :, :], ALU.mult),
        lambda: dve.reduce_sum(r2[:, :, 0], o0[:, :, :], X),
        lambda: dve.reduce_sum(r2[:, :, 1], o1[:, :, :], X),
        lambda: dve.tensor_copy(k.rank[:, kept, :], r2[:, :, :]),
        lambda: dve.tensor_copy(k.expert[:, kept, :], if8[:, :, :]),
        lambda: dve.tensor_tensor(over[:, :, :], pairs(r2).unsqueeze(2).broadcast_to([P, 2 * SUB, NK]),
                                  k.step.unsqueeze(1).broadcast_to([P, 2 * SUB, NK]), ALU.is_ge),
        lambda: dve.reduce_sum(tk[:, :], over[:, :, :], X),
        lambda: dve.scalar_tensor_tensor(lane[:, :], tk[:, :], float(-P), pairs(r2), ALU.mult, ALU.add),
        lambda: dve.scalar_tensor_tensor(col[:, :], pairs(if8), float(NK), tk[:, :], ALU.mult, ALU.add),
    ]
    assert len(steps) == ROUTE0
    for n in range(lo, hi):
        steps[n]().then_inc(k.route, 1)
        reach_then(dve, k.route, base + n + 1, k.passed)


def route1_steps(dve, k, lo, hi):
    base = k.group * ROUTE1
    vt, vr, er, wt, v8, i8, if8, st, c22, rest, lg = k.t

    def each(a, n):
        return a.unsqueeze(2).broadcast_to([P, SUB, n])

    steps = [
        lambda: dve.tensor_copy(lg[:, :, :], k.logits[:, :, 0:E]),
        lambda: dve.tensor_tensor(lg[:, :, :], lg[:, :, :], k.logits[:, :, E:2 * E], ALU.add),
    ] + [
        (lambda s=s: dve.max(v8[:, s, :], lg[:, s, :])) for s in range(SUB)
    ] + [
        lambda: dve.tensor_copy(vt[:, :, 0:2], v8[:, :, 0:2]),
        lambda: dve.transpose(vr[:, :], vt[:, :, :].rearrange("p s f -> p (s f)")),
        lambda: dve.reduce_max(st[:, :, 0], by_sub(vr), X),
        lambda: dve.tensor_tensor(by_sub(vr), by_sub(vr), each(st[:, :, 0], S), ALU.subtract),
    ] + [
        (lambda s=s: dve.max_index(i8[:, s, :], v8[:, s, :], lg[:, s, :])) for s in range(SUB)
    ] + [
        lambda: dve.tensor_copy(if8[:, :, :], i8[:, :, 0:2]),
        lambda: dve.tensor_tensor(c22[:, :, 0:E], k.iota, each(if8[:, :, 0], E), ALU.is_equal),
        lambda: dve.tensor_tensor(c22[:, :, E:2 * E], k.iota, each(if8[:, :, 1], E), ALU.is_equal),
        lambda: dve.reduce_sum(st[:, :, 1], by_sub(er), X),
        lambda: dve.reciprocal(st[:, :, 2], st[:, :, 1]),
        lambda: dve.tensor_tensor(by_sub(er), by_sub(er), each(st[:, :, 2], S), ALU.mult),
        lambda: dve.transpose(wt[:, :, :].rearrange("p s f -> p (s f)"), er[:, :]),
        lambda: dve.tensor_copy(c22[:, :, 2 * E:2 * E + 2], wt[:, :, 0:2]),
        lambda: dve.tensor_tensor(rest[:, :, :], wt[:, :, 0:2], c22[:, :, 2 * E:2 * E + 2], ALU.subtract),
        lambda: dve.tensor_copy(c22[:, :, 2 * E + 2:2 * E + 4], rest[:, :, :]),
        lambda: dve.tensor_tensor(c22[:, :, 2 * E + 4:2 * E + 6], rest[:, :, :], c22[:, :, 2 * E + 2:2 * E + 4], ALU.subtract),
    ]
    assert len(steps) == ROUTE1
    for n in range(lo, hi):
        steps[n]().then_inc(k.route, 1)
        reach_then(dve, k.route, base + n + 1, k.passed)


def by_sub(rows):
    return rows[:, :].rearrange("p (s t) -> p s t", t=S)


ROUTE0 = 35
EXP0 = 5
TOP0 = 16
TAKEN0 = 23
ROUTE1 = 25
EXP1 = 10
MASKS1 = 17
CUT1 = 21


class Route:

    def __init__(self, group, passed, route, logits, iota, t):
        self.passed, self.group, self.route, self.logits, self.iota, self.t = passed, group, route, logits, iota, t


def phase_1(nc, A, big, signals):
    wh, wl, mh, ml, raw, cf, ident = (big[n] for n in ("wh", "wl", "mh", "ml", "raw", "cf", "ident"))
    iota = cf[:, 2:2 + SUB * E].rearrange("p (s e) -> p s e", e=E)

    def parts(a, b):
        if a >= SPLIT:
            return big["xwh"][:, a - SPLIT:b - SPLIT], big["xwl"][:, a - SPLIT:b - SPLIT]
        assert b <= SPLIT
        return wh[:, a:b], wl[:, a:b]

    with ExitStack() as memory:
        m = Mem(nc, memory, signals, "p1")
        sp_passed, dve_passed, pool_passed = m.sem("sp_passed"), m.sem("dve_passed"), m.sem("pool_passed")
        xraw, xh, xl = big["xraw"], big["xh"], big["xl"]
        xam = m.sb("xam", [P, 2, G])
        xah, xal = m.sb("xah", [P, 2, G], F32R), m.sb("xal", [P, 2, G], F32R)
        s = m.sb("s", [P, 2, G])
        hh, hl = m.sb("hh", [P, RING, G], F32R), m.sb("hl", [P, RING, G], F32R)
        dm = xam[:, 0, :]
        dh, dl = m.sb("dh", [P, G], F32R), m.sb("dl", [P, G], F32R)
        oh, ol = m.sb("oh", [P, KD, G], F32R), m.sb("ol", [P, KD, G], F32R)
        rows = m.sb("rows", [P, SUB, D])
        stage = m.sb("stage", [P, 2, PM])
        mask = m.sb("mask", [P, B], BF16)
        idx = rows[:, 0, 0:B].bitcast(I32)
        ck = m.sb("ck", [P, CK_COLS])
        cb = m.sb("cb", [P, 2 * P + E * NK], BF16)
        iota_w = cb[:, 2 * P:2 * P + E * NK]
        turner = m.sb("turner", [P, KD, NROW], F32R)
        lg = m.sb("lg", [P, SUB, KD, 2 * E])
        tiles = [m.sb(n, [P, SUB, w], dt) for n, w, dt in (
            ("z", E, F32), ("ex", E, F32), ("pr", E, F32), ("v8", 8, F32), ("i8", 8, U32), ("if8", 2, F32),
            ("st", 4, F32), ("o0", E, F32), ("o1", E, F32), ("taken", E, BF16))]
        z, ex, taken = tiles[0], tiles[1], tiles[-1]
        ranks = tiles[2]
        upto = m.sb("upto", [P, E])
        r2 = m.sb("r2", [P, SUB, 2])
        tk, lane, col = (m.sb(n, [P, 2 * SUB]) for n in ("tk", "lane", "col"))
        number = m.sb("number", [P, SUB])
        at_row = m.sb("at_row", [P, 2, P], F32R)
        at_col = m.sb("at_col", [P, 2, E * NK], F32R)
        over = at_col[:, 0, :].rearrange("p (n k) -> p n k", k=NK)
        tiles += [lg, ranks, upto, r2, over, tk, lane, col]
        lists = m.sb("lists", [P, E * NK])
        owned, count, flag, flagb, flage, tn = (m.sb(n, [P, 2] + w, dt) for n, w, dt in (
            ("owned", [E], F32), ("count", [], F32), ("flag", [], F32), ("flagb", [], BF16), ("flage", [], F32),
            ("tn", [], F32)))
        flags = m.sb("flags", [P, 2, E], BF16)
        pick = at_col[:, :, 0:NT]
        picke = s[:, 0, :].bitcast(BF16)[:, 0:2 * NT].rearrange("p (n t) -> p n t", t=NT)
        turned_lists = at_row

        pair = [[m.pb(f"pair{i}{j}", [P, G]) for j in range(2)] for i in range(2)]
        po = m.pb("po", [P, KD, G])
        pd = m.pb("pd", [P, G])
        pm = m.pb("pm", [P, G])
        spare = (pm, pair[0][0], pair[0][1], pair[1][0])
        before = pm[:, 0:SUB * E].rearrange("p (s e) -> p s e", e=E)
        total = pm[:, SUB * E:SUB * E + E]
        listed = pm[:, E * NK:2 * E * NK]

        raw_in = [m.sem(f"raw_in{n}") for n in range(C0 + 3)]
        (w_hi, w_lo, x_in, x_hi, x_lo, idx_in, mask_made, xa_done, xa_masked, xa_hi, xa_lo, gu_done, s_done,
         h_done, h_hi, h_lo, down_done, d_masked, d_hi, d_lo, out_done, out_hi, out_lo, stored, ck_in, turner_made,
         rows_done, rows_taken, route, e_done, counted, number_made, picked, listed_done, lists_made, piece_hi,
         piece_lo, index, sized, lists_turned, lists_taken, found) = (
            m.sem(n) for n in (
                "w_hi w_lo x_in x_hi x_lo idx_in mask_made xa_done xa_masked xa_hi xa_lo gu_done s_done "
                "h_done h_hi h_lo down_done d_masked d_hi d_lo out_done out_hi out_lo stored ck_in turner_made "
                "rows_done rows_taken route e_done counted number_made picked listed_done lists_made piece_hi "
                "piece_lo index sized lists_turned lists_taken found").split())
        piece_in = [m.sem(f"piece_in{n}") for n in range(2)]

        x_v = A["xT"].rearrange("(k p) t -> p k t", p=P)
        h_v = A["h"].rearrange("(b p) d -> p b d", p=P)
        ends = [0, W0_BLK] + [W0_BLK + (c + 1) * BLK0 for c in range(C0)] + [W0_COLS]
        cuts = list(zip(sorted({*ends[:-1], SPLIT}), sorted({*ends[1:], SPLIT})))
        split_for = [sum(b <= ends[c + 2] for _, b in cuts) for c in range(C0)]

        def w(o, n=P):
            return parts(o, o + n)

        def x(k):
            return xh[:, k, :], xl[:, k, :]

        def turned(bank):
            return bank[:, 0:KD * NROW].rearrange("p (k n) -> p k n", n=NROW)

        def free_slot(c):
            return last_user(c, C0, RING)

        with nc.Block() as block:
            @block.sync
            def _(sp):
                sp.dma_start(xraw[:, :, :], x_v[:, :, 0:G]).then_inc(x_in, 16)
                sp.dma_start(raw[:, cuts[0][0]:cuts[0][1]], A["w0"][:, cuts[0][0]:cuts[0][1]]).then_inc(raw_in[0], 16)
                sp.dma_start(idx, A["idx0"].partition_broadcast(P)).then_inc(idx_in, 16)
                sp.dma_start(ck[:, :], A["ck"]).then_inc(ck_in, 16)
                sp.dma_start(cb[:, :], A["cb"]).then_inc(ck_in, 16)
                for n, (a, b) in enumerate(cuts[1:]):
                    sp.dma_start(raw[:, a:b], A["w0"][:, a:b]).then_inc(raw_in[n + 1], 16)

                def store(t):
                    reach_then(sp, rows_taken, (t + 1) * SUB, sp_passed)
                    sp.dma_start(h_v[:, bass.ds(t * SUB, SUB), :], rows[:, :, :]).then_inc(stored, 16)

                def body(t, first, last):
                    if not last:
                        reach_then(sp, x_lo, t + 1, sp_passed)
                        sp.dma_start(xraw[:, :, :], x_v[:, :, bass.ds((t + 1) * G, G)]).then_inc(x_in, 16)
                    if first:
                        return
                    for j in range(PIECES):
                        n = (t - 1) * PIECES + j
                        reach_then(sp, piece_lo, n + 1, sp_passed)
                        sp.dma_start(stage[:, j % 2, :], A["wm"][:, bass.ds(n * PM, PM)]).then_inc(piece_in[j % 2], 16)
                        if j == 1:
                            store(t - 1)

                over_groups(sp, body)
                store(NG - 1)
                sp.wait_ge(stored, 16 * NG)

            @block.tensor
            def _(pe):
                def adapters(t):
                    pe.wait_ge(x_lo, t + 1)
                    reach(pe, lists_made, t)
                    for j in range(2):
                        if j == 1:
                            reach(pe, h_done, t * C0)
                        out = (pm, pair[1][0])[j]
                        for k in range(KD):
                            last = mm3(pe, out[:, :], w(W0_A + (j * KD + k) * P), x(k), k == 0, k == KD - 1)
                        last.then_inc(xa_done, 1)

                def gate_up(t, c, first, between=None):
                    if first:
                        pe.wait_ge(w_lo, split_for[c])
                    reach(pe, h_done, t * C0 + c - 1)
                    o = W0_BLK + c * BLK0
                    for j in range(2):
                        for k in range(KD):
                            mm3(pe, pair[c % 2][j][:, :], w(o + (j * KD + k) * P), x(k), k == 0, False)
                        if between and j == 0:
                            between()
                    for j in range(2):
                        if c == 0:
                            pe.wait_ge(xa_lo, 2 * t + j + 1)
                        last = mm3(pe, pair[c % 2][j][:, :], w(o + 2 * D + j * P), (xah[:, j, :], xal[:, j, :]), False, True)
                    last.then_inc(gu_done, 1)

                def down(t, c):
                    pe.wait_ge(h_lo, t * C0 + c + 1)
                    if c == 0:
                        reach(pe, d_masked, t)
                        reach(pe, out_hi, t)
                        reach(pe, out_lo, t)
                    o = W0_BLK + c * BLK0 + 2 * D + 2 * P
                    h = hh[:, c % RING, :], hl[:, c % RING, :]
                    mm3(pe, pd[:, :], w(o + D), h, c == 0, c == C0 - 1)
                    for k in range(KD):
                        last = mm3(pe, po[:, k, :], w(o + k * P), h, c == 0, False)
                    last.then_inc(down_done, 1)

                def adapted(t):
                    pe.wait_ge(d_lo, t + 1)
                    for k in range(KD):
                        last = mm3(pe, po[:, k, :], w(W0_BD + k * P), (dh[:, :], dl[:, :]), False, True)
                    last.then_inc(out_done, 1)

                def turn(t, b, bank=pm):
                    pe.wait_ge(out_lo, t + 1)
                    if bank is pm:
                        reach(pe, rows_taken, t * SUB + b)
                    if b == 0:
                        if isinstance(t, int) and t == 0:
                            pe.wait_ge(turner_made, 5)
                        pe.wait_ge(xa_masked, 2 * NG if isinstance(t, int) and t == NG - 1 else 2 * (t + 2))
                    tok = slice(b * P, (b + 1) * P)
                    for k in range(KD):
                        pe.matmul(turned(bank)[:, k, :], oh[:, k, tok], turner[:, k, :], start=True, stop=False,
                                  skip_group_check=True)
                        last = pe.matmul(turned(bank)[:, k, :], ol[:, k, tok], turner[:, k, :], start=False, stop=True,
                                         skip_group_check=True)
                    last.then_inc(rows_done, 1)

                def count_pairs(t):
                    pe.wait_ge(route, t * ROUTE0 + TAKEN0)
                    earlier, ones = cb[:, 0:P], cb[:, P:2 * P]
                    pe.matmul(before[:, :, :], earlier, taken[:, :, :], start=True, stop=False, skip_group_check=True)
                    for n in range(1, SUB):
                        pe.matmul(before[:, n:SUB, :], ones, taken[:, 0:SUB - n, :], start=False, stop=n == SUB - 1,
                                  skip_group_check=True)
                    for b in range(SUB):
                        last = pe.matmul(total, ones, taken[:, b, :], start=b == 0, stop=b == SUB - 1, skip_group_check=True)
                    last.then_inc(counted, 1)

                def list_pairs(t, lo, hi):
                    for n in range(lo, hi):
                        pe.wait_ge(picked, 2 * (t * 2 * SUB + n + 1))
                        pe.matmul(listed, at_row[:, n % 2, :], at_col[:, n % 2, :], start=n == 0, stop=n == 2 * SUB - 1,
                                  skip_group_check=True).then_inc(listed_done, 1)

                def body(t, first, last):
                    g = t - 1
                    for c in range(C0):
                        between = None
                        if c == 2 and not first:
                            between = lambda: turn(g, 1)
                        if c == 7 and not first:
                            between = lambda: list_pairs(g, 2, 4)
                        gate_up(t, c, first, between)
                        if c == 0 and not first:
                            adapted(g)
                        if c == 1 and not first:
                            turn(g, 0)
                        if c == 2 and not first:
                            turn(g, 2)
                        if c == 5 and not first:
                            count_pairs(g)
                        if c == 7 and not first:
                            list_pairs(g, 4, 6)
                        if c >= 2:
                            down(t, c - 2)
                        if c == 2 and not first:
                            turn(g, 3)
                        if c == 6 and not first:
                            list_pairs(g, 0, 2)
                    if not first:
                        list_pairs(g, 6, 8)
                    down(t, C0 - 2)
                    if not last:
                        adapters(t + 1)
                    down(t, C0 - 1)

                pe.wait_ge(w_lo, 1)
                adapters(0)
                over_groups(pe, body)
                g = NG - 1
                adapted(g)
                for b in range(SUB):
                    turn(g, b, spare[b])
                count_pairs(g)
                list_pairs(g, 0, 2 * SUB)

                pe.wait_ge(index, 6)
                earlier, ones = cb[:, 0:P], cb[:, P:2 * P]
                pe.matmul(po[:, 0, 0:2], earlier, flagb[:, :], start=True, stop=False, skip_group_check=True)
                pe.matmul(po[:, 0, 1:2], ones, flagb[:, 0:1], start=False, stop=True, skip_group_check=True)
                for n in range(2):
                    last = pe.matmul(po[:, 0, E:2 * E], ones, flags[:, n, :], start=n == 0, stop=n == 1, skip_group_check=True)
                last.then_inc(sized, 1)
                pe.wait_ge(lists_made, NG + 1)
                for n in range(2):
                    last = pe.transpose(pd[:, n * P:(n + 1) * P], lists[:, n * P:(n + 1) * P], big["ident_f"][:, :])
                last.then_inc(lists_turned, 1)
                pe.wait_ge(index, 12)
                for n in range(2):
                    pe.matmul(po[:, 0, P:P + NT], ones, picke[:, n, :], start=n == 0, stop=n == 1, skip_group_check=True)
                pe.wait_ge(lists_taken, 1)
                for n in range(2):
                    last = pe.matmul(po[:, 0, 2 * P:2 * P + NT], turned_lists[:, n, :], pick[:, n, :], start=n == 0, stop=n == 1,
                                     skip_group_check=True)
                last.then_inc(found, 1)

            @block.scalar
            def _(act):
                def split_weights(n):
                    a, b = cuts[n]
                    act.wait_ge(raw_in[n], 16)
                    nc.scalar.copy(parts(a, b)[0], raw[:, a:b]).then_inc(w_hi, 1)

                def split_x(t):
                    act.wait_ge(x_in, 16 * (t + 1))
                    reach(act, gu_done, t * C0)
                    nc.scalar.copy(xh[:, :, :], xraw[:, :, :]).then_inc(x_hi, 1)

                def split_adapters(t):
                    for j in range(2):
                        act.wait_ge(xa_masked, 2 * t + j + 1)
                        nc.scalar.copy(xah[:, j, :], xam[:, j, :]).then_inc(xa_hi, 1)

                def silu(t, c):
                    act.wait_ge(gu_done, t * C0 + c + 1)
                    reach(act, h_lo, t * C0 + c - 1)
                    nc.scalar.activation(s[:, c % 2, :], pair[c % 2][0][:, :], ACT.Silu).then_inc(s_done, 1)

                def split_hidden(t, c):
                    act.wait_ge(h_done, t * C0 + c + 1)
                    reach(act, down_done, t * C0 + free_slot(c) + 1)
                    nc.scalar.copy(hh[:, c % RING, :], s[:, c % 2, :]).then_inc(h_hi, 1)

                def split_down(t):
                    act.wait_ge(d_masked, t + 1)
                    reach(act, out_done, t)
                    nc.scalar.copy(dh[:, :], dm).then_inc(d_hi, 1)

                def take_output(t):
                    act.wait_ge(out_done, t + 1)
                    reach(act, rows_done, t * SUB)
                    nc.scalar.copy(oh[:, :, :], po[:, :, :]).then_inc(out_hi, 1)

                def route_exp(t):
                    act.wait_ge(route, t * ROUTE0 + EXP0)
                    nc.scalar.activation(ex[:, :, :], z[:, :, :], ACT.Exp).then_inc(e_done, 1)

                def take_rows(t, b, bank=pm):
                    act.wait_ge(rows_done, t * SUB + b + 1)
                    if b == 0:
                        reach(act, stored, 16 * t)
                        reach(act, route, t * ROUTE0)
                    nc.scalar.copy(lg[:, b, :, :], turned(bank)[:, :, P:NROW])
                    nc.scalar.copy(rows[:, b, :].rearrange("p (k f) -> p k f", f=P), turned(bank)[:, :, 0:P]).then_inc(rows_taken, 1)

                def body(t, first, last):
                    if not first:
                        split_down(t - 1)
                    for c in range(C0):
                        if first:
                            for n in range(split_for[c], split_for[c + 1] if c + 1 < C0 else len(cuts)):
                                split_weights(n)
                        silu(t, c)
                        if c == 0 and not first:
                            take_output(t - 1)
                        if c >= 1:
                            split_hidden(t, c - 1)
                        if c == 1 and not first:
                            take_rows(t - 1, 0)
                            take_rows(t - 1, 1)
                        if c == 2 and not first:
                            take_rows(t - 1, 2)
                            take_rows(t - 1, 3)
                        if c == 3 and not first:
                            route_exp(t - 1)
                    if not last:
                        split_x(t + 1)
                    split_hidden(t, C0 - 1)
                    if not last:
                        split_adapters(t + 1)

                split_weights(0)
                split_x(0)
                split_weights(1)
                split_adapters(0)
                over_groups(act, body)
                split_down(NG - 1)
                take_output(NG - 1)
                for b in range(SUB):
                    take_rows(NG - 1, b, spare[b])
                route_exp(NG - 1)
                act.wait_ge(lists_turned, 1)
                act.wait_ge(listed_done, NG * 2 * SUB)
                nc.scalar.copy(turned_lists[:, :, :].rearrange("p n r -> p (n r)"), pd[:, 0:2 * P]).then_inc(lists_taken, 1)

            @block.vector
            def _(dve):
                def split_weights(n):
                    a, b = cuts[n]
                    dve.wait_ge(w_hi, n + 1)
                    nc.vector.tensor_tensor(parts(a, b)[1], raw[:, a:b], parts(a, b)[0], ALU.subtract).then_inc(w_lo, 1)

                def split_x(t):
                    dve.wait_ge(x_hi, t + 1)
                    nc.vector.tensor_tensor(xl[:, :, :], xraw[:, :, :], xh[:, :, :], ALU.subtract).then_inc(x_lo, 1)

                def mask_adapters(t):
                    for j in range(2):
                        dve.wait_ge(xa_done, 2 * t + j + 1)
                        if j == 0:
                            reach(dve, d_lo, t - 1)
                        else:
                            reach(dve, xa_lo, 2 * t)
                        nc.vector.tensor_tensor(by_batch(xam[:, j, :]), by_batch((pm, pair[1][0])[j][:, :]),
                                                over_tokens(mask, t), ALU.mult).then_inc(xa_masked, 1)
                    for j in range(2):
                        dve.wait_ge(xa_hi, 2 * t + j + 1)
                        nc.vector.tensor_tensor(xal[:, j, :], xam[:, j, :], xah[:, j, :], ALU.subtract).then_inc(xa_lo, 1)

                def hidden(t, c):
                    dve.wait_ge(s_done, t * C0 + c + 1)
                    nc.vector.tensor_tensor(s[:, c % 2, :], s[:, c % 2, :], pair[c % 2][1][:, :], ALU.mult).then_inc(h_done, 1)

                def mask_down(t):
                    dve.wait_ge(down_done, (t + 1) * C0)
                    dve.wait_ge(xa_lo, 2 * NG if isinstance(t, int) and t == NG - 1 else 2 * (t + 2))
                    nc.vector.tensor_tensor(by_batch(dm), by_batch(pd[:, :]), over_tokens(mask, t),
                                            ALU.mult).then_inc(d_masked, 1)
                    dve.wait_ge(d_hi, t + 1)
                    nc.vector.tensor_tensor(dl[:, :], dm, dh[:, :], ALU.subtract).then_inc(d_lo, 1)

                def split_output(t):
                    dve.wait_ge(out_hi, t + 1)
                    nc.vector.tensor_tensor(ol[:, :, :], po[:, :, :], oh[:, :, :], ALU.subtract).then_inc(out_lo, 1)

                def route_part(t, part):
                    r = Route(t, dve_passed, route, None, iota, tiles)
                    r.share, r.rank, r.expert = big["share"], big["rank"], big["expert"]
                    r.before, r.total, r.step = before, total, ck[:, CK_STEP:CK_STEP + NK]
                    if part == 0:
                        reach_then(dve, rows_taken, (t + 1) * SUB, dve_passed)
                        route0_steps(nc.vector, r, 0, EXP0)
                        dve.wait_ge(e_done, t + 1)
                        route0_steps(nc.vector, r, EXP0, TOP0)
                    elif part == 1:
                        route0_steps(nc.vector, r, TOP0, TAKEN0)
                    else:
                        reach_then(dve, counted, t + 1, dve_passed)
                        route0_steps(nc.vector, r, TAKEN0, ROUTE0)

                def pick_pairs(t, lo, hi):
                    for n in range(lo, hi):
                        p = t * 2 * SUB + n
                        if n >= 2:
                            dve.wait_ge(listed_done, p - 1)
                        else:
                            dve.wait_ge(number_made, t + 1)
                        nc.vector.tensor_scalar(at_row[:, n % 2, :], iota_w[:, 0:P], lane[:, n:n + 1], None,
                                                ALU.is_equal).then_inc(picked, 1)
                        nc.vector.tensor_scalar(at_col[:, n % 2, :], iota_w, col[:, n:n + 1],
                                                number[:, n // 2:n // 2 + 1], ALU.is_equal, ALU.mult).then_inc(picked, 1)

                def add_lists(t):
                    dve.wait_ge(listed_done, (t + 1) * 2 * SUB)
                    dve.wait_ge(lists_made, t + 1)
                    nc.vector.tensor_tensor(lists[:, :], lists[:, :], listed, ALU.add).then_inc(lists_made, 1)
                    nc.vector.tensor_scalar(number[:, :], number[:, :], float(G), None, ALU.add).then_inc(number_made, 1)

                def body(t, first, last):
                    if not first:
                        mask_down(t - 1)
                    for c in range(C0):
                        if first:
                            for n in range(split_for[c], split_for[c + 1] if c + 1 < C0 else len(cuts)):
                                split_weights(n)
                        if c == 6 and not first:
                            pick_pairs(t - 1, 0, 2)
                        if c == 7 and not first:
                            pick_pairs(t - 1, 4, 7)
                        hidden(t, c)
                        if first:
                            if c == 0:
                                make_turner(0)
                            if c == C0 - 1:
                                make_turner(1)
                            continue
                        if c == 0:
                            split_output(t - 1)
                        if 3 <= c <= 5:
                            route_part(t - 1, c - 3)
                        if c == 6:
                            pick_pairs(t - 1, 2, 4)
                        if c == 7:
                            pick_pairs(t - 1, 7, 8)
                            add_lists(t - 1)
                    if not last:
                        split_x(t + 1)
                        mask_adapters(t + 1)

                def make_turner(part):
                    if part == 0:
                        dve.wait_ge(ck_in, 32)
                        for k in range(KD):
                            nc.vector.tensor_copy(turner[:, k, 0:P], big["ident_f"][:, :]).then_inc(turner_made, 1)
                        nc.vector.memset(lists[:, :], 0.0).then_inc(lists_made, 1)
                        nc.vector.memset(upto[:, :], 0.0).then_inc(turner_made, 1)
                        nc.vector.tensor_copy(number[:, :], ck[:, CK_TOKEN:CK_TOKEN + SUB]).then_inc(number_made, 1)
                    else:
                        dve.wait_ge(w_lo, len(cuts))
                        for n, router in enumerate(parts(W0_WR, W0_WR + KD * E)):
                            nc.vector.tensor_copy(turner[:, :, P + n * E:P + (n + 1) * E],
                                                  router.rearrange("p (k e) -> p k e", e=E)).then_inc(turner_made, 1)

                dve.wait_ge(idx_in, 16)
                dve.wait_ge(big["cst_in"], 48)
                nc.vector.tensor_scalar(mask[:, :], idx, cf[:, 0:1], None, ALU.is_equal).then_inc(mask_made, 1)
                split_weights(0)
                split_x(0)
                split_weights(1)
                dve.wait_ge(mask_made, 1)
                mask_adapters(0)
                over_groups(dve, body)
                g = NG - 1
                mask_down(g)
                split_output(g)
                for part in range(3):
                    route_part(g, part)

                done = [0]

                def step(instruction):
                    instruction.then_inc(index, 1)
                    done[0] += 1
                    dve.wait_ge(index, done[0])

                V = nc.vector
                owner = ck[:, CK_OWNER:CK_OWNER + 2 * E].rearrange("p (m e) -> p m e", e=E)
                prior = ck[:, CK_BEFORE:CK_BEFORE + 2 * E].rearrange("p (m e) -> p m e", e=E)
                step(V.tensor_tensor(owned[:, :, :], owner, upto[:, :].unsqueeze(1).broadcast_to([P, 2, E]), ALU.mult))
                step(V.reduce_sum(count[:, :], owned[:, :, :], X))
                step(V.tensor_scalar(flag[:, :], count[:, :], ck[:, CK_FROM:CK_FROM + 1], None, ALU.is_gt))
                step(V.tensor_copy(flagb[:, :], flag[:, :]))
                step(V.tensor_tensor(flags[:, :, :], prior, flag[:, :].unsqueeze(2).broadcast_to([P, 2, E]), ALU.mult))
                step(V.tensor_tensor(flage[:, :], flag[:, :], ck[:, CK_EXPERT:CK_EXPERT + 2], ALU.mult))
                pick_pairs(g, 0, 2 * SUB)
                add_lists(g)
                dve.wait_ge(sized, 1)
                step(V.tensor_copy(tn[:, :], po[:, 0, 0:2]))
                step(V.tensor_scalar(big["first"][:, :], po[:, 0, E:2 * E], float(P), None, ALU.mult))
                for n in range(2):
                    step(V.tensor_scalar(picke[:, n, :], iota_w[:, 0:NT], tn[:, n:n + 1], flage[:, n:n + 1],
                                         ALU.is_equal, ALU.mult))
                for n in range(2):
                    step(V.tensor_scalar(pick[:, n, :], iota_w[:, 0:NT], tn[:, n:n + 1], flag[:, n:n + 1],
                                         ALU.is_equal, ALU.mult))
                dve.wait_ge(found, 1)
                digits, words = s[:, 1, 0:NT].rearrange("p (i j) -> p i j", j=UNROLL), s[:, 1, NT:NT + TURNS]
                step(V.tensor_tensor(digits, po[:, 0, P:P + NT].rearrange("p (i j) -> p i j", j=UNROLL),
                                     ck[:, CK_POWER:CK_POWER + UNROLL].unsqueeze(1).broadcast_to([P, TURNS, UNROLL]), ALU.mult))
                step(V.reduce_sum(words, digits, X))
                step(V.tensor_copy(big["turn_experts"][:, :], words))
                step(V.tensor_scalar(big["tile_tokens"][:, :], po[:, 0, 2 * P:2 * P + NT], float(T // 2), None, ALU.add))

            @block.gpsimd
            def _(pool):
                def body(t, first, last):
                    for c in range(C0):
                        pool.wait_ge(h_hi, t * C0 + c + 1)
                        nc.gpsimd.tensor_tensor(hl[:, c % RING, :], s[:, c % 2, :], hh[:, c % RING, :],
                                                ALU.subtract).then_inc(h_lo, 1)
                        if not first and c % 2 == 1:
                            split_piece(t, c // 2)

                def split_piece(t, j):
                    n = (t - 1) * PIECES + j
                    pool.wait_ge(piece_in[j % 2], 16 * ((t - 1) * (PIECES // 2) + j // 2 + 1))
                    pool.wait_ge(w_lo, len(cuts))
                    nc.gpsimd.tensor_copy(mh[:, bass.ds(n * PM, PM)], stage[:, j % 2, :]).then_inc(piece_hi, 1)
                    pool.wait_ge(piece_hi, n + 1)
                    nc.gpsimd.tensor_tensor(ml[:, bass.ds(n * PM, PM)], stage[:, j % 2, :], mh[:, bass.ds(n * PM, PM)],
                                            ALU.subtract).then_inc(piece_lo, 1)

                pool.sem_inc(piece_lo, 2)
                over_groups(pool, body)


def phase_2(nc, A, big, signals):
    wh, wl, mh, ml, ident = (big[n] for n in ("wh", "wl", "mh", "ml", "ident_f"))
    RX, R4 = UNROLL, 4
    cf_iota = big["cf"][:, 2:2 + E]
    with ExitStack() as memory:
        m = Mem(nc, memory, signals, "p2")
        sp_passed, dve_passed, pool_passed, pe_passed = (
            m.sem(n) for n in ("sp_passed", "dve_passed", "pool_passed", "pe_passed"))
        tokens = [m.sb(f"tokens{n}", [P, UNROLL // 2], U32) for n in range(2)]
        xg = m.sb("xg", [P, RX, D])
        xh, xl = (big[n][:, :, :].rearrange("p k (n d) -> p (k n) d", d=D) for n in ("xh", "xl"))
        hid = m.sb("hid", [P, R4, 2 * P])
        hh, hl = m.sb("hh", [P, R4, 2 * P], F32R), m.sb("hl", [P, R4, 2 * P], F32R)
        yb = m.sb("yb", [P, R4, D])
        draw = m.sb("draw", [IMR, E * D])
        dwh, dwl = m.sb("dwh", [IMR, E * D], F32R), m.sb("dwl", [IMR, E * D], F32R)
        stage = m.sb("stage", [P, PIECES, P1W])
        own = m.sb("own", [P, 2 * NG * SUB, E])
        start = m.sb("start", [P, 2 * NG * SUB])

        px, pg, ph, py = ([m.pb(f"{n}{i}", [P, G]) for i in range(2)] for n in ("px", "pg", "ph", "py"))

        (x_turned, x_hi, x_lo, gu_done, s_done, hu_done, h_turned, h_hi, h_lo, y_done, y_taken, tokens_copied,
         piece_hi, piece_lo, down_in, down_hi, down_lo, hid_zero, placed) = (m.sem(n) for n in (
             "x_turned x_hi x_lo gu_done s_done hu_done h_turned h_hi h_lo y_done y_taken tokens_copied "
             "piece_hi piece_lo down_in down_hi down_lo hid_zero placed").split())
        piece_in = [m.sem(f"piece_in{n}") for n in range(PIECES)]
        x_in = [m.sem(f"x_in{n}") for n in range(RX)]
        y_stored = [m.sem(f"y_stored{n}") for n in range(R4)]

        def over_turns(eng, body):
            body(0, True, False)
            with eng.Fori(1, TURNS - 1) as i:
                body(i, False, False)
            body(TURNS - 1, False, True)

        def steps(i, first, last):
            for j in range(UNROLL + (2 if last else 0)):
                yield j, i * UNROLL + j

        def runs(j, lag, first, last):
            return not (first and j < lag) and not (last and j - lag >= UNROLL)

        with nc.Block() as block:
            @block.sync
            def _(sp):
                def body(i, first, last):
                    for j, n in steps(i, first, last):
                        if runs(j, 2, first, last):
                            reach_then(sp, y_taken, n - 1, sp_passed)
                            sp.dma_start(A["y"][bass.ds((n - 2) * P, P), :], yb[:, (j - 2) % R4, :]).then_inc(
                                y_stored[(j - 2) % R4], 16)
                        if j % 2 == 1 and j < UNROLL and not last:
                            q = i * PIECES + j // 2
                            reach_then(sp, piece_lo, q + 1, sp_passed)
                            load_piece(q + PIECES, j // 2)

                def load_piece(q, room):
                    sp.dma_start(stage[:, room, :], A["w1"][:, bass.ds(q * P1W, P1W)]).then_inc(piece_in[room], 16)

                sp.dma_start(draw[:, :], A["wd2"]).then_inc(down_in, 16)
                for q in range(PIECES):
                    load_piece(q, q)
                over_turns(sp, body)
                for n in range(R4):
                    sp.wait_ge(y_stored[n], 16 * NT // R4)

            @block.tensor
            def _(pe):
                def turn_x(n, j):
                    pe.wait_ge(x_in[j % RX], 16 * (turn_of[0] + j // UNROLL + 1))
                    reach_then(pe, x_lo, n - 1, pe_passed)
                    for k in range(KD):
                        last = pe.transpose(px[j % 2][:, k * P:(k + 1) * P], xg[:, j % RX, k * P:(k + 1) * P], ident[:, :])
                    last.then_inc(x_turned, 1)

                def gate_up(n, j, expert):
                    pe.wait_ge(x_lo, n + 1)
                    reach(pe, hu_done, n - 1)
                    for k in range(KD):
                        last = mm3(pe, pg[j % 2][:, 0:2 * IM],
                                   (xh[:, j % R4, k * P:(k + 1) * P], xl[:, j % R4, k * P:(k + 1) * P]),
                                   tuple(a[:, bass.ds(expert * BLKM + k * 2 * IM, 2 * IM)] for a in (mh, ml)),
                                   k == 0, k == KD - 1)
                    last.then_inc(gu_done, 1)

                def turn_hidden(n, j):
                    pe.wait_ge(hu_done, n + 1)
                    reach_then(pe, h_lo, n - 1, pe_passed)
                    for k in range(2):
                        last = pe.transpose(ph[j % 2][:, k * P:(k + 1) * P], hid[:, j % R4, k * P:(k + 1) * P], ident[:, :])
                    last.then_inc(h_turned, 1)

                def down(n, j, expert):
                    pe.wait_ge(h_lo, n + 1)
                    reach(pe, y_taken, n - 1)
                    out, s = py[j % 2][:, 0:D], j % R4
                    mm3(pe, out, (hh[:, s, 0:P], hl[:, s, 0:P]),
                        tuple(a[:, bass.ds(expert * BLKM + KD * 2 * IM, D)] for a in (mh, ml)), True, False)
                    mm3(pe, out, (hh[0:IMR, s, P:2 * P], hl[0:IMR, s, P:2 * P]),
                        tuple(a[:, bass.ds(expert * D, D)] for a in (dwh, dwl)), False, True).then_inc(y_done, 1)

                turn_of = [0]

                def body(i, first, last):
                    turn_of[0] = i
                    def word(turn):
                        return nc.tensor.value_load(big["turn_experts"][0:1, bass.ds(turn, 1)],
                                                    min_val=0, max_val=E ** UNROLL - 1)

                    def expert(j):
                        return words[int(j < 0)] // E ** (j % UNROLL) % E

                    words = [word(i), None]
                    for j, n in steps(i, first, last):
                        if runs(j, 0, first, last):
                            gate_up(n, j, expert(j))
                        if runs(j, -2, first, last):
                            turn_x(n + 2, j + 2)
                        if runs(j, 2, first, last):
                            if first and j == 2:
                                pe.wait_ge(down_lo, 1)
                            if not first and j == 0:
                                words[1] = word(i - 1)
                            down(n - 2, j - 2, expert(j - 2))
                        if runs(j, 1, first, last):
                            turn_hidden(n - 1, j - 1)

                turn_x(0, 0)
                turn_x(1, 1)
                pe.wait_ge(hid_zero, 1)
                over_turns(pe, body)

            @block.scalar
            def _(act):
                def split_x(n, j):
                    act.wait_ge(x_turned, n + 1)
                    reach(act, gu_done, n - R4 + 1)
                    nc.scalar.copy(xh[:, j % R4, :], px[j % 2][:, 0:D]).then_inc(x_hi, 1)

                def silu(n, j):
                    act.wait_ge(gu_done, n + 1)
                    reach(act, h_turned, n - R4 + 1)
                    nc.scalar.activation(hid[:, j % R4, 0:IM], pg[j % 2][:, 0:IM], ACT.Silu).then_inc(s_done, 1)

                def split_hidden(n, j):
                    act.wait_ge(h_turned, n + 1)
                    reach(act, y_done, n - R4 + 1)
                    nc.scalar.copy(hh[:, j % R4, :], ph[j % 2][:, 0:2 * P]).then_inc(h_hi, 1)

                def body(i, first, last):
                    for j, n in steps(i, first, last):
                        if runs(j, 0, first, last):
                            silu(n, j)
                        if runs(j, -2, first, last):
                            split_x(n + 2, j + 2)
                        if runs(j, 1, first, last):
                            split_hidden(n - 1, j - 1)

                act.wait_ge(down_in, 16)
                nc.scalar.copy(dwh[:, :], draw[:, :]).then_inc(down_hi, 1)
                split_x(0, 0)
                split_x(1, 1)
                act.wait_ge(hid_zero, 1)
                over_turns(act, body)

            @block.vector
            def _(dve):
                V = nc.vector

                def split_x(n, j):
                    dve.wait_ge(x_hi, n + 1)
                    V.tensor_tensor(xl[:, j % R4, :], px[j % 2][:, 0:D], xh[:, j % R4, :], ALU.subtract).then_inc(x_lo, 1)

                def hidden(n, j):
                    dve.wait_ge(s_done, n + 1)
                    V.tensor_tensor(hid[:, j % R4, 0:IM], hid[:, j % R4, 0:IM], pg[j % 2][:, IM:2 * IM],
                                    ALU.mult).then_inc(hu_done, 1)

                def split_hidden(n, j):
                    dve.wait_ge(h_hi, n + 1)
                    V.tensor_tensor(hl[:, j % R4, :], ph[j % 2][:, 0:2 * P], hh[:, j % R4, :], ALU.subtract).then_inc(h_lo, 1)

                def take_y(n, j, i):
                    dve.wait_ge(y_done, n + 1)
                    uses = i * (UNROLL // R4) + j // R4
                    reach(dve, y_stored[j % R4], 16 * uses)
                    V.tensor_copy(yb[:, j % R4, :], py[j % 2][:, 0:D]).then_inc(y_taken, 1)

                def body(i, first, last):
                    for j, n in steps(i, first, last):
                        if runs(j, 0, first, last):
                            hidden(n, j)
                        if runs(j, -2, first, last):
                            split_x(n + 2, j + 2)
                        if runs(j, 2, first, last):
                            take_y(n - 2, j - 2, i)
                        if runs(j, 1, first, last):
                            split_hidden(n - 1, j - 1)

                V.memset(hid[:, :, IM:2 * P], 0.0).then_inc(hid_zero, 1)
                npairs = 2 * NG * SUB
                flat = {n: big[n][:, :, :].rearrange("p s k -> p (s k)") for n in ("expert", "rank")}
                V.tensor_tensor(own[:, :, :], cf_iota.unsqueeze(1).broadcast_to([P, npairs, E]),
                                flat["expert"].unsqueeze(2).broadcast_to([P, npairs, E]), ALU.is_equal).then_inc(placed, 1)
                dve.wait_ge(placed, 1)
                V.tensor_tensor(own[:, :, :], own[:, :, :], big["first"][:, :].unsqueeze(1).broadcast_to([P, npairs, E]),
                                ALU.mult).then_inc(placed, 1)
                dve.wait_ge(placed, 2)
                V.reduce_sum(start[:, :], own[:, :, :], X).then_inc(placed, 1)
                dve.wait_ge(placed, 3)
                V.tensor_tensor(big["place"][:, :], start[:, :], flat["rank"], ALU.add).then_inc(placed, 1)
                dve.wait_ge(down_hi, 1)
                V.tensor_tensor(dwl[:, :], draw[:, :], dwh[:, :], ALU.subtract).then_inc(down_lo, 1)
                split_x(0, 0)
                split_x(1, 1)
                over_turns(dve, body)

            @block.gpsimd
            def _(pool):
                def split_piece(i, j):
                    n = i * PIECES + j
                    reach_then(pool, piece_in[j], 16 * (i + 1), pool_passed)
                    nc.gpsimd.tensor_copy(wh[:, bass.ds(n * P1W, P1W)], stage[:, j, :]).then_inc(piece_hi, 1)
                    pool.wait_ge(piece_hi, n + 1)
                    nc.gpsimd.tensor_tensor(wl[:, bass.ds(n * P1W, P1W)], stage[:, j, :], wh[:, bass.ds(n * P1W, P1W)],
                                            ALU.subtract).then_inc(piece_lo, 1)

                def body(i, first, last):
                    for j in range(UNROLL):
                        half, place = divmod(j, UNROLL // 2)
                        if place == 0:
                            if not first:
                                for k in range(j, j + UNROLL // 2):
                                    reach_then(pool, x_in[k], 16 * i, pool_passed)
                            nc.gpsimd.tensor_copy(tokens[half][:, :], big["tile_tokens"][
                                :, bass.ds(i * UNROLL + j, UNROLL // 2)]).then_inc(tokens_copied, 1)
                        reach(pool, x_turned, (i - 1) * UNROLL + j + 1 if not first else 0)
                        reach_then(pool, tokens_copied, 2 * i + half + 1, pool_passed)
                        nc.gpsimd.indirect_dma_start(xg[:, j, :], None, A["h"], bass.IndirectOffsetOnAxis(
                            ap=tokens[half][:, place:place + 1], axis=0)).then_inc(x_in[j], 16)
                        if j % 2 == 1:
                            split_piece(i, j // 2)

                over_turns(pool, body)


EVENTS = [(0, 0)] + [e for c in range(1, C1) for e in ((c, 0), (c - 1, 1))] + [(C1 - 1, 1)]
NE = len(EVENTS)
AT = {e: n for n, e in enumerate(EVENTS)}


def phase_3(nc, A, big, signals):
    wh, wl, cf, ident = (big[n] for n in ("wh", "wl", "cf", "ident"))
    iota = cf[:, 2:2 + SUB * E].rearrange("p (s e) -> p s e", e=E)
    ident_f = big["ident_f"][0:2 * E, 0:2 * E]
    with ExitStack() as memory:
        m = Mem(nc, memory, signals, "p3")
        sp_passed, dve_passed, pe_passed, pool_passed = (
            m.sem(n) for n in ("sp_passed", "dve_passed", "pe_passed", "pool_passed"))
        xh, xl = big["xh"], big["xl"]
        yg = big["xraw"][:, :, :].rearrange("p b (k d) -> p b k d", d=D)
        xc = m.sb("xc", [P, SUB, D])
        places = m.sb("places", [P, 2 * SUB], U32)
        xah, xal = m.sb("xah", [P, G], F32R), m.sb("xal", [P, G], F32R)
        yh, yl = m.sb("yh", [P, 2, KD, G], F32R), m.sb("yl", [P, 2, KD, G], F32R)
        ua = m.sb("ua", [P, 2, G])
        um = m.sb("um", [P, 2, G])
        xam = um[:, 0, :]
        uh, ul = m.sb("uh", [P, 4, G], F32R), m.sb("ul", [P, 4, G], F32R)
        mk = m.sb("mk", [P, 2, 3, G], BF16)
        wv = m.sb("wv", [P, 2, 2, G])
        s = m.sb("s", [P, 2, 2, G])
        ch, cl = m.sb("ch", [P, 2, 2, G], F32R), m.sb("cl", [P, 2, 2, G], F32R)
        mx = m.sb("mx", [P, 2, G])
        mh, ml = m.sb("mh", [P, C1, G], F32R), m.sb("ml", [P, C1, G], F32R)
        ta = um
        th, tl = xah, xal
        yo = m.sb("yo", [P, SUB, D])
        mask = m.sb("mask", [P, B])
        idx = yo[:, 0, 0:B].bitcast(I32)
        vt = m.sb("vt", [P, SUB, S])
        vr = m.sb("vr", [P, SUB * S])
        v8 = m.sb("v8", [P, SUB, 8])
        i8 = m.sb("i8", [P, SUB, 8], U32)
        if8 = m.sb("if8", [P, SUB, 2])
        st = m.sb("st", [P, SUB, 3])
        c22 = m.sb("c22", [P, SUB, NC1], BF16)
        rest = m.sb("rest", [P, SUB, 2])
        lg = m.sb("lg", [P, SUB, E])
        gw = m.sb("gw", [P, KD, 2 * E], F32R)
        lT = xam[0:2 * E, :]
        cT = m.sb("cT", [NC1, G], BF16)
        sel = m.sb("sel", [NC1, N_SEL1 * P], BF16)
        tiles = (vt, vr, vr, vt, v8, i8, if8, st, c22, rest, lg)

        pair = [[m.pb(f"pair{i}{j}", [P, G]) for j in range(2)] for i in range(2)]
        pa = m.pb("pa", [P, 2, G])
        pf = m.pb("pf", [P, 2, G])
        logits = pf[:, 1, 0:SUB * 2 * E].rearrange("p (s e) -> p s e", e=2 * E)
        turned = pf[:, 0, :].bitcast(BF16)[0:NC1, 0:G]

        (x_in, x_hi, x_lo, idx_in, mask_made, xa_done, xa_masked, xa_hi, xa_lo, y_done, y_hi, y_lo,
         logits_done, route, e_done, ua_done, ua_copied, turned_done, turned_copied, bc_done, bc_copied, um_done,
         u_hi, u_lo, p_done, s_done, m_done, c_done, c_hi, c_lo, acc_done, mix_done, mix_hi, mix_lo, down_done,
         t_masked, t_done, t_hi, t_lo, out_done, res_in, added, stored, prepared, lt_done, lt_copied,
         rows_in, places_made, weighed, combined, x1_stored, x_turned) = (m.sem(n) for n in (
             "x_in x_hi x_lo idx_in mask_made xa_done xa_masked xa_hi xa_lo y_done y_hi y_lo "
             "logits_done route e_done ua_done ua_copied turned_done turned_copied bc_done bc_copied um_done "
             "u_hi u_lo p_done s_done m_done c_done c_hi c_lo acc_done mix_done mix_hi mix_lo down_done "
             "t_masked t_done t_hi t_lo out_done res_in added stored "
             "prepared lt_done lt_copied "
             "rows_in places_made weighed combined x1_stored x_turned").split())

        y_in = [m.sem(f"y_in{n}") for n in range(2)]

        x_v, x1_v, out_v = (A[n].rearrange("(b p) d -> p b d", p=P) for n in ("x", "x1", "out"))

        def w(o, n=P, c=0):
            return wh[r(c), o:o + n], wl[r(c), o:o + n]

        def r(c):
            return slice(0, min(P, H1 - c * P))

        def up_gate(c):
            if c == C1 - 1:
                return pair[c % 2][0][0:HALF, :], pair[c % 2][0][HALF:P, :]
            return pair[c % 2][0][:, :], pair[c % 2][1][:, :]

        def x(k):
            return xh[:, k, :], xl[:, k, :]

        def of_group(t):
            return bass.ds(t * SUB, SUB)

        def over_pairs_ahead(eng, body):
            body(0, 0, True, False, True)
            with eng.Fori(0, NG // 2 - 2) as i:
                body(i * 2 + 1, 1, False, False, True)
                body(i * 2 + 2, 0, False, False, True)
            body(NG - 3, 1, False, False, True)
            body(NG - 2, 0, False, False, False)
            body(NG - 1, 1, False, True, False)

        def event(t, c, slot):
            if c < 0:
                return (t - 1) * NE + AT[(c + C1, slot)] + 1
            return t * NE + AT[(c, slot)] + 1

        BC = [(0, 1), (1, 0), (2, 1), (3, 1), (4, 1)]

        with nc.Block() as block:
            @block.sync
            def _(sp):
                def load(g):
                    reach_then(sp, x_turned, g, sp_passed)
                    reach_then(sp, x1_stored, 16 * g, sp_passed)
                    sp.dma_start(xc[:, :, :], x_v[:, of_group(g), :]).then_inc(rows_in, 16)

                def store_x1(g):
                    reach_then(sp, combined, SUB * (g + 1), sp_passed)
                    sp.dma_start(x1_v[:, of_group(g), :], xc[:, :, :]).then_inc(x1_stored, 16)

                def store(t):
                    reach_then(sp, added, t + 1, sp_passed)
                    sp.dma_start(out_v[:, of_group(t), :], yo[:, :, :]).then_inc(stored, 16)

                def body(t, ahead):
                    if isinstance(t, int) and t == 0:
                        sp.wait_ge(mask_made, 1)
                    else:
                        store(t - 1)
                        reach_then(sp, stored, 16 * t, sp_passed)
                    reach_then(sp, x1_stored, 16 * (t + 1), sp_passed)
                    sp.dma_start(yo[:, :, :], x1_v[:, of_group(t), :]).then_inc(res_in, 16)
                    if ahead:
                        load(t + 2)
                        store_x1(t + 2)

                load(0)
                sp.dma_start(idx, A["idx1"].partition_broadcast(P)).then_inc(idx_in, 16)
                sp.dma_start(sel[:, :], A["sel_1"]).then_inc(idx_in, 16)
                for g in range(2):
                    if g:
                        load(g)
                    store_x1(g)
                body(0, True)
                with sp.Fori(1, NG - 2) as t:
                    body(t, True)
                body(NG - 2, False)
                body(NG - 1, False)
                store(NG - 1)
                sp.wait_ge(x1_stored, 16 * NG)
                sp.wait_ge(stored, 16 * NG)

            @block.tensor
            def _(pe):
                def turn_x(g):
                    reach(pe, added, g - 1)
                    reach_then(pe, combined, SUB * (g + 1), pe_passed)
                    for k in range(KD):
                        for b in range(SUB):
                            last = pe.transpose(pf[:, k, b * P:(b + 1) * P], xc[:, b, k * P:(k + 1) * P], big["ident_f"][:, :])
                    last.then_inc(x_turned, 1)

                def adapters(g):
                    pe.wait_ge(x_lo, g + 1)
                    for k in range(KD):
                        last = mm3(pe, pf[:, 0, :], w(W1_A + k * P), x(k), k == 0, k == KD - 1)
                    last.then_inc(xa_done, 1)

                def project(g):
                    pe.wait_ge(xa_lo, g + 1)
                    for o in range(KD):
                        for k in range(KD):
                            mm3(pe, pf[:, o, :], w(W1_W + k * D + o * P), x(k), k == 0, False)
                        last = mm3(pe, pf[:, o, :], w(W1_B + o * P), (xah[:, :], xal[:, :]), False, True)
                    last.then_inc(y_done, 1)

                def prepare_c(g, q):
                    pe.wait_ge(y_lo, g + 1)
                    if isinstance(g, int) and g == 0:
                        pe.wait_ge(prepared, 3)
                    for k in range(KD):
                        pe.matmul(pf[0:2 * E, 1, :], gw[:, k, :], yh[:, q, k, :], start=k == 0, stop=False,
                                  skip_group_check=True)
                        last = pe.matmul(pf[0:E, 1, :], gw[:, k, 0:E], yl[:, q, k, :], start=False, stop=k == KD - 1,
                                         skip_group_check=True)
                    last.then_inc(lt_done, 1)
                    for k in range(KD):
                        last = mm3(pe, pf[:, 0, :], w(W1_UA + k * P), (yh[:, q, k, :], yl[:, q, k, :]), k == 0, k == KD - 1)
                    last.then_inc(ua_done, 1)
                    reach_then(pe, lt_copied, g + 1, pe_passed)
                    for b in range(SUB):
                        last = pe.transpose(logits[:, b, :], lT[:, b * P:(b + 1) * P], ident_f)
                    last.then_inc(logits_done, 1)

                def prepare_ag(g, q):
                    pe.wait_ge(route, g * ROUTE1 + 2)
                    for k in range(KD):
                        last = mm3(pe, pf[:, 1, :], w(W1_GA + k * P), (yh[:, q, k, :], yl[:, q, k, :]), k == 0, k == KD - 1)
                    last.then_inc(ua_done, 1)

                def turn(g):
                    pe.wait_ge(route, (g + 1) * ROUTE1)
                    pe.wait_ge(ua_copied, 2 * g + 1)
                    for b in range(SUB):
                        last = pe.transpose(turned[:, b * P:(b + 1) * P], c22[:, b, :], ident[:, :])
                    last.then_inc(turned_done, 1)

                def spread(g, n):
                    pe.wait_ge(turned_copied, g + 1)
                    if n == 0:
                        pe.wait_ge(ua_copied, 2 * g + 2)
                    elif n > 1:
                        pe.wait_ge(bc_copied, g * N_SEL1 + max(i for i in range(n) if BC[i][1] == BC[n][1]) + 1)
                    i, bank = BC[n]
                    pe.matmul(pf[:, bank, :], sel[:, i * P:(i + 1) * P], cT[:, :],
                              start=True, stop=True).then_inc(bc_done, 1)

                def main(t, c, q):
                    if c < 2:
                        reach(pe, m_done, event(t, c - 2, 1) if not (isinstance(t, int) and t == 0) else 0)
                    else:
                        pe.wait_ge(m_done, event(t, c - 2, 1))
                    o = W1_BLK + c * BLK1
                    for j in range(1 if c == C1 - 1 else 2):
                        for k in range(KD):
                            mm3(pe, pair[c % 2][j][:, :], w(o + (j * KD + k) * P), (yh[:, q, k, :], yl[:, q, k, :]), k == 0, False)
                    if c == 0:
                        pe.wait_ge(u_lo, 4 * (t + 1))
                    for j in range(2):
                        last = mm3(pe, pair[c % 2][0 if c == C1 - 1 else j][:, :], w(o + 2 * D + j * P), (uh[:, 2 * j, :], ul[:, 2 * j, :]), False, True)
                    last.then_inc(p_done, 1)

                def delta(t, c):
                    pe.wait_ge(m_done, event(t, c, 0))
                    o = W1_BLK + c * BLK1 + 2 * D
                    for j in range(2):
                        last = mm3(pe, pair[c % 2][0 if c == C1 - 1 else j][:, :], w(o + j * P), (uh[:, 2 * j + 1, :], ul[:, 2 * j + 1, :]), False, True)
                    last.then_inc(p_done, 1)

                def accumulate(t, c):
                    pe.wait_ge(c_lo, event(t, c, 1))
                    if c == 0:
                        reach(pe, t_masked, 2 * t)
                    for i in range(2):
                        last = mm3(pe, pa[:, i, :], w(W1_BLK + c * BLK1 + 2 * D + 2 * P, P, c), (ch[r(c), c % 2, i, :], cl[r(c), c % 2, i, :]),
                                   c == 0, c == C1 - 1)
                    last.then_inc(acc_done, 1)

                def down(t, last_group, part):
                    def out(b):
                        return pf[:, b // 2, (b % 2) * D:(b % 2 + 1) * D]

                    def tokens(a, b):
                        return a[:, b * P:(b + 1) * P]

                    def block(o, c):
                        pe.wait_ge(mix_lo, t * C1 + c + 1)
                        for b in (2 * o, 2 * o + 1):
                            last = mm3(pe, out(b), (tokens(mh[r(c), c, :], b), tokens(ml[r(c), c, :], b)),
                                       w(W1_BLK + c * BLK1 + 2 * D + 3 * P, D, c), c == 0 and b % 2 == 0, False)
                        return last

                    if part == 0:
                        if not last_group:
                            pe.wait_ge(bc_copied, N_SEL1 * (t + 1) + 2)
                        block(0, 0)
                        block(0, 1)
                        return
                    for c in range(2, C1 - 1):
                        block(0, c)
                    accumulate(t, C1 - 1)
                    if not last_group:
                        pe.wait_ge(bc_copied, N_SEL1 * (t + 2))
                    for c in range(C1 - 1):
                        block(1, c)
                    for o in range(KD):
                        last = block(o, C1 - 1)
                    last.then_inc(down_done, 1)
                    pe.wait_ge(t_lo, t + 1)
                    for b in range(SUB):
                        last = mm3(pe, out(b), (tokens(th, b), tokens(tl, b)), w(W1_DB, D), False, True)
                    last.then_inc(out_done, 1)

                def body(t, q, first, last):
                    more = not last
                    g, other = t + 1, 1 - q
                    main(t, 0, q)
                    if more:
                        turn_x(g)
                    main(t, 1, q)
                    delta(t, 0)
                    if more:
                        adapters(g)
                    main(t, 2, q)
                    delta(t, 1)
                    accumulate(t, 0)
                    if more:
                        project(g)
                    main(t, 3, q)
                    if more:
                        prepare_c(g, other)
                    delta(t, 2)
                    accumulate(t, 1)
                    main(t, 4, q)
                    delta(t, 3)
                    accumulate(t, 2)
                    if more:
                        prepare_ag(g, other)
                    main(t, 5, q)
                    if more:
                        turn(g)
                    delta(t, 4)
                    if more:
                        spread(g, 0)
                    accumulate(t, 3)
                    if more:
                        spread(g, 1)
                    delta(t, 5)
                    if more:
                        spread(g, 2)
                    down(t, last, 0)
                    if more:
                        spread(g, 3)
                    accumulate(t, 4)
                    if more:
                        spread(g, 4)
                    down(t, last, 1)

                turn_x(0)
                adapters(0)
                project(0)
                prepare_c(0, 0)
                prepare_ag(0, 0)
                turn(0)
                pe.wait_ge(idx_in, 32)
                for n in range(N_SEL1):
                    spread(0, n)
                over_pairs(pe, body)

            @block.scalar
            def _(act):
                def split_x(g):
                    act.wait_ge(x_turned, g + 1)
                    reach(act, y_done, g)
                    nc.scalar.copy(xh[:, :, :], pf[:, :, :]).then_inc(x_hi, 1)

                def split_adapters(g):
                    act.wait_ge(xa_masked, g + 1)
                    reach(act, out_done, g - 1)
                    nc.scalar.copy(xah[:, :], xam[:, :]).then_inc(xa_hi, 1)

                def split_y(g, q):
                    act.wait_ge(y_done, g + 1)
                    nc.scalar.copy(yh[:, q, :, :], pf[:, :, :]).then_inc(y_hi, 1)

                def take_logits(g):
                    act.wait_ge(lt_done, g + 1)
                    act.wait_ge(xa_lo, g + 1)
                    nc.scalar.copy(lT, pf[0:2 * E, 1, :]).then_inc(lt_copied, 1)

                def take_ua(g, j):
                    act.wait_ge(ua_done, 2 * g + j + 1)
                    reach(act, um_done, 4 * g)
                    nc.scalar.copy(ua[:, j, :], pf[:, j, :]).then_inc(ua_copied, 1)

                def route_exp(g):
                    act.wait_ge(route, g * ROUTE1 + EXP1)
                    nc.scalar.activation(vr[:, :], vr[:, :], ACT.Exp).then_inc(e_done, 1)

                def take_turned(g):
                    act.wait_ge(turned_done, g + 1)
                    nc.scalar.copy(cT[:, :], turned).then_inc(turned_copied, 1)

                def take_spread(g, n, q):
                    i, bank = BC[n]
                    act.wait_ge(bc_done, g * N_SEL1 + n + 1)
                    to = mk[:, q, i, :] if i < 3 else wv[:, q, i - 3, :]
                    nc.scalar.copy(to, pf[:, bank, :]).then_inc(bc_copied, 1)

                def split_u(g, a, b):
                    for n in range(a, b):
                        act.wait_ge(um_done, 4 * g + n + 1)
                        nc.scalar.copy(uh[:, n, :], um[:, n % 2, :]).then_inc(u_hi, 1)

                def silu(t, c, i):
                    act.wait_ge(p_done, event(t, c, i))
                    if not (isinstance(t, int) and t == 0 and c < 2):
                        act.wait_ge(mix_done, t * C1 + c - 1)
                        act.wait_ge(c_lo, event(t, c - 2, i))
                    nc.scalar.activation(s[r(c), c % 2, i, :], up_gate(c)[0], ACT.Silu).then_inc(s_done, 1)

                def split_c(t, c, i):
                    act.wait_ge(c_done, event(t, c, i))
                    reach(act, acc_done, t * C1 + c - 1)
                    nc.scalar.copy(ch[r(c), c % 2, i, :], s[r(c), c % 2, i, :]).then_inc(c_hi, 1)

                def split_mix(t, c):
                    act.wait_ge(mix_done, t * C1 + c + 1)
                    reach(act, down_done, t)
                    nc.scalar.copy(mh[r(c), c, :], mx[r(c), c % 2, :]).then_inc(mix_hi, 1)

                def split_t(t, more):
                    act.wait_ge(t_done, t + 1)
                    act.wait_ge(y_done, t + 2 if more else NG)
                    nc.scalar.copy(th[:, :], ta[:, 0, :]).then_inc(t_hi, 1)

                def body(t, q, first, last):
                    more = not last
                    g, other = t + 1, 1 - q
                    for n, (c, i) in enumerate(EVENTS):
                        silu(t, c, i)
                        if more and n == 10:
                            take_spread(g, 0, other)
                        if more and n == NE - 1:
                            take_spread(g, 2, other)
                            split_u(g, 0, 2)
                            take_spread(g, 3, other)
                        if n >= 1 and EVENTS[n - 1][1] == 0:
                            split_c(t, *EVENTS[n - 1])
                        if more and n == 10:
                            take_spread(g, 1, other)
                        if i == 1:
                            split_c(t, c, i)
                            if c < C1 - 1:
                                split_mix(t, c)
                        if not more:
                            continue
                        if n == 0:
                            split_x(g)
                        if n == 2:
                            split_adapters(g)
                        if n == 4:
                            split_y(g, other)
                        if n == 5:
                            take_logits(g)
                        if n == 6:
                            take_ua(g, 0)
                            route_exp(g)
                        if n == 8:
                            take_ua(g, 1)
                        if n == 9:
                            take_turned(g)
                    if more:
                        take_spread(g, 4, other)
                        split_u(g, 2, 4)
                    split_mix(t, C1 - 1)
                    split_t(t, more)

                split_x(0)
                split_adapters(0)
                split_y(0, 0)
                take_logits(0)
                take_ua(0, 0)
                route_exp(0)
                take_ua(0, 1)
                take_turned(0)
                for n in range(N_SEL1):
                    take_spread(0, n, 0)
                split_u(0, 0, 4)
                over_pairs(act, body)

            @block.vector
            def _(dve):
                V = nc.vector

                def combine(g, b):
                    if b == 0:
                        dve.wait_ge(rows_in, 16 * (g + 1))
                    dve.wait_ge(y_in[b % 2], 16 * (4 * g + 2 * (b // 2) + 2))
                    for k in range(2):
                        if k:
                            dve.wait_ge(weighed, g * SUB + b + 1)
                        V.scalar_tensor_tensor(xc[:, b, :], yg[:, b % 2, k, :], big["share"][:, g * SUB + b, k:k + 1]
                                               if isinstance(g, int) else big["share"][:, bass.ds(g * SUB + b, 1), k],
                                               xc[:, b, :], ALU.mult, ALU.add).then_inc((weighed, combined)[k], 1)

                def split_x(g):
                    dve.wait_ge(x_hi, g + 1)
                    V.tensor_tensor(xl[:, :, :], pf[:, :, :], xh[:, :, :], ALU.subtract).then_inc(x_lo, 1)

                def mask_adapters(g):
                    dve.wait_ge(xa_done, g + 1)
                    reach(dve, u_lo, 4 * g)
                    reach(dve, t_lo, g - 1)
                    reach(dve, out_done, g - 1)
                    V.tensor_tensor(by_batch(xam[:, :]), by_batch(pf[:, 0, :]), over_tokens(mask, g),
                                    ALU.mult).then_inc(xa_masked, 1)
                    dve.wait_ge(xa_hi, g + 1)
                    V.tensor_tensor(xal[:, :], xam[:, :], xah[:, :], ALU.subtract).then_inc(xa_lo, 1)

                def split_y(g, q):
                    dve.wait_ge(y_hi, g + 1)
                    V.tensor_tensor(yl[:, q, :, :], pf[:, :, :], yh[:, q, :, :], ALU.subtract).then_inc(y_lo, 1)

                def route_part(g, part):
                    steps = Route(g, dve_passed, route, logits, iota, tiles)
                    if part == 0:
                        reach_then(dve, logits_done, g + 1, dve_passed)
                        route1_steps(V, steps, 0, 2 + SUB)
                    elif part == 1:
                        route1_steps(V, steps, 2 + SUB, EXP1)
                        reach_then(dve, turned_done, g, dve_passed)
                        route1_steps(V, steps, EXP1, MASKS1)
                        dve.wait_ge(e_done, g + 1)
                        route1_steps(V, steps, MASKS1, CUT1)
                    else:
                        route1_steps(V, steps, CUT1, ROUTE1)

                def mask_u(g, q, a, b):
                    dve.wait_ge(ua_copied, 2 * (g + 1))
                    dve.wait_ge(logits_done, g + 1)
                    reach(dve, t_lo, g - 1 if a == 0 else 0)
                    for n in range(a, b):
                        if n < 2:
                            dve.wait_ge(bc_copied, g * N_SEL1 + n + 1)
                        reach(dve, u_lo, 4 * g + n - 1)
                        V.tensor_tensor(um[:, n % 2, :], ua[:, n // 2, :], mk[:, q, n % 2, :], ALU.mult).then_inc(um_done, 1)
                    if b == 4:
                        dve.wait_ge(u_hi, 4 * g + b)
                        V.tensor_tensor(ul[:, 3, :], um[:, 1, :], uh[:, 3, :], ALU.subtract).then_inc(u_lo, 1)

                def hidden(t, c, i, q):
                    dve.wait_ge(s_done, event(t, c, i))
                    sv = s[r(c), c % 2, i, :]
                    V.tensor_tensor(sv, sv, up_gate(c)[1], ALU.mult).then_inc(m_done, 1)
                    dve.wait_ge(m_done, event(t, c, i))
                    V.tensor_tensor(sv, sv, wv[r(c), q, i, :], ALU.mult).then_inc(c_done, 1)
                    if i == 1:
                        dve.wait_ge(c_done, event(t, c, i))
                        reach(dve, mix_lo, t * C1 + c - 1)
                        V.tensor_tensor(mx[r(c), c % 2, :], s[r(c), c % 2, 0, :], s[r(c), c % 2, 1, :], ALU.add).then_inc(mix_done, 1)

                def tail(t, q, more):
                    dve.wait_ge(acc_done, (t + 1) * C1)
                    reach(dve, t_lo, t)
                    dve.wait_ge(u_lo, 4 * (t + 2) if more else 4 * NG)
                    V.tensor_tensor(ta[:, 0, :], pa[:, 0, :], mk[:, q, 0, :], ALU.mult).then_inc(t_masked, 1)
                    V.tensor_tensor(ta[:, 1, :], pa[:, 1, :], mk[:, q, 2, :], ALU.mult).then_inc(t_masked, 1)
                    dve.wait_ge(t_masked, 2 * (t + 1))
                    V.tensor_tensor(ta[:, 0, :], ta[:, 0, :], ta[:, 1, :], ALU.add).then_inc(t_done, 1)
                    dve.wait_ge(t_hi, t + 1)
                    V.tensor_tensor(tl[:, :], ta[:, 0, :], th[:, :], ALU.subtract).then_inc(t_lo, 1)

                def add(t):
                    dve.wait_ge(out_done, t + 1)
                    dve.wait_ge(res_in, 16 * (t + 1))
                    V.tensor_tensor(yo[:, :, :], yo[:, :, :], pf[:, :, :].rearrange("p k (h d) -> p (k h) d", d=D), ALU.add).then_inc(added, 1)

                def body(t, q, first, last, ahead):
                    more = not last
                    g, other = t + 1, 1 - q
                    if not first:
                        add(t - 1)
                    for n, (c, i) in enumerate(EVENTS):
                        if more and n == NE - 1:
                            mask_u(g, other, 0, 2)
                        hidden(t, c, i, q)
                        if ahead and n == 4:
                            combine(t + 2, 0)
                        if not more:
                            continue
                        if n == 0:
                            split_x(g)
                        if n == 2:
                            mask_adapters(g)
                        if n == 4:
                            split_y(g, other)
                        if n == 5 or n == 6:
                            route_part(g, n - 5)
                        if n == 8:
                            route_part(g, 2)
                            if ahead:
                                combine(t + 2, 1)
                    if more:
                        mask_u(g, other, 2, 4)
                    tail(t, q, more)
                    if ahead:
                        combine(t + 2, 2)
                        combine(t + 2, 3)

                V.memset(vt[:, :, :], 0.0).then_inc(prepared, 1)
                for n, part in enumerate((wh, wl)):
                    V.tensor_copy(gw[:, :, n * E:(n + 1) * E],
                                  part[:, W1_GW:W1_GW + KD * E].rearrange("p (k e) -> p k e", e=E)).then_inc(prepared, 1)
                for b in range(SUB):
                    combine(0, b)
                dve.wait_ge(idx_in, 32)
                V.tensor_scalar(mask[:, :], idx, cf[:, 0:1], cf[:, 1:2], ALU.is_equal, ALU.mult).then_inc(mask_made, 1)
                split_x(0)
                dve.wait_ge(mask_made, 1)
                mask_adapters(0)
                split_y(0, 0)
                dve.wait_ge(prepared, 3)
                for part in range(3):
                    route_part(0, part)
                for b in range(SUB):
                    combine(1, b)
                mask_u(0, 0, 0, 4)
                over_pairs_ahead(dve, body)
                add(NG - 1)

            @block.gpsimd
            def _(pool):
                GATHER = (3, 5, 6, 9)
                def sub(out, a, b, sem):
                    nc.gpsimd.tensor_tensor(out, a, b, ALU.subtract).then_inc(sem, 1)

                def split_u(g, a, b):
                    for n in range(a, b):
                        pool.wait_ge(u_hi, 4 * g + n + 1)
                        sub(ul[:, n, :], um[:, n % 2, :], uh[:, n, :], u_lo)

                def split_mix(t, c):
                    pool.wait_ge(mix_hi, t * C1 + c + 1)
                    sub(ml[r(c), c, :], mx[r(c), c % 2, :], mh[r(c), c, :], mix_lo)

                def gather(g, b):
                    if b == 0:
                        for n in range(2):
                            reach_then(pool, y_in[n], 16 * 4 * g, pool_passed)
                        nc.gpsimd.tensor_copy(places[:, :], big["place"][:, bass.ds(g * 2 * SUB, 2 * SUB)]).then_inc(places_made, 1)
                    for k in range(2):
                        reach(pool, combined, g * SUB + b - 1)
                        reach_then(pool, places_made, g + 1, pool_passed)
                        nc.gpsimd.indirect_dma_start(yg[:, b % 2, k, :], None, A["y"], bass.IndirectOffsetOnAxis(
                            ap=places[:, 2 * b + k:2 * b + k + 1], axis=0)).then_inc(y_in[b % 2], 16)

                def body(t, q, first, last, ahead):
                    for n, (c, i) in enumerate(EVENTS):
                        if ahead and n in GATHER:
                            gather(t + 2, GATHER.index(n))
                        if not last and n == NE - 1:
                            split_u(t + 1, 0, 1)
                        pool.wait_ge(c_hi, event(t, c, i))
                        sub(cl[r(c), c % 2, i, :], s[r(c), c % 2, i, :], ch[r(c), c % 2, i, :], c_lo)
                        if not last and n == NE - 1:
                            split_u(t + 1, 1, 3)
                        if i == 1:
                            split_mix(t, c)

                for g in range(2):
                    for b in range(SUB):
                        gather(g, b)
                split_u(0, 0, 3)
                over_pairs_ahead(pool, body)


def program(nc, A):
    with ExitStack() as ctx:
        signals = ctx.enter_context(ExitStack())
        m = Mem(nc, ctx, signals, "w")
        big = {"wh": m.sb("wh", [P, SPLIT], F32R), "wl": m.sb("wl", [P, SPLIT], F32R),
               "cf": m.sb("cf", [P, 2 + SUB * E]), "ident": m.sb("ident", [P, P], BF16),
               "ident_f": m.sb("ident_f", [P, P]),
               **{n: m.sb(n, [P, NG * SUB, 2]) for n in ("expert", "rank", "share")},
               "place": m.sb("place", [P, NG * SUB * 2], U32),
               "first": m.sb("first", [P, E]),
               "turn_experts": m.sb("turn_experts", [P, TURNS], I32),
               "tile_tokens": m.sb("tile_tokens", [P, NT], U32),
               "xraw": m.sb("xraw", [P, KD, G]),
               "xh": m.sb("xh", [P, KD, G], F32R), "xl": m.sb("xl", [P, KD, G], F32R),
               "cst_in": m.sem("cst_in")}
        with nc.Block() as block:
            @block.sync
            def _(sp):
                sp.dma_start(big["cf"][:, :], A["cf"]).then_inc(big["cst_in"], 16)
                sp.dma_start(big["ident"][:, :], A["ident"]).then_inc(big["cst_in"], 16)
                sp.dma_start(big["ident_f"][:, :], A["ident_f"]).then_inc(big["cst_in"], 16)
                sp.wait_ge(big["cst_in"], 48)
        with ExitStack() as experts:
            e = Mem(nc, experts, signals, "m")
            big["xwh"] = e.sb("xwh", [P, W0_COLS - SPLIT], F32R)
            big["xwl"] = e.sb("xwl", [P, W0_COLS - SPLIT], F32R)
            with nc.sbuf_tensor("w_raw", [P, W0_COLS], F32) as raw:
                big["raw"] = raw
            big["mh"] = e.sb("mh", [P, WM_PAD], F32R)
            big["ml"] = e.sb("ml", [P, WM_PAD], F32R)
            phase_1(nc, A, big, signals)
            phase_2(nc, A, big, signals)
        phase_3(nc, A, big, signals)


def _rows(a):
    k = a.shape[0] // P
    return np.ascontiguousarray(a.reshape(k, P, a.shape[1]).transpose(1, 0, 2)).reshape(P, -1)


def _cols(parts, width):
    out = np.concatenate(parts, axis=1)
    return np.ascontiguousarray(np.concatenate([out, np.zeros((P, width - out.shape[1]), np.float32)], axis=1))


def _a_cols(a):
    return a.transpose(1, 0, 2).reshape(a.shape[1], E * R)


def _b_rows(a):
    return a.reshape(E * R, a.shape[2])


def _pack_0(v):
    parts = [_rows(_a_cols(v["L0_cond_Ag"])), _rows(_a_cols(v["L0_cond_Au"]))]
    ad = _a_cols(v["L0_cond_Ad"])
    for c in range(C0):
        b = slice(c * P, (c + 1) * P)
        parts += [_rows(v["L0_cond_Wg"][:, b]), _rows(v["L0_cond_Wu"][:, b]), _b_rows(v["L0_cond_Bg"])[:, b],
                  _b_rows(v["L0_cond_Bu"])[:, b], v["L0_cond_Wd"][b], ad[b]]
    parts += [_b_rows(v["L0_cond_Bd"]), _rows(v["L0_ffn_Wr"])]
    return _cols(parts, W0_COLS)


def _pack_m(v):
    parts = []
    for e in range(E):
        parts += [_rows(np.concatenate([v["L0_ffn_Wg"][e], v["L0_ffn_Wu"][e]], axis=1)), v["L0_ffn_Wd"][e, :P]]
    return _cols(parts, WM_PAD)


def _pack_1(v):
    def wide(a):
        return np.concatenate([a, np.zeros((a.shape[0], C1 * P - H1), np.float32)], axis=1)

    up, gate = wide(v["L1_ffn_w_up"].T), wide(v["L1_ffn_w_gate"].T)
    ub, gb = (wide(_b_rows(v[n].transpose(0, 2, 1))) for n in ("L1_ffn_up_B", "L1_ffn_gate_B"))
    da = wide(v["L1_ffn_down_A"].reshape(E * R, H1)).T
    wd = wide(v["L1_ffn_w_down"]).T
    parts = [_rows(v["L1_cond_A"].reshape(E * R, D).T), _rows(v["L1_cond_W"].T),
             _b_rows(v["L1_cond_Bm"].transpose(0, 2, 1)), _rows(v["L1_ffn_gate_w"].T),
             _rows(v["L1_ffn_up_A"].reshape(E * R, D).T), _rows(v["L1_ffn_gate_A"].reshape(E * R, D).T)]
    for c in range(C1):
        b = slice(c * P, (c + 1) * P)
        if c < C1 - 1:
            parts += [_rows(up[:, b]), _rows(gate[:, b]), ub[:, b], gb[:, b], da[b], wd[b]]
        else:
            a, n = slice(c * P, H1), np.zeros((P, HALF), np.float32)
            parts += [_rows(np.concatenate([up[:, a], gate[:, a]], axis=1)), np.zeros((P, D), np.float32),
                      ub[:, a], n, n, gb[:, a], da[b], wd[b]]
    parts += [_b_rows(v["L1_ffn_down_B"].transpose(0, 2, 1))]
    return _cols(parts, W1_PAD)


def _constants(scalings):
    row = np.arange(P)
    cf = np.concatenate([(row // R).astype(np.float32)[:, None], np.repeat(scalings, R)[:, None],
                         np.tile(np.arange(E, dtype=np.float32), (P, SUB))], axis=1).astype(np.float32)
    sel_1 = np.zeros((NC1, N_SEL1, P), np.float32)
    for e in range(E):
        rows = row[row // R == e]
        sel_1[e, 0, rows] = ALPHA
        sel_1[E + e, 1, rows] = ALPHA
        sel_1[e, 1, rows] = -ALPHA
        sel_1[E + e, 2, rows] = ALPHA
    for part in range(3):
        for slot in range(2):
            sel_1[2 * E + 2 * part + slot, 3 + slot] = 1.0
    bf16 = mybir.dt.np(BF16)
    column = np.arange(E * NK).reshape(2, P).T
    expert = np.arange(E)
    ck = np.concatenate([np.tile(P * np.arange(1, NK + 1), (P, 1)),
                         row[:, None] + P * np.arange(SUB) - T // 2, (column[:, :, None] // NK == expert).reshape(P, -1),
                         P * (row % NK)[:, None], (column[:, :, None] < NK * expert).reshape(P, -1),
                         column // NK, np.tile(E ** np.arange(UNROLL), (P, 1))], axis=1).astype(np.float32)
    assert ck.shape[1] == CK_COLS
    return {"cf": cf, "ident": np.eye(P).astype(bf16), "ident_f": np.eye(P, dtype=np.float32),
            "ck": ck, "cb": np.concatenate([row[:, None] < row, np.ones((P, P)), np.tile(np.arange(E * NK), (P, 1))], axis=1).astype(bf16),
            "sel_1": sel_1.reshape(NC1, -1).astype(bf16)}


def kernel(**inputs):
    import concourse.bacc as bacc
    from concourse.bass_utils import run_bass_kernel_spmd

    v = {n: np.asarray(a) for n, a in inputs.items()}
    arrays = {
        "x": np.ascontiguousarray(v["x"].reshape(T, D)),
        "wd2": np.ascontiguousarray(v["L0_ffn_Wd"][:, P:].transpose(1, 0, 2)).reshape(IMR, E * D),
        "xT": np.ascontiguousarray(v["x"].reshape(T, D).T),
        "idx0": np.ascontiguousarray(v["itok_B_0_7"]),
        "idx1": np.ascontiguousarray(v["itok_B_0_6"]),
        "w0": _pack_0(v), "wm": _pack_m(v), "w1": _pack_1(v),
        **_constants(v["L1_cond_scalings"]),
    }
    nc = bacc.Bacc("TRN2", target_bir_lowering=False, num_devices=1)
    A = {n: nc.dram_tensor(n, a.shape, mybir.dt.from_np(a.dtype), kind="ExternalInput").ap() for n, a in arrays.items()}
    A["out"] = nc.dram_tensor("out", (T, D), F32, kind="ExternalOutput").ap()
    A["h"] = nc.dram_tensor("h", (T, D), F32).ap()
    A["y"] = nc.dram_tensor("y", (NT * P, D), F32).ap()
    A["x1"] = nc.dram_tensor("x1", (T, D), F32).ap()
    program(nc, A)
    r = run_bass_kernel_spmd(nc, [arrays], core_ids=[0])
    return r.results[0]["out"].reshape(B, S, D)
```
